# Optimizing a Trainium2 kernel written in Bass

```python
import numpy as np
import jax
import jax.numpy as jnp

def _softmax(x, axis=-1):
    return jax.nn.softmax(x, axis=axis)

def _gelu(x):
    return jax.nn.gelu(x, approximate=True)

def _silu(x):
    return jax.nn.silu(x)

def _sigmoid(x):
    return jax.nn.sigmoid(x)

def _layernorm(x, axis=-1, eps=1e-05):
    m = jnp.mean(x, axis=axis, keepdims=True)
    v = jnp.var(x, axis=axis, keepdims=True)
    return (x - m) / jnp.sqrt(v + eps)

def _scatter_add(tgt, idx, src, axis=0):
    return tgt.at[idx].add(src)

def _segment_sum(src, seg, n):
    return jax.ops.segment_sum(src, seg, n)
kernel_name = 'mk_adaln_ffn_d1_seqx_r4_ae4c08'

def setup_inputs(seed: int=0):
    np.random.seed(seed)
    _w = jnp.asarray

    def _rec_inputs():
        import jax
        import jax.numpy as jnp
        _rk = jax.random.key(seed)
        x = 7.22e-05 + 1 * jax.random.normal(jax.random.fold_in(_rk, 1), (2, 1024, 256), jnp.float32)
        _lenS = 1024 - jax.random.randint(jax.random.fold_in(_rk, 7), (2,), 0, max(1, 1024 // 4) + 1, jnp.int32)
        _lenS2 = 1024 - jax.random.randint(jax.random.fold_in(_rk, 8), (2,), 0, max(1, 1024 // 4) + 1, jnp.int32)
        itok_BxS_0_999 = jax.random.randint(jax.random.fold_in(_rk, 11), (2, 1024), 0, 250, jnp.int32)
        itok_BxS_0_4 = jax.random.randint(jax.random.fold_in(_rk, 12), (2, 1024), 0, 5, jnp.int32)
        cond_512 = 0.00199304 + 1.00034 * jax.random.normal(jax.random.fold_in(_rk, 14), (2, 128), jnp.float32)
        cond_64 = 0.0990542 + 1.04422 * jax.random.normal(jax.random.fold_in(_rk, 15), (2, 64), jnp.float32)
        fside_Bx32_0 = -0.136436 + 0.990155 * jax.random.normal(jax.random.fold_in(_rk, 16), (2, 32), jnp.float32)
        _validS = jnp.arange(1024)[None, :] < _lenS[:, None]
        _validS2 = jnp.arange(1024)[None, :] < _lenS2[:, None]
        _causal = jnp.tril(jnp.ones((1024, 1024), dtype=bool))
        mask_BxS_ik0 = jnp.where(jnp.broadcast_to(_validS[:, :], (2, 1024)), 0, 1).astype(jnp.int32)
        return (x, itok_BxS_0_999, itok_BxS_0_4, cond_512, cond_64, fside_Bx32_0, mask_BxS_ik0)
    x, itok_BxS_0_999, itok_BxS_0_4, cond_512, cond_64, fside_Bx32_0, mask_BxS_ik0 = _rec_inputs()

    def _L0_cond_setup():
        import jax, jax.numpy as jnp
        import numpy as np
        EPS = 1e-05

        def _ln(x, g, b):
            m = jnp.mean(x, axis=-1, keepdims=True)
            v = jnp.mean((x - m) ** 2, axis=-1, keepdims=True)
            return (x - m) * jax.lax.rsqrt(v + EPS) * g + b

        def _mlp_ln(s, W1, b1, W2, b2, g, b):
            h = jax.nn.silu(s @ W1 + b1) @ W2 + b2
            return _ln(h, g, b)
        key = jax.random.key(seed)
        B, S, D = (4, 512, 256)
        MEM, NOI, RES = (128, 64, 32)
        ks = jax.random.split(key, 40)
        ki = iter(range(40))

        def nrm(shape, scale=0.02):
            return jax.random.normal(ks[next(ki)], shape, jnp.float32) * scale

        def gamma(shape):
            return jnp.ones(shape, jnp.float32) + nrm(shape)
        inp = {'x': jax.random.normal(ks[next(ki)], (B, S, D), jnp.float32), 'pathway_ids': jax.random.randint(ks[next(ki)], (B, S), 0, 250), 'compartment_ids': jax.random.randint(ks[next(ki)], (B, S), 0, 5), 'time_steps': jax.random.randint(ks[next(ki)], (B, S), 0, 5), 'scale_type': jax.random.randint(ks[next(ki)], (B, S), 0, 3), 'memory_state': jax.random.normal(ks[next(ki)], (B, MEM), jnp.float32), 'noise_state': jax.random.normal(ks[next(ki)], (B, NOI), jnp.float32), 'resource_state': jax.random.normal(ks[next(ki)], (B, RES), jnp.float32), 'pw_g': gamma((250, D)), 'pw_b': nrm((250, D)), 'cp_g': gamma((5, D)), 'cp_b': nrm((5, D)), 'tm_g': gamma((5, D)), 'tm_b': nrm((5, D)), 'ms_g': gamma((3, D)), 'ms_b': nrm((3, D)), 'mem_W1': nrm((MEM, D)), 'mem_b1': jnp.zeros((D,)), 'mem_W2': nrm((D, D)), 'mem_b2': jnp.zeros((D,)), 'mem_g': gamma((D,)), 'mem_be': jnp.zeros((D,)), 'noi_W1': nrm((NOI, D)), 'noi_b1': jnp.zeros((D,)), 'noi_W2': nrm((D, D)), 'noi_b2': jnp.zeros((D,)), 'noi_g': gamma((D,)), 'noi_be': jnp.zeros((D,)), 'res_W1': nrm((RES, D)), 'res_b1': jnp.zeros((D,)), 'res_W2': nrm((D, D)), 'res_b2': jnp.zeros((D,)), 'res_g': gamma((D,)), 'res_be': jnp.zeros((D,)), 'int_W1': nrm((6 * D, D)), 'int_b1': jnp.zeros((D,)), 'int_W2': nrm((D, D)), 'int_b2': jnp.zeros((D,)), 'int_g': gamma((D,)), 'int_be': jnp.zeros((D,)), 'aw': jnp.ones((6,), jnp.float32) / 6.0}
        return inp
    _L0_cond_all = _L0_cond_setup()
    _L0_cond_in = {k: v for k, v in _L0_cond_all.items() if k in ('pw_g', 'pw_b', 'cp_g', 'cp_b', 'tm_g', 'tm_b', 'ms_g', 'ms_b', 'mem_W1', 'mem_b1', 'mem_W2', 'mem_b2', 'mem_g', 'mem_be', 'noi_W1', 'noi_b1', 'noi_W2', 'noi_b2', 'noi_g', 'noi_be', 'res_W1', 'res_b1', 'res_W2', 'res_b2', 'res_g', 'res_be', 'int_W1', 'int_b1', 'int_W2', 'int_b2', 'int_g', 'int_be', 'aw')}
    del _L0_cond_all

    def _L0_ffn_setup():
        import jax, jax.numpy as jnp
        import numpy as np
        DIM = 256
        HID = 512
        E = 8
        K = 2
        R = 16
        B_, S_ = (2, 256)

        def _lora_in(xf, W, b, A, B):
            base = jnp.einsum('td,ehd->teh', xf, W)
            low = jnp.einsum('ter,ehr->teh', jnp.einsum('td,erd->ter', xf, A), B)
            return base + low + b

        def _lora_out(g, W, b, A, B):
            base = jnp.einsum('teh,edh->ted', g, W)
            low = jnp.einsum('ter,edr->ted', jnp.einsum('teh,erh->ter', g, A), B)
            return base + low + b
        key = jax.random.key(seed)
        ks = jax.random.split(key, 14)
        n = lambda k, shape, scale: jax.random.normal(k, shape, jnp.float32) * scale
        inp = {'x': jax.random.normal(ks[0], (B_, S_, DIM), jnp.float32), 'Wg': n(ks[1], (E, DIM), DIM ** (-0.5)), 'W1': n(ks[2], (E, HID, DIM), DIM ** (-0.5)), 'b1': jnp.zeros((E, HID), jnp.float32), 'A1': n(ks[3], (E, R, DIM), DIM ** (-0.5)), 'B1': n(ks[4], (E, HID, R), 0.01), 'W2': n(ks[5], (E, DIM, HID), HID ** (-0.5)), 'b2': jnp.zeros((E, DIM), jnp.float32), 'A2': n(ks[6], (E, R, HID), HID ** (-0.5)), 'B2': n(ks[7], (E, DIM, R), 0.01), 'W3': n(ks[8], (E, HID, DIM), DIM ** (-0.5)), 'b3': jnp.zeros((E, HID), jnp.float32), 'A3': n(ks[9], (E, R, DIM), DIM ** (-0.5)), 'B3': n(ks[10], (E, HID, R), 0.01)}
        return inp
    _L0_ffn_all = _L0_ffn_setup()
    _L0_ffn_in = {k: v for k, v in _L0_ffn_all.items() if k in ('Wg', 'W1', 'b1', 'A1', 'B1', 'W2', 'b2', 'A2', 'B2', 'W3', 'b3', 'A3', 'B3')}
    del _L0_ffn_all
    return {'x': x, 'itok_BxS_0_999': itok_BxS_0_999, 'itok_BxS_0_4': itok_BxS_0_4, 'cond_512': cond_512, 'cond_64': cond_64, 'fside_Bx32_0': fside_Bx32_0, 'mask_BxS_ik0': mask_BxS_ik0, 'L0_cond_pw_g': _L0_cond_in['pw_g'], 'L0_cond_pw_b': _L0_cond_in['pw_b'], 'L0_cond_cp_g': _L0_cond_in['cp_g'], 'L0_cond_cp_b': _L0_cond_in['cp_b'], 'L0_cond_tm_g': _L0_cond_in['tm_g'], 'L0_cond_tm_b': _L0_cond_in['tm_b'], 'L0_cond_ms_g': _L0_cond_in['ms_g'], 'L0_cond_ms_b': _L0_cond_in['ms_b'], 'L0_cond_mem_W1': _L0_cond_in['mem_W1'], 'L0_cond_mem_b1': _L0_cond_in['mem_b1'], 'L0_cond_mem_W2': _L0_cond_in['mem_W2'], 'L0_cond_mem_b2': _L0_cond_in['mem_b2'], 'L0_cond_mem_g': _L0_cond_in['mem_g'], 'L0_cond_mem_be': _L0_cond_in['mem_be'], 'L0_cond_noi_W1': _L0_cond_in['noi_W1'], 'L0_cond_noi_b1': _L0_cond_in['noi_b1'], 'L0_cond_noi_W2': _L0_cond_in['noi_W2'], 'L0_cond_noi_b2': _L0_cond_in['noi_b2'], 'L0_cond_noi_g': _L0_cond_in['noi_g'], 'L0_cond_noi_be': _L0_cond_in['noi_be'], 'L0_cond_res_W1': _L0_cond_in['res_W1'], 'L0_cond_res_b1': _L0_cond_in['res_b1'], 'L0_cond_res_W2': _L0_cond_in['res_W2'], 'L0_cond_res_b2': _L0_cond_in['res_b2'], 'L0_cond_res_g': _L0_cond_in['res_g'], 'L0_cond_res_be': _L0_cond_in['res_be'], 'L0_cond_int_W1': _L0_cond_in['int_W1'], 'L0_cond_int_b1': _L0_cond_in['int_b1'], 'L0_cond_int_W2': _L0_cond_in['int_W2'], 'L0_cond_int_b2': _L0_cond_in['int_b2'], 'L0_cond_int_g': _L0_cond_in['int_g'], 'L0_cond_int_be': _L0_cond_in['int_be'], 'L0_cond_aw': _L0_cond_in['aw'], 'L0_ffn_Wg': _L0_ffn_in['Wg'], 'L0_ffn_W1': _L0_ffn_in['W1'], 'L0_ffn_b1': _L0_ffn_in['b1'], 'L0_ffn_A1': _L0_ffn_in['A1'], 'L0_ffn_B1': _L0_ffn_in['B1'], 'L0_ffn_W2': _L0_ffn_in['W2'], 'L0_ffn_b2': _L0_ffn_in['b2'], 'L0_ffn_A2': _L0_ffn_in['A2'], 'L0_ffn_B2': _L0_ffn_in['B2'], 'L0_ffn_W3': _L0_ffn_in['W3'], 'L0_ffn_b3': _L0_ffn_in['b3'], 'L0_ffn_A3': _L0_ffn_in['A3'], 'L0_ffn_B3': _L0_ffn_in['B3']}

def reference(x, itok_BxS_0_999, itok_BxS_0_4, cond_512, cond_64, fside_Bx32_0, mask_BxS_ik0, L0_cond_pw_g, L0_cond_pw_b, L0_cond_cp_g, L0_cond_cp_b, L0_cond_tm_g, L0_cond_tm_b, L0_cond_ms_g, L0_cond_ms_b, L0_cond_mem_W1, L0_cond_mem_b1, L0_cond_mem_W2, L0_cond_mem_b2, L0_cond_mem_g, L0_cond_mem_be, L0_cond_noi_W1, L0_cond_noi_b1, L0_cond_noi_W2, L0_cond_noi_b2, L0_cond_noi_g, L0_cond_noi_be, L0_cond_res_W1, L0_cond_res_b1, L0_cond_res_W2, L0_cond_res_b2, L0_cond_res_g, L0_cond_res_be, L0_cond_int_W1, L0_cond_int_b1, L0_cond_int_W2, L0_cond_int_b2, L0_cond_int_g, L0_cond_int_be, L0_cond_aw, L0_ffn_Wg, L0_ffn_W1, L0_ffn_b1, L0_ffn_A1, L0_ffn_B1, L0_ffn_W2, L0_ffn_b2, L0_ffn_A2, L0_ffn_B2, L0_ffn_W3, L0_ffn_b3, L0_ffn_A3, L0_ffn_B3):
    import jax
    import jax.numpy as jnp

    def _L0_cond_ref(x, pathway_ids, compartment_ids, time_steps, scale_type, memory_state, noise_state, resource_state, pw_g, pw_b, cp_g, cp_b, tm_g, tm_b, ms_g, ms_b, mem_W1, mem_b1, mem_W2, mem_b2, mem_g, mem_be, noi_W1, noi_b1, noi_W2, noi_b2, noi_g, noi_be, res_W1, res_b1, res_W2, res_b2, res_g, res_be, int_W1, int_b1, int_W2, int_b2, int_g, int_be, aw):
        import jax, jax.numpy as jnp
        import numpy as np
        EPS = 1e-05

        def _ln(x, g, b):
            m = jnp.mean(x, axis=-1, keepdims=True)
            v = jnp.mean((x - m) ** 2, axis=-1, keepdims=True)
            return (x - m) * jax.lax.rsqrt(v + EPS) * g + b

        def _mlp_ln(s, W1, b1, W2, b2, g, b):
            h = jax.nn.silu(s @ W1 + b1) @ W2 + b2
            return _ln(h, g, b)
        h = _ln(x, pw_g[pathway_ids], pw_b[pathway_ids])
        h = _ln(h, cp_g[compartment_ids], cp_b[compartment_ids])
        t = _ln(x, tm_g[time_steps], tm_b[time_steps])
        m = x + _mlp_ln(memory_state, mem_W1, mem_b1, mem_W2, mem_b2, mem_g, mem_be)[:, None, :]
        n = x + _mlp_ln(noise_state, noi_W1, noi_b1, noi_W2, noi_b2, noi_g, noi_be)[:, None, :]
        r = x + _mlp_ln(resource_state, res_W1, res_b1, res_W2, res_b2, res_g, res_be)[:, None, :]
        s = _ln(x, ms_g[scale_type], ms_b[scale_type])
        w = jax.nn.softmax(aw)
        cat = jnp.concatenate([w[0] * h, w[1] * t, w[2] * m, w[3] * n, w[4] * r, w[5] * s], axis=-1)
        return _mlp_ln(cat, int_W1, int_b1, int_W2, int_b2, int_g, int_be)

    def _L0_ffn_ref(x, Wg, W1, b1, A1, B1, W2, b2, A2, B2, W3, b3, A3, B3):
        import jax, jax.numpy as jnp
        import numpy as np
        DIM = 256
        HID = 512
        E = 8
        K = 2
        R = 16
        B_, S_ = (2, 256)

        def _lora_in(xf, W, b, A, B):
            base = jnp.einsum('td,ehd->teh', xf, W)
            low = jnp.einsum('ter,ehr->teh', jnp.einsum('td,erd->ter', xf, A), B)
            return base + low + b

        def _lora_out(g, W, b, A, B):
            base = jnp.einsum('teh,edh->ted', g, W)
            low = jnp.einsum('ter,edr->ted', jnp.einsum('teh,erh->ter', g, A), B)
            return base + low + b
        orig_shape = x.shape
        xf = x.reshape(-1, x.shape[-1])
        scores = jax.nn.softmax(xf @ Wg.T, axis=-1)
        expert_weights, expert_indices = jax.lax.top_k(scores, K)
        expert_weights = expert_weights / expert_weights.sum(-1, keepdims=True)
        gates = (jax.nn.one_hot(expert_indices, E, dtype=xf.dtype) * expert_weights[..., None]).sum(axis=1)
        h1 = _lora_in(xf, W1, b1, A1, B1)
        h3 = _lora_in(xf, W3, b3, A3, B3)
        g = jax.nn.silu(h1) * h3
        y_e = _lora_out(g, W2, b2, A2, B2)
        y = jnp.einsum('te,ted->td', gates, y_e)
        return y.reshape(orig_shape)
    x = x + _L0_ffn_ref(_L0_cond_ref(x, itok_BxS_0_999, itok_BxS_0_4, itok_BxS_0_4, mask_BxS_ik0, cond_512, cond_64, fside_Bx32_0, L0_cond_pw_g, L0_cond_pw_b, L0_cond_cp_g, L0_cond_cp_b, L0_cond_tm_g, L0_cond_tm_b, L0_cond_ms_g, L0_cond_ms_b, L0_cond_mem_W1, L0_cond_mem_b1, L0_cond_mem_W2, L0_cond_mem_b2, L0_cond_mem_g, L0_cond_mem_be, L0_cond_noi_W1, L0_cond_noi_b1, L0_cond_noi_W2, L0_cond_noi_b2, L0_cond_noi_g, L0_cond_noi_be, L0_cond_res_W1, L0_cond_res_b1, L0_cond_res_W2, L0_cond_res_b2, L0_cond_res_g, L0_cond_res_be, L0_cond_int_W1, L0_cond_int_b1, L0_cond_int_W2, L0_cond_int_b2, L0_cond_int_g, L0_cond_int_be, L0_cond_aw), L0_ffn_Wg, L0_ffn_W1, L0_ffn_b1, L0_ffn_A1, L0_ffn_B1, L0_ffn_W2, L0_ffn_b2, L0_ffn_A2, L0_ffn_B2, L0_ffn_W3, L0_ffn_b3, L0_ffn_A3, L0_ffn_B3)
    return x

_drawn_inputs = setup_inputs


def setup_inputs(seed=0):
    import zlib

    import numpy as np

    out = dict(_drawn_inputs(seed))
    spreads = {'L0_cond_mem_b1': (0.0, 0.8),
     'L0_cond_mem_b2': (0.0, 0.1),
     'L0_cond_mem_be': (0.0, 0.8),
     'L0_cond_noi_b1': (0.0, 0.8),
     'L0_cond_noi_b2': (0.0, 0.1),
     'L0_cond_noi_be': (0.0, 0.8),
     'L0_cond_res_b1': (0.0, 0.8),
     'L0_cond_res_b2': (0.0, 0.1),
     'L0_cond_res_be': (0.0, 0.8),
     'L0_cond_int_b1': (0.0, 0.1),
     'L0_cond_int_b2': (0.0, 0.1),
     'L0_cond_int_be': (0.0, 0.1),
     'L0_cond_aw': (0.1666666716337204, 0.6),
     'L0_ffn_b1': (0.0, 0.4),
     'L0_ffn_b2': (0.0, 0.8),
     'L0_ffn_b3': (0.0, 0.452)}
    factors = {'cond_512': 3.477,
     'cond_64': 3.7,
     'fside_Bx32_0': 5.29,
     'L0_cond_pw_g': 8.0,
     'L0_cond_pw_b': 8.0,
     'L0_cond_cp_g': 8.0,
     'L0_cond_cp_b': 8.0,
     'L0_cond_tm_g': 8.0,
     'L0_cond_tm_b': 8.0,
     'L0_cond_ms_g': 8.0,
     'L0_cond_ms_b': 8.0,
     'L0_cond_mem_W2': 3.405,
     'L0_cond_mem_g': 8.0,
     'L0_cond_noi_W1': 4.698,
     'L0_cond_noi_W2': 3.24,
     'L0_cond_noi_g': 8.0,
     'L0_cond_res_W1': 4.32,
     'L0_cond_res_W2': 3.912,
     'L0_cond_res_g': 8.0,
     'L0_cond_int_g': 4.64,
     'L0_ffn_A1': 3.116,
     'L0_ffn_B1': 3.251,
     'L0_ffn_A2': 4.086,
     'L0_ffn_B2': 4.345,
     'L0_ffn_A3': 3.853,
     'L0_ffn_B3': 3.641}
    for name, (base, spread) in spreads.items():
        noise = np.random.default_rng([zlib.crc32(name.encode()), seed]).standard_normal(out[name].shape)
        drawn = base * np.exp(spread * noise) if base else spread * noise
        out[name] = jnp.asarray(drawn.astype(out[name].dtype))
    for name, factor in factors.items():
        out[name] = (out[name] * factor).astype(out[name].dtype)
    return out
```

```python
from collections import namedtuple
from contextlib import ExitStack

import numpy as np

import concourse.bass as bass
from concourse import mybir

F32 = mybir.dt.float32
F16 = mybir.dt.float16
BF16 = mybir.dt.bfloat16
I32 = mybir.dt.int32
U32 = mybir.dt.uint32
ALU = mybir.AluOpType
ACT = mybir.ActivationFunctionType
AX_X = mybir.AxisListType.X

P = 128
T, D, H, E, R, K = 2048, 256, 512, 8, 16, 2
DC, HC = D // P, H // P
TILES = T // P
KB = 2
BT = KB * P
NB = T // BT
NBATCH = 2
SLOT_TILES = (T * K) // P + E - 1
PAD = P
WE = 2 * D * H // P + D * H // P
HALF = 512
HALVES = WE // HALF
LORA = 2 * D + H + 2 * H + D
LA = 2 * D + H
BE = 2 * H + D
WSCALE = 64.0
EPS = 1e-5
NKIND = 3
ROWS = 96
NET_S, NET_B1 = 0, NKIND * NBATCH
NET_INT, NET_W1 = NET_B1 + 3 * DC, NET_B1 + 4 * DC
NET_W2 = NET_W1 + 3 * D
NET = NET_W2 + 3 * DC * D
ds = bass.ds


def build(nc, a, out):
    with ExitStack() as ctx:
        def sb(name, shape, dt):
            return ctx.enter_context(nc.sbuf_tensor(name, shape, dt))

        def psum(name, shape, dt=F32):
            return ctx.enter_context(nc.psum_tensor(name, shape, dt))

        S = namedtuple("Semaphores", SEMAPHORES)(*[ctx.enter_context(nc.semaphore(n)) for n in SEMAPHORES.split()])

        u_rows = nc.dram_tensor("u_rows", (T, 2 * D), F16, kind="Internal").ap()
        lora_hi_d = nc.dram_tensor("lora_hi_d", (P, LORA), F16, kind="Internal").ap()
        lora_lo_d = nc.dram_tensor("lora_lo_d", (P, LORA), F16, kind="Internal").ap()

        w_hi = sb("w_hi", [P, E * WE], F16)
        w_lo = sb("w_lo", [P, E * WE], F16)
        ident = sb("ident", [P, P], F32)
        ident16 = sb("ident16", [P, P], F16)
        ones16 = sb("ones16", [P, P], F16)
        before = sb("before", [P, P], F16)
        before8 = sb("before8", [P, E, E], F32)
        iota_p = sb("iota_p", [P, P], F16)
        iota_e = sb("iota_e", [P, E], F32)
        iota_s = sb("iota_s", [P, SLOT_TILES], F32)
        token1 = sb("token1", [P, K, TILES], F32)
        pad_row = sb("pad_row", [P, 1], F32)
        top = sb("top", [P, TILES * 8], F32)
        top_e = sb("top_e", [P, TILES * 8], U32)

        region = sb("region", [P, REGION], F32)
        at = [0]

        def part(words, dt=F32):
            v = region[:, at[0]:at[0] + words]
            at[0] += words
            return v if dt == F32 else v.bitcast(dt)

        x_tok = part(TILES * D)
        xT = part(DC * T).rearrange("p (c t) -> p c t", c=DC)
        int_w1 = part(12 * D).rearrange("p (c n) -> p c n", c=12)
        wx = part(DC * D).rearrange("p (c n) -> p c n", c=DC)
        int_w2g = part(DC * (D + E)).rearrange("p (c n) -> p c n", c=DC)
        int_w2, wgT = int_w2g[:, :, 0:D], int_w2g[:, :, D:]
        onehot = part(T // 2, BF16)[0:ROWS, :]
        gain_tab = part(4 * D // 2, BF16)[0:ROWS, :].rearrange("p (k d) -> p k d", k=4)
        norm_flat = part(3 * D)
        norm_rows = norm_flat.rearrange("p (k d) -> p k d", k=3)
        bias_blk = part(NB * DC)
        xh = part(KB * D).rearrange("p (k d) -> p k d", k=KB)
        hh = part(KB * D).rearrange("p (k d) -> p k d", k=KB)
        xhT = part(DC * BT)
        hhT = part(DC * BT)
        prod_t = part(DC * BT)
        prod_s = part(DC * BT)
        prod_h = part(DC * BT)
        zT = part(DC * BT).rearrange("p (c t) -> p c t", c=DC)
        c_flat = part(KB * D)
        c_sb = c_flat.rearrange("p (k d) -> p k d", k=KB)
        u = part(KB * D).rearrange("p (k d) -> p k d", k=KB)
        u_split = part(KB * D, F16).rearrange("p (k n) -> p k n", k=KB)
        uT_sb = part(KB * D)
        pw_rows = part(KB * 2 * D).rearrange("p (k n) -> p k n", k=KB)
        w_stage = [part(2 * HALF) for _ in range(3)]
        w_full = [part(HALF) for _ in range(3)]
        lora_k = part(LORA // 2, F16)
        small = part(96)
        x_st, x_mv = small[:, 0:12], small[:, 12:16].rearrange("p (k n) -> p k n", k=KB)
        h_st, h_mv = small[:, 16:28], small[:, 28:32].rearrange("p (k n) -> p k n", k=KB)
        c_st, c_mv = small[:, 32:44], small[:, 44:48].rearrange("p (k n) -> p k n", k=KB)
        x_ve, x_rs = small[:, 48:50], small[:, 50:52]
        h_ve, h_rs = small[:, 52:54], small[:, 54:56]
        c_ve, c_rs = small[:, 56:58], small[:, 58:60]
        v_ve, v_rs = small[:, 60:63], small[:, 63:66]
        minus_half, eps_sb = small[:, 66:69], small[:, 92:95]
        aw_e, aw_m, aw_s, aw_r = small[:, 70:76], small[:, 76:77], small[:, 77:78], small[:, 78:79]
        mixw = small[:, 80:86]
        lg_sb = part(KB * E)
        top_now = part(KB * 8)
        top_e_now = part(KB * 8, U32)
        path_ids = part(TILES, I32)
        path_now = part(KB, I32)
        aw_sb = part(6)
        cond_end = at[0]

        lo5 = w_lo[:, 3 * WE + 2 * LORA:6 * WE].bitcast(F32)
        hi5 = w_hi[:, 3 * WE + 2 * LORA:6 * WE].bitcast(F32)
        ids_i = hi5[:, 0:T].bitcast(I32)
        setup_f = hi5[:, T:T + P]
        gain_f = lo5[0:ROWS, 0:4 * D].rearrange("p (k d) -> p k d", k=4)
        gain_r = lo5[0:ROWS, 4 * D:8 * D].rearrange("p (k d) -> p k d", k=4)
        gain_h = c_flat[0:ROWS, :].bitcast(BF16).rearrange("p (k d) -> p k d", k=4)
        row16, row16_f = small[:, 88:90].bitcast(I32), small[:, 90:91]
        wl = w_lo[:, (E - 2) * WE:E * WE].bitcast(F32)
        wh = w_hi[:, (E - 2) * WE:E * WE].bitcast(F32)
        net = wl[:, 0:NET]
        mlp_s = net[:, NET_S:NET_B1].rearrange("p (k b) -> p k b", k=3)
        mlp_b1 = net[:, NET_B1:NET_INT].rearrange("p (k c) -> p k c", k=3)
        int_b1 = net[:, NET_INT:NET_W1]
        mlp_w1 = net[:, NET_W1:NET_W2].rearrange("p (k n) -> p k n", k=3)
        mlp_w2 = net[:, NET_W2:].rearrange("p (k c n) -> p k c n", k=3, c=DC)
        shift_Z = wl[:, NET:NET + DC * NKIND * ROWS].rearrange("p (c k r) -> p c k r", c=DC, k=NKIND)
        net_small = wl[:, NET + DC * NKIND * ROWS:]
        mlp_h = net_small[:, 0:12].rearrange("p (k c b) -> p k c b", k=3, c=DC)
        mlp_vT = net_small[:, 12:24].rearrange("p (k b) -> p k b", b=NBATCH)
        mlp_st = net_small[:, 24:42].rearrange("p (k n) -> p k n", k=3)
        mlp_mv = net_small[:, 42:48].rearrange("p (k n) -> p k n", k=3)
        net_rows = wh[:, 0:9 * D]
        mlp_b2, mlp_g, mlp_be = (net_rows[:, n * 3 * D:(n + 1) * 3 * D].rearrange("p (k n) -> p k n", k=3)
                                 for n in range(3))
        mlp_v = wh[:, 9 * D:12 * D].rearrange("p (k n) -> p k n", k=3)
        lora_f = w_lo[:, 3 * WE:3 * WE + 2 * LORA].bitcast(F32)
        lora_h = w_hi[:, 3 * WE:3 * WE + LORA]
        lora_l = w_hi[:, 3 * WE + LORA:3 * WE + 2 * LORA]

        at[0] = 0
        biases = part(E * BE)
        rows_in = [part(D, F16) for _ in range(2)]
        rowsT = [part(D, F16) for _ in range(2)]
        h1_sb = [part(H) for _ in range(2)]
        h3_sb = [part(H) for _ in range(2)]
        silu_sb = [part(H) for _ in range(2)]
        g_sb = [part(H) for _ in range(2)]
        gT_hi = [part(H // 2, F16) for _ in range(2)]
        gT_lo = [part(H // 2, F16) for _ in range(2)]
        y_sb = [part(D) for _ in range(2)]
        y_gated = [part(D) for _ in range(2)]
        gather_now = [part(1, I32) for _ in range(2)]
        scatter_now = [part(1, I32) for _ in range(2)]
        slot_rows = part(SLOT_TILES * 2, I32).rearrange("p (i n) -> p i n", n=2)
        slot_gate = part(SLOT_TILES)
        tile_expert = part(SLOT_TILES, I32)
        NC_ = K * TILES
        chosen = part(NC_ * E).rearrange("p (k j e) -> p k j e", k=K, e=E)
        picked = part((TILES + 1) * E // 2, F16).rearrange("p (j e) -> p j e", e=E)
        place = part(TILES * E).rearrange("p (j e) -> p j e", e=E)
        place2 = part(NC_ * E).rearrange("p (k j e) -> p k j e", k=K, e=E)
        slot_f = part(NC_)
        slot_i = part(NC_, I32)
        slot_tile = part(NC_, I32)
        slot_col = part(NC_, I32)
        slot_tile_f = part(NC_)
        slot_col_f = part(NC_)
        tiles_i = part(E, I32)
        tiles_f = part(E)
        tri_f = part(E * E).rearrange("p (a b) -> p a b", a=E)
        first_tile = part(E)
        started = part(SLOT_TILES * E).rearrange("p (i e) -> p i e", e=E)
        started_n = part(SLOT_TILES)
        gap = part(TILES)
        e2 = part(TILES)
        den = part(TILES)
        gate = part(K * TILES).rearrange("p (k j) -> p k j", k=K)
        gate_f = part(K * TILES).rearrange("p (k j) -> p k j", k=K)
        gate_h = part(K * TILES // 2, F16).rearrange("p (k j) -> p k j", k=K)
        in_tile = part(NC_ * SLOT_TILES).rearrange("p (n s) -> p n s", n=NC_)
        col_hot = part(NC_ * P // 2, F16).rearrange("p (n c) -> p n c", n=NC_)
        tile_val = part(NC_ * 3 * SLOT_TILES // 2, F16).rearrange("p (n v s) -> p n v s", n=NC_, v=3)
        slot_v = part(3 * SLOT_TILES).rearrange("p (v s) -> p v s", v=3)
        empty = part(SLOT_TILES)
        main_end = at[0]
        assert max(cond_end, main_end) <= REGION, (cond_end, main_end)

        bank = [psum(f"bank{i}", [P, 512]) for i in range(8)]
        ps_xT, ps_hT, ps_g0, ps_g1, ps_l1, ps_l2, ps_u, ps_lora = bank
        ps_h1, ps_h3 = bank[0:2], bank[2:4]
        ps_rowsT = [bank[4][:, 0:256].bitcast(F16), bank[5][:, 0:256].bitcast(F16)]
        ps_gT, ps_y = bank[6], bank[7]

        block = ctx.enter_context(nc.Block())

        def after(engine, semaphore, count):
            if not isinstance(count, int) or count > 0:
                engine.wait_ge(semaphore, count)

        def before_plain(engine, semaphore, count):
            engine.wait_ge(semaphore, count)
            if not isinstance(count, int):
                engine.sem_inc(S.passed, 1)

        @block.sync
        def _(sp):
            x_v = a.x.rearrange("(j p) d -> p j d", p=P)
            xt_v = x_tok.rearrange("p (j d) -> p j d", d=D)
            sp.dma_start(path_ids, a.path_ids).then_inc(S.ids_in, 16)
            sp.dma_start(xt_v[:, 0:2 * KB, :], x_v[:, 0:2 * KB, :]).then_inc(S.x_first, 16)
            sp.dma_start(ids_i[0:ROWS, :], a.onehot_ids).then_inc(S.onehot_ids_in, 16)
            w1_v = a.int_W1.rearrange("(c p) n -> p c n", p=P)
            sp.dma_start(int_w1[:, 0:4, :], w1_v[:, 0:4, :]).then_inc(S.w1_in, 16)
            sp.dma_start(int_w1[:, 10:12, :], w1_v[:, 10:12, :]).then_inc(S.w1_in, 16)
            sp.dma_start(int_w1[:, 4:10, :], w1_v[:, 4:10, :]).then_inc(S.w1x_in, 16)
            sp.dma_start(net, a.net).then_inc(S.net_in, 16)
            sp.dma_start(net_rows[0:NBATCH, :], a.net_rows.partition_broadcast(NBATCH)).then_inc(S.net_rows_in, 16)
            xT_v = a.xT.rearrange("(c p) t -> p c t", p=P)
            sp.dma_start(xT[:, :, 0:2 * BT], xT_v[:, :, 0:2 * BT]).then_inc(S.xT_first, 16)

            def load_weights(e, parts):
                for p in parts:
                    w = (a.W1T, a.W3T, a.W2T)[p]
                    after(sp, S.w_sum, (e - 1) * HALVES + 2 * p + 2)
                    sp.dma_start(w_stage[p], w[ds(e * P, P), :]).then_inc((S.w1s_in, S.w3s_in, S.w2s_in)[p], 16)

            def load_lora(e):
                after(sp, S.lora_ps, e * HALVES)
                hi, lo = lora_hi_d[ds(e * R, R), :], lora_lo_d[ds(e * R, R), :]
                sp.dma_start(lora_k[0:R, :], hi).then_inc(S.lora_k_in, 16)
                sp.dma_start(lora_k[R:2 * R, 0:LA], hi[:, 0:LA]).then_inc(S.lora_k_in, 16)
                sp.dma_start(lora_k[R:2 * R, LA:], lo[:, LA:]).then_inc(S.lora_k_in, 16)
                sp.dma_start(lora_k[2 * R:3 * R, 0:LA], lo[:, 0:LA]).then_inc(S.lora_k_in, 16)
                sp.dma_start(lora_k[2 * R:3 * R, LA:], hi[:, LA:]).then_inc(S.lora_k_in, 16)

            def store_rows(b):
                after(sp, S.u_lo, b + 1)
                sp.dma_start(u_rows[ds(b * BT, BT), :].rearrange("(k p) n -> p k n", p=P),
                             u_split).then_inc(S.u_out, 16)

            def load_expert(e):
                load_weights(e, (0, 1))
                load_lora(e)
                load_weights(e, (2,))

            load_weights(0, (0,))
            sp.dma_start(int_w2g, a.int_w2g.rearrange("(c p) n -> p c n", p=P)).then_inc(S.int_w2_in, 16)
            sp.dma_start(norm_flat, a.norm_rows.partition_broadcast(P)).then_inc(S.norm_in, 16)
            load_weights(0, (1, 2))
            sp.wait_ge(S.lora_lo, 2)
            sp.dma_start(lora_lo_d, lora_l).then_inc(S.lora_d_out, 16)
            sp.wait_ge(S.lora_d_out, 32)
            load_lora(0)
            sp.dma_start(xt_v[:, 2 * KB:, :], x_v[:, 2 * KB:, :]).then_inc(S.x_rest, 16)
            sp.dma_start(xT[:, :, 2 * BT:], xT_v[:, :, 2 * BT:]).then_inc(S.xT_rest, 16)
            load_expert(1)
            sp.dma_start(out[0:T, :], a.x).then_inc(S.out_in, 16)
            sp.dma_start(out[T:T + PAD, :], a.x[0:PAD, :]).then_inc(S.out_in, 16)
            with sp.Fori(2, E) as e:
                load_expert(e)
                store_rows(e - 2)
            store_rows(NB - 2)
            store_rows(NB - 1)
            sp.wait_ge(S.lg, NB)
            sp.wait_ge(S.u_lo, NB)
            sp.wait_ge(S.w_lo, E * HALVES)
            sp.wait_ge(S.u_out, 16 * NB)
            sp.dma_start(biases, a.biases.partition_broadcast(P)).then_inc(S.biases_in, 16)
            sp.wait_ge(S.added0, 16 * ((SLOT_TILES + 1) // 2))
            sp.wait_ge(S.added1, 16 * (SLOT_TILES // 2))

        @block.gpsimd
        def _(pool):
            eq, gt = ALU.not_equal, ALU.is_gt
            pool.memset(ident[:, :], 0.0).then_inc(S.const0, 1)
            pool.memset(setup_f, 1.0).then_inc(S.const0, 1)
            pool.memset(before8[:, :, :], 1.0).then_inc(S.const0, 1)
            pool.memset(minus_half, -0.5).then_inc(S.const0, 1)
            pool.memset(eps_sb, EPS).then_inc(S.const0, 1)
            pool.wait_ge(S.const0, 5)
            pool.affine_select(out=ident[:, :], in_=ident[:, :], compare_op=eq, fill=1.0, base=0,
                               pattern=[[-1, P]], channel_multiplier=1).then_inc(S.const, 1)
            pool.affine_select(out=setup_f, in_=setup_f, compare_op=gt, fill=0.0, base=0,
                               pattern=[[1, P]], channel_multiplier=-1).then_inc(S.const, 1)
            pool.affine_select(out=before8[:, :, :], in_=before8[:, :, :], compare_op=gt, fill=0.0, base=0,
                               pattern=[[1, E], [-1, E]], channel_multiplier=0).then_inc(S.const, 1)
            pool.iota(row16[:, 0:1], [[0, 1]], base=0, channel_multiplier=1).then_inc(S.const, 1)

            def gather_path(b):
                if not isinstance(b, int) or b:
                    pool.wait_ge(S.h_pre, b)
                n = b + 1
                pool.tensor_copy(path_now, path_ids[:, ds(b * KB, KB)]).then_inc(S.path_now, 1)
                before_plain(pool, S.path_now, n)
                for k in range(KB):
                    pool.indirect_dma_start(pw_rows[:, k, :], None, a.path_tab,
                                            bass.IndirectOffsetOnAxis(ap=path_now[:, k:k + 1], axis=0)
                                            ).then_inc(S.path_in, 16)

            def rstd(mv, ve, rs, mv_ready, n, shifted, done, count):
                pool.wait_ge(mv_ready, n)
                pool.tensor_tensor(ve, mv, eps_sb[0:rs.shape[0], 0:rs.shape[1]], ALU.add).then_inc(shifted, 1)
                pool.wait_ge(shifted, count)
                pool.tensor_tensor(rs, ve, minus_half[0:rs.shape[0], 0:rs.shape[1]], ALU.pow).then_inc(done, 1)

            def rstd_x(b):
                rstd(x_mv[:, :, 1], x_ve, x_rs, S.x_mv, (b + 1) * KB, S.x_ve, S.x_rstd, b + 1)

            def rstd_h(b):
                rstd(h_mv[:, :, 1], h_ve, h_rs, S.h_mv, (b + 1) * KB, S.h_ve, S.h_rstd, b + 1)

            def rstd_c(b):
                rstd(c_mv[:, :, 1], c_ve, c_rs, S.c_mv, (b + 1) * KB, S.c_ve, S.c_rstd, b + 1)

            def low_part(e, h):
                n = e * HALVES + h
                pool.wait_ge(S.w_hi, n + 1)
                pool.tensor_tensor(w_lo[:, ds(e * WE + h * HALF, HALF)], w_full[h % 3],
                                   w_hi[:, ds(e * WE + h * HALF, HALF)], ALU.subtract).then_inc(S.w_lo, 1)

            def scale_u(b):
                pool.wait_ge(S.chat, (b + 1) * KB)
                after(pool, S.uT_ps, b)
                after(pool, S.u_lo, b)
                g = norm_rows[:, 1:2, :].to_broadcast([P, KB, D])
                be = norm_rows[:, 2:3, :].to_broadcast([P, KB, D])
                pool.tensor_tensor(u, c_sb, g, ALU.mult).then_inc(S.u_scaled, 1)
                pool.wait_ge(S.u_scaled, b + 1)
                pool.tensor_tensor(u, u, be, ALU.add).then_inc(S.u, 1)

            pool.wait_ge(S.ids_in, 16)
            gather_path(0)
            pool.iota(iota_p[:, :], [[1, P]], base=0, channel_multiplier=0,
                      allow_small_or_imprecise_dtypes=True).then_inc(S.const, 1)
            pool.iota(iota_e[:, :], [[1, E]], base=0, channel_multiplier=0,
                      allow_small_or_imprecise_dtypes=True).then_inc(S.const, 1)
            pool.iota(iota_s[:, :], [[1, SLOT_TILES]], base=0, channel_multiplier=0,
                      allow_small_or_imprecise_dtypes=True).then_inc(S.const, 1)
            pool.iota(token1[:, :, :], [[0, K], [P, TILES]], base=1, channel_multiplier=1,
                      allow_small_or_imprecise_dtypes=True).then_inc(S.const, 1)
            pool.iota(pad_row[:, :], [[0, 1]], base=T + 1, channel_multiplier=1,
                      allow_small_or_imprecise_dtypes=True).then_inc(S.const, 1)
            pool.memset(ones16[:, :], 1.0).then_inc(S.const, 1)
            rstd_x(0)
            rstd_h(0)
            gather_path(1)
            pool.wait_ge(S.lora_hi, 2)
            for n, part_ in enumerate((slice(0, LA), slice(LA, LORA))):
                pool.tensor_tensor(lora_l[:, part_], lora_f[:, part_], lora_h[:, part_], ALU.subtract).then_inc(S.lora_lo, 1)

            def block_of(b, first=False, last=False, paths=True):
                if not first:
                    rstd_c(b - 1)
                if not last:
                    rstd_x(b + 1)
                low_part(b, 0)
                if first:
                    rstd(mlp_mv[0:NBATCH, :, 1], v_ve[0:NBATCH, :], v_rs[0:NBATCH, :], S.v_mv, 3, S.v_ve, S.v_rstd, 1)
                else:
                    scale_u(b - 1)
                if not last:
                    rstd_h(b + 1)
                for h in range(1, 4):
                    low_part(b, h)
                if paths:
                    gather_path(b + 2)
                for h in range(4, HALVES):
                    low_part(b, h)

            block_of(0, first=True)
            block_of(1)
            with pool.Fori(2, NB - 2) as b:
                block_of(b)
            block_of(NB - 2, paths=False)
            block_of(NB - 1, last=True, paths=False)
            rstd_c(NB - 1)
            scale_u(NB - 1)

            def gather_rows(i, h, v):
                after(pool, (S.rowsT_ps0, S.rowsT_ps1)[v], h)
                n = i + 1
                pool.tensor_copy(gather_now[v], slot_rows[:, ds(i, 1), 0]).then_inc(S.gather_now, 1)
                before_plain(pool, S.gather_now, n)
                pool.indirect_dma_start(rows_in[v], None, u_rows,
                                        bass.IndirectOffsetOnAxis(ap=gather_now[v], axis=0)
                                        ).then_inc((S.rows0, S.rows1)[v], 16)

            def add_rows(i, h, v):
                after(pool, (S.added1, S.added0)[v], 16 * (h + v))
                n = i + 1
                pool.tensor_copy(scatter_now[v], slot_rows[:, ds(i, 1), 1]).then_inc(S.scatter_now, 1)
                pool.wait_ge(S.scatter_now, n)
                before_plain(pool, S.y_gated, n)
                pool.indirect_dma_start(out, bass.IndirectOffsetOnAxis(ap=scatter_now[v], axis=0),
                                        y_gated[v], None, compute_op=ALU.add
                                        ).then_inc((S.added0, S.added1)[v], 16)

            pool.wait_ge(S.u_out, 16 * NB)
            pool.wait_ge(S.slot_rows, 2)
            pool.wait_ge(S.out_in, 32)
            ahead = 5
            for i in range(ahead):
                gather_rows(i, i // 2, i % 2)
            for i in range(2):
                add_rows(i, 0, i)
                gather_rows(i + ahead, (i + ahead) // 2, (i + ahead) % 2)
            turns = (SLOT_TILES - ahead) // 2
            with pool.Fori(1, turns) as m:
                for v in range(2):
                    add_rows(m * 2 + v, m, v)
                    gather_rows(m * 2 + v + ahead, m + (v + ahead) // 2, 1 - v)
            for i in range(2 * turns, SLOT_TILES):
                add_rows(i, i // 2, i % 2)
                if i + ahead < SLOT_TILES:
                    gather_rows(i + ahead, (i + ahead) // 2, (i + ahead) % 2)

        @block.scalar
        def _(act):
            act.dma_start(aw_sb, a.aw.partition_broadcast(P)).then_inc(S.aw_in, 16)
            act.dma_start(gain_f, a.gains).then_inc(S.gain_in, 16)
            act.dma_start(shift_Z, a.shiftZ.rearrange("(c p) k r -> p c k r", p=P)).then_inc(S.shift_in, 16)
            act.dma_start(lora_f, a.lora).then_inc(S.lora_in, 16)
            act.wait_ge(S.aw_max, 1)
            act.activation(aw_e, aw_sb, ACT.Exp, bias=aw_m, accum_out=aw_s).then_inc(S.aw_exp, 1)
            act.wait_ge(S.lora_in, 16)
            act.activation(lora_f[:, 0:LA], lora_f[:, 0:LA], ACT.Copy, scale=WSCALE).then_inc(S.lora_scaled, 1)
            act.copy(lora_h[:, LA:], lora_f[:, LA:]).then_inc(S.lora_hi, 1)
            act.wait_ge(S.lora_scaled, 1)
            act.copy(lora_h[:, 0:LA], lora_f[:, 0:LA]).then_inc(S.lora_hi, 1)
            act.wait_ge(S.lora_hi, 2)
            act.dma_start(lora_hi_d, lora_h).then_inc(S.lora_d_out, 16)
            act.wait_ge(S.mlp_h_ps, 1)
            for k in range(3):
                for c in range(DC):
                    act.activation(mlp_h[:, k, c, :], ps_lora[:, (k * DC + c) * 2:(k * DC + c) * 2 + 2], ACT.Silu,
                                   bias=mlp_b1[:, k, c:c + 1]).then_inc(S.mlp_h, 1)

            def high_part(e, h):
                n = e * HALVES + h
                act.wait_ge(S.w_sum, n + 1)
                act.copy(w_hi[:, ds(e * WE + h * HALF, HALF)], w_full[h % 3]).then_inc(S.w_hi, 1)

            def copy_T(b):
                act.wait_ge(S.xT_ps, b + 1)
                after(act, S.prod_s, b)
                act.copy(xhT, ps_xT[:, :]).then_inc(S.xhT, 1)
                act.wait_ge(S.hT_ps, b + 1)
                after(act, S.prod_h, b)
                act.copy(hhT, ps_hT[:, :]).then_inc(S.hhT, 1)

            def hidden(b):
                act.wait_ge(S.l1_ps, b + 1)
                after(act, S.l2_ps, b)
                for c in range(DC):
                    act.activation(zT[:, c, :], ps_l1[:, c * BT:(c + 1) * BT], ACT.Silu,
                                   bias=bias_blk[:, ds(b * DC + c, 1)]).then_inc(S.zT, 1)

            def u_high(b):
                act.wait_ge(S.u, b + 1)
                after(act, S.u_out, 16 * b)
                act.copy(u_split[:, :, 0:D], u).then_inc(S.u_hi, 1)

            def copy_uT(b):
                act.wait_ge(S.uT_ps, b + 1)
                after(act, S.lg_ps, b)
                act.copy(uT_sb, ps_u[:, :]).then_inc(S.uT, 1)

            copy_T(0)

            def block_of(b, first=False, last=False):
                high_part(b, 0)
                if not first:
                    u_high(b - 1)
                high_part(b, 1)
                if first:
                    act.wait_ge(S.bias_blk, DC * NBATCH)
                hidden(b)
                high_part(b, 2)
                if not first:
                    copy_uT(b - 1)
                if not last:
                    copy_T(b + 1)
                for h in range(3, HALVES):
                    high_part(b, h)

            block_of(0, first=True)
            block_of(1)
            with act.Fori(2, NB - 1) as b:
                block_of(b)
            block_of(NB - 1, last=True)
            u_high(NB - 1)
            copy_uT(NB - 1)

            act.wait_ge(S.gap, 1)
            act.activation(e2, gap, ACT.Exp).then_inc(S.e2, 1)

            def copy_rowsT(i, v):
                act.wait_ge((S.rowsT_ps0, S.rowsT_ps1)[v], i[1] + 1)
                after(act, S.h3_ps, i[0] - 1)
                act.copy(rowsT[v], ps_rowsT[v]).then_inc(S.rowsT, 1)

            def silu_of(i, v):
                act.wait_ge(S.h1, i[0] + 1)
                act.activation(silu_sb[v], h1_sb[v], ACT.Silu).then_inc(S.silu, 1)

            def gT_high(i, v):
                act.wait_ge(S.gT_ps, i[0] + 1)
                after(act, S.y_ps, i[0] - 1)
                act.copy(gT_hi[v], ps_gT[:, :]).then_inc(S.gT_hi, 1)

            def gated(i, v):
                act.wait_ge(S.y, i[0] + 1)
                after(act, (S.added0, S.added1)[v], 16 * i[1])
                act.activation(y_gated[v], y_sb[v], ACT.Copy, scale=slot_gate[:, ds(i[0], 1)]).then_inc(S.y_gated, 1)

            def step(i, h, v, peeled=False):
                n = SLOT_TILES
                if not peeled or i + 1 < n:
                    copy_rowsT((i + 1, h + v), 1 - v)
                if not peeled or 1 <= i <= n:
                    gT_high((i - 1, h - 1 + v), 1 - v)
                if not peeled or i < n:
                    silu_of((i, h), v)
                if not peeled or 2 <= i:
                    gated((i - 2, h - 1), v)

            act.wait_ge(S.slot_gate, 1)
            copy_rowsT((0, 0), 0)
            for i in range(4):
                step(i, i // 2, i % 2, peeled=True)
            turns = (SLOT_TILES - 5) // 2
            with act.Fori(2, 2 + turns) as m:
                for v in range(2):
                    step(m * 2 + v, m, v)
            for i in range(4 + 2 * turns, SLOT_TILES + 2):
                step(i, i // 2, i % 2, peeled=True)

        @block.vector
        def _(dve):
            mul, add, sub = ALU.mult, ALU.add, ALU.subtract

            def norm_x(b):
                n = (b + 1) * KB
                for k in range(KB):
                    dve.bn_stats(x_st[:, 6 * k:6 * k + 6], x_tok[:, ds((b * KB + k) * D, D)]).then_inc(S.x_st, 1)
                before_plain(dve, S.x_st, n)
                for k in range(KB):
                    dve.bn_aggr(x_mv[:, k, :], x_st[:, 6 * k:6 * k + 6]).then_inc(S.x_mv, 1)

            def norm_h(b):
                n = (b + 1) * KB
                dve.wait_ge(S.x_rstd, b + 1)
                after(dve, S.xT_ps, b)
                for k in range(KB):
                    dve.tensor_scalar(xh[:, k, :], x_tok[:, ds((b * KB + k) * D, D)], x_mv[:, k, 0:1],
                                      x_rs[:, k:k + 1], sub, mul).then_inc(S.xhat, 1)
                dve.wait_ge(S.xhat, (b + 1) * KB)
                dve.wait_ge(S.path_in, (b + 1) * KB * 16)
                after(dve, S.hT_ps, b)
                dve.tensor_tensor(hh, xh, pw_rows[:, :, 0:D], mul).then_inc(S.h_scaled, 1)
                dve.wait_ge(S.h_scaled, b + 1)
                dve.tensor_tensor(hh, hh, pw_rows[:, :, D:], add).then_inc(S.h_pre, 1)
                dve.wait_ge(S.h_pre, b + 1)
                for k in range(KB):
                    dve.bn_stats(h_st[:, 6 * k:6 * k + 6], hh[:, k, :]).then_inc(S.h_st, 1)
                before_plain(dve, S.h_st, n)
                for k in range(KB):
                    dve.bn_aggr(h_mv[:, k, :], h_st[:, 6 * k:6 * k + 6]).then_inc(S.h_mv, 1)

            def finish_h(b):
                dve.wait_ge(S.h_rstd, b + 1)
                for k in range(KB):
                    dve.tensor_scalar(hh[:, k, :], hh[:, k, :], h_mv[:, k, 0:1], h_rs[:, k:k + 1],
                                      sub, mul).then_inc(S.hhat, 1)

            def products_x(b):
                dve.wait_ge(S.xhT, b + 1)
                dve.wait_ge(S.gt_ps, b + 1)
                after(dve, S.l1_ps, b)
                dve.tensor_tensor(prod_t, xhT, ps_g0[:, :], mul).then_inc(S.prod_t, 1)
                dve.wait_ge(S.gs_ps, b + 1)
                dve.tensor_tensor(prod_s, xhT, ps_g1[:, :], mul).then_inc(S.prod_s, 1)

            def products_h(b):
                dve.wait_ge(S.hhT, b + 1)
                dve.wait_ge(S.gh_ps, b + 1)
                dve.tensor_tensor(prod_h, hhT, ps_g0[:, :], mul).then_inc(S.prod_h, 1)

            def second_layer(b):
                n = (b + 1) * KB
                dve.wait_ge(S.l2_ps, b + 1)
                after(dve, S.u_scaled, b)
                dve.tensor_tensor(c_sb, ps_l2[:, :].rearrange("p (k d) -> p k d", k=KB),
                                  norm_rows[:, 0:1, :].to_broadcast([P, KB, D]), add).then_inc(S.c, 1)
                dve.wait_ge(S.c, b + 1)
                for k in range(KB):
                    dve.bn_stats(c_st[:, 6 * k:6 * k + 6], c_sb[:, k, :]).then_inc(S.c_st, 1)
                before_plain(dve, S.c_st, n)
                for k in range(KB):
                    dve.bn_aggr(c_mv[:, k, :], c_st[:, 6 * k:6 * k + 6]).then_inc(S.c_mv, 1)

            def norm_c(b):
                dve.wait_ge(S.c_rstd, b + 1)
                for k in range(KB):
                    dve.tensor_scalar(c_sb[:, k, :], c_sb[:, k, :], c_mv[:, k, 0:1], c_rs[:, k:k + 1],
                                      sub, mul).then_inc(S.chat, 1)

            def u_low(b):
                dve.wait_ge(S.u_hi, b + 1)
                dve.tensor_tensor(u_split[:, :, D:], u, u_split[:, :, 0:D], sub).then_inc(S.u_lo, 1)

            def top_two(b):
                n = (b + 1) * KB
                dve.wait_ge(S.lg_ps, b + 1)
                after(dve, S.top_e, b * 2)
                dve.tensor_copy(lg_sb, ps_u[:, 0:KB * E]).then_inc(S.lg, 1)
                before_plain(dve, S.lg, b + 1)
                for k in range(KB):
                    dve.max(top_now[:, k * 8:(k + 1) * 8], lg_sb[:, k * E:(k + 1) * E]).then_inc(S.top, 1)
                before_plain(dve, S.top, n)
                for k in range(KB):
                    dve.max_index(top_e_now[:, k * 8:(k + 1) * 8], top_now[:, k * 8:(k + 1) * 8],
                                  lg_sb[:, k * E:(k + 1) * E]).then_inc(S.top_i, 1)
                dve.wait_ge(S.top_i, (b + 1) * KB)
                dve.tensor_copy(top[:, ds(b * KB * 8, KB * 8)], top_now).then_inc(S.top_e, 1)
                dve.tensor_copy(top_e[:, ds(b * KB * 8, KB * 8)], top_e_now).then_inc(S.top_e, 1)

            def merge(e, h):
                n = e * HALVES + h
                dve.wait_ge(S.lora_ps, n + 1)
                dve.wait_ge((S.w1s_in, S.w3s_in, S.w2s_in)[h // 2], (e + 1) * 16)
                after(dve, S.w_lo, n - 2)
                dve.scalar_tensor_tensor(w_full[h % 3], w_stage[h // 2][:, (h % 2) * HALF:(h % 2 + 1) * HALF],
                                         WSCALE, ps_lora[:, :], mul, add).then_inc(S.w_sum, 1)

            def split_table(kinds, n):
                dve.wait_ge(S.gain_s, 3 + n)
                dve.tensor_copy(gain_tab[:, kinds, :], gain_f[:, kinds, :]).then_inc(S.tab, 1)
                dve.wait_ge(S.tab, 5 * n + 1)
                dve.tensor_tensor(gain_r[:, kinds, :], gain_f[:, kinds, :], gain_tab[:, kinds, :], sub).then_inc(S.tab, 1)
                dve.wait_ge(S.tab, 5 * n + 2)
                dve.tensor_copy(gain_tab[32:64, kinds, :], gain_r[32:64, kinds, :]).then_inc(S.tab, 1)
                dve.tensor_copy(gain_h[:, kinds, :], gain_r[:, kinds, :]).then_inc(S.tab, 1)
                dve.wait_ge(S.tab, 5 * n + 4)
                dve.tensor_tensor(gain_tab[64:96, kinds, :], gain_r[64:96, kinds, :], gain_h[64:96, kinds, :], sub).then_inc(S.tab, 1)

            dve.wait_ge(S.aw_in, 16)
            dve.tensor_reduce(aw_m, aw_sb, AX_X, ALU.max, negate=True).then_inc(S.aw_max, 1)
            dve.wait_ge(S.x_first, 16)
            norm_x(0)
            dve.wait_ge(S.const, 4)
            dve.tensor_copy(ident16[:, :], ident[:, :]).then_inc(S.const_d, 1)
            dve.tensor_copy(before[:, :], setup_f).then_inc(S.const_d, 1)
            dve.tensor_scalar(row16[:, 1:2], row16[:, 0:1], 15, None, ALU.bitwise_and).then_inc(S.row16, 1)
            dve.wait_ge(S.row16, 1)
            dve.tensor_copy(row16_f, row16[:, 1:2]).then_inc(S.row16, 1)
            dve.wait_ge(S.aw_exp, 1)
            dve.reciprocal(aw_r, aw_s).then_inc(S.mixw, 1)
            dve.wait_ge(S.mixw, 1)
            dve.tensor_scalar(mixw, aw_e, aw_r, None, mul).then_inc(S.mixw, 1)
            dve.wait_ge(S.mixw, 2)
            dve.wait_ge(S.gain_in, 16)
            for k, w in enumerate((0, 1, 5)):
                dve.tensor_scalar(gain_f[:, k, :], gain_f[:, k, :], mixw[0:ROWS, w:w + 1], None, mul).then_inc(S.gain_s, 1)
            dve.wait_ge(S.shift_in, 16)
            for k, w in enumerate((0, 1, 5)):
                dve.tensor_scalar(shift_Z[:, :, k, :], shift_Z[:, :, k, :], mixw[:, w:w + 1], None, mul).then_inc(S.shift_z, 1)
            norm_h(0)
            dve.wait_ge(S.onehot_ids_in, 16)
            dve.wait_ge(S.row16, 2)
            dve.tensor_scalar(onehot, ids_i[0:ROWS, :], row16_f[0:ROWS, :], None, ALU.is_equal).then_inc(S.onehot, 1)
            finish_h(0)
            split_table(slice(0, NKIND), 0)
            dve.wait_ge(S.shift_ps, 1)
            dve.tensor_copy(gain_f[:, 3, :], ps_hT[0:ROWS, 0:D]).then_inc(S.gain_s, 1)
            split_table(slice(NKIND, NKIND + 1), 1)
            dve.wait_ge(S.w1x_in, 16)
            dve.tensor_scalar(wx, int_w1[:, 4:6, :], mixw[:, 2:3], None, mul).then_inc(S.wx, 1)
            for n in (3, 4):
                dve.wait_ge(S.wx, n - 2)
                dve.scalar_tensor_tensor(wx, int_w1[:, 2 * n:2 * n + 2, :], mixw[:, n:n + 1], wx, mul, add).then_inc(S.wx, 1)
            products_x(0)
            products_h(0)

            v = mlp_v[0:NBATCH, :, :]

            def networks_add():
                dve.wait_ge(S.mlp_o_ps, 1)
                dve.wait_ge(S.net_rows_in, 16)
                dve.tensor_tensor(v[:, 0:2, :], ps_u[0:NBATCH, :].rearrange("p (k n) -> p k n", k=2),
                                  mlp_b2[0:NBATCH, 0:2, :], add).then_inc(S.v, 1)
                dve.tensor_tensor(v[:, 2, :], ps_l2[0:NBATCH, 0:D], mlp_b2[0:NBATCH, 2, :], add).then_inc(S.v, 1)
                dve.wait_ge(S.v, 2)
                for k in range(3):
                    dve.bn_stats(mlp_st[0:NBATCH, k, :], v[:, k, :]).then_inc(S.v_st, 1)
                dve.wait_ge(S.v_st, 3)
                for k in range(3):
                    dve.bn_aggr(mlp_mv[0:NBATCH, k, :], mlp_st[0:NBATCH, k, :]).then_inc(S.v_mv, 1)

            def networks_norm():
                dve.wait_ge(S.v_rstd, 1)
                for k in range(3):
                    dve.tensor_scalar(v[:, k, :], v[:, k, :], mlp_mv[0:NBATCH, k, 0:1], v_rs[0:NBATCH, k:k + 1],
                                      sub, mul).then_inc(S.v, 1)
                dve.wait_ge(S.v, 5)
                dve.tensor_tensor(v, v, mlp_g[0:NBATCH, :, :], mul).then_inc(S.v, 1)
                dve.wait_ge(S.v, 6)
                dve.tensor_tensor(v, v, mlp_be[0:NBATCH, :, :], add).then_inc(S.v, 1)
                dve.wait_ge(S.v, 7)
                for k in range(3):
                    dve.tensor_scalar(v[:, k, :], v[:, k, :], mixw[0:NBATCH, 2 + k:3 + k], None, mul).then_inc(S.v, 1)
                dve.wait_ge(S.vT_ps, 1)
                dve.tensor_copy(mlp_vT, ps_l2[:, D:D + 12].rearrange("p (k b) -> p k b", b=NBATCH)).then_inc(S.vT, 1)
                dve.wait_ge(S.bias_ps, 1)
                for bat in range(NBATCH):
                    for c in range(DC):
                        n = NB // NBATCH
                        dst = bias_blk.rearrange("p (b c) -> p b c", c=DC)[:, bat * n:(bat + 1) * n, c]
                        src = ps_u[:, c * NBATCH + bat:c * NBATCH + bat + 1].to_broadcast([P, n])
                        dve.tensor_scalar(dst, src, int_b1[:, c:c + 1], None, add).then_inc(S.bias_blk, 1)

            def block_of(b, first=False, last=False):
                if not first:
                    second_layer(b - 1)
                if not last:
                    norm_x(b + 1)
                if not first:
                    norm_c(b - 1)
                merge(b, 0)
                if first:
                    networks_add()
                if not last:
                    norm_h(b + 1)
                merge(b, 1)
                if first:
                    networks_norm()
                if not last:
                    finish_h(b + 1)
                merge(b, 2)
                if not first:
                    u_low(b - 1)
                if not last:
                    products_x(b + 1)
                merge(b, 3)
                if not first:
                    top_two(b - 1)
                if not last:
                    products_h(b + 1)
                merge(b, 4)
                merge(b, 5)

            block_of(0, first=True)
            dve.wait_ge(S.x_rest, 16)
            dve.wait_ge(S.norm_in, 16)
            block_of(1)
            with dve.Fori(2, NB - 1) as b:
                block_of(b)
            block_of(NB - 1, last=True)
            second_layer(NB - 1)
            norm_c(NB - 1)
            u_low(NB - 1)
            top_two(NB - 1)

            dve.wait_ge(S.const, 10)
            top3 = top[:, :].rearrange("p (j n) -> p j n", n=8)
            tope3 = top_e[:, :].rearrange("p (j n) -> p j n", n=8)
            dve.wait_ge(S.top_e, 2 * NB)
            dve.wait_ge(S.w_lo, E * HALVES)
            dve.wait_ge(S.u_out, 16 * NB)
            ie = iota_e[:, :].unsqueeze(1).to_broadcast([P, TILES, E])
            for k in range(K):
                dve.tensor_tensor(chosen[:, k, :, :], ie, tope3[:, :, k:k + 1].to_broadcast([P, TILES, E]),
                                  ALU.is_equal).then_inc(S.chosen, 1)
            dve.memset(picked[:, TILES, :], 0.0).then_inc(S.picked, 1)
            dve.tensor_tensor(gap, top3[:, :, 1], top3[:, :, 0], sub).then_inc(S.gap, 1)
            dve.wait_ge(S.chosen, 2)
            dve.tensor_tensor(picked[:, 0:TILES, :], chosen[:, 0, :, :], chosen[:, 1, :, :], add).then_inc(S.picked, 1)
            dve.wait_ge(S.e2, 1)
            dve.tensor_scalar(den, e2, 1.0, None, add).then_inc(S.gate, 1)
            dve.wait_ge(S.gate, 1)
            dve.reciprocal(gate[:, 0, :], den).then_inc(S.gate, 1)
            dve.wait_ge(S.gate, 2)
            dve.tensor_tensor(gate[:, 1, :], gate[:, 0, :], e2, mul).then_inc(S.gate, 1)
            dve.wait_ge(S.gate, 3)
            dve.tensor_copy(gate_h, gate).then_inc(S.gate, 1)
            dve.wait_ge(S.gate, 4)
            dve.tensor_tensor(gate_f, gate, gate_h, sub).then_inc(S.gate, 1)
            dve.wait_ge(S.place_ps, 1)
            counts = ps_l1[:, 0:(TILES + 1) * E].rearrange("p (j e) -> p j e", e=E)
            dve.tensor_scalar(tiles_i, counts[:, TILES, :], float(P - 1), None, add).then_inc(S.tiles, 1)
            dve.wait_ge(S.tiles, 1)
            dve.tensor_scalar(tiles_i, tiles_i, 7, None, ALU.logical_shift_right).then_inc(S.tiles, 1)
            dve.wait_ge(S.tiles, 2)
            dve.tensor_tensor(tri_f, before8[:, :, :], tiles_i.unsqueeze(1).to_broadcast([P, E, E]), mul).then_inc(S.tiles, 1)
            dve.wait_ge(S.tiles, 3)
            dve.tensor_reduce(first_tile, tri_f, AX_X, add).then_inc(S.tiles, 1)
            dve.wait_ge(S.tiles, 4)
            dve.scalar_tensor_tensor(place, first_tile.unsqueeze(1).to_broadcast([P, TILES, E]), float(P),
                                     counts[:, 0:TILES, :], mul, add).then_inc(S.place, 1)
            dve.wait_ge(S.place, 1)
            for k in range(K):
                dve.tensor_tensor(place2[:, k, :, :], chosen[:, k, :, :], place, mul).then_inc(S.place, 1)
            dve.wait_ge(S.place, 3)
            dve.tensor_reduce(slot_f.rearrange("p (n o) -> p n o", o=1), place2.rearrange("p k j e -> p (k j) e"),
                              AX_X, add).then_inc(S.place, 1)
            dve.wait_ge(S.place, 4)
            dve.tensor_copy(slot_i, slot_f).then_inc(S.place, 1)
            dve.wait_ge(S.place, 5)
            dve.tensor_scalar(slot_tile, slot_i, 7, None, ALU.logical_shift_right).then_inc(S.place, 1)
            dve.tensor_scalar(slot_col, slot_i, P - 1, None, ALU.bitwise_and).then_inc(S.place, 1)
            dve.wait_ge(S.place, 7)
            dve.tensor_copy(slot_tile_f, slot_tile).then_inc(S.place, 1)
            dve.tensor_copy(slot_col_f, slot_col).then_inc(S.place, 1)
            dve.wait_ge(S.place, 9)
            dve.tensor_tensor(in_tile, iota_s[:, :].unsqueeze(1).to_broadcast([P, NC_, SLOT_TILES]),
                              slot_tile_f.unsqueeze(2).to_broadcast([P, NC_, SLOT_TILES]), ALU.is_equal).then_inc(S.in_tile, 1)
            dve.wait_ge(S.in_tile, 1)
            dve.wait_ge(S.gate, 5)
            for n, val in enumerate((token1[:, :, :], gate_h, gate_f)):
                vv = val.rearrange("p k j -> p (k j)").unsqueeze(2).to_broadcast([P, NC_, SLOT_TILES])
                dve.tensor_tensor(tile_val[:, :, n, :], in_tile, vv, mul).then_inc(S.tile_val, 1)
            for n in range(NC_):
                dve.tensor_scalar(col_hot[:, n, :], iota_p[:, :], slot_col_f[:, n:n + 1], None,
                                  ALU.is_equal).then_inc(S.col_hot, 1)
            dve.tensor_tensor(started, first_tile.unsqueeze(1).to_broadcast([P, SLOT_TILES, E]),
                              iota_s[:, :].unsqueeze(2).to_broadcast([P, SLOT_TILES, E]), ALU.is_le).then_inc(S.started, 1)
            dve.wait_ge(S.started, 1)
            dve.tensor_reduce(started_n, started, AX_X, add).then_inc(S.started, 1)
            dve.wait_ge(S.started, 2)
            dve.tensor_scalar(tile_expert, started_n, -1.0, None, add).then_inc(S.tile_expert, 1)
            dve.wait_ge(S.slots_ps, 1)
            dve.tensor_copy(slot_v, ps_l2[:, 0:3 * SLOT_TILES].rearrange("p (v s) -> p v s", v=3)).then_inc(S.slot_v, 1)
            dve.wait_ge(S.slot_v, 1)
            dve.tensor_scalar(slot_rows[:, :, 0], slot_v[:, 0, :], -1.0, 0.0, add, ALU.max).then_inc(S.slot_rows, 1)
            dve.tensor_scalar(empty, slot_v[:, 0, :], 0.0, pad_row[:, 0:1], ALU.is_equal, mul).then_inc(S.slot_v, 1)
            dve.tensor_tensor(slot_gate, slot_v[:, 1, :], slot_v[:, 2, :], add).then_inc(S.slot_gate, 1)
            dve.wait_ge(S.slot_v, 2)
            dve.scalar_tensor_tensor(slot_rows[:, :, 1], slot_v[:, 0, :], -1.0, empty, add, add).then_inc(S.slot_rows, 1)

            inv = 1.0 / WSCALE

            def bias_of(i):
                e = dve.value_load(tile_expert[0:1, ds(i, 1)], min_val=0, max_val=E - 1)
                return e * BE

            def h1_of(i, v, at):
                dve.wait_ge(S.h1_ps, i + 1)
                after(dve, S.silu, i - 1)
                dve.scalar_tensor_tensor(h1_sb[v], ps_h1[v][:, :], inv, biases[:, ds(at, H)], mul, add).then_inc(S.h1, 1)

            def g_of(i, v, at):
                dve.wait_ge(S.h3_ps, i + 1)
                dve.scalar_tensor_tensor(h3_sb[v], ps_h3[v][:, :], inv, biases[:, ds(at + H, H)], mul, add).then_inc(S.h3, 1)
                dve.wait_ge(S.h3, i + 1)
                dve.wait_ge(S.silu, i + 1)
                after(dve, S.gT_ps, i - 1)
                dve.tensor_tensor(g_sb[v], h3_sb[v], silu_sb[v], mul).then_inc(S.g, 1)

            def gT_low(i, v):
                dve.wait_ge(S.gT_hi, i + 1)
                dve.tensor_tensor(gT_lo[v], ps_gT[:, :], gT_hi[v], sub).then_inc(S.gT_lo, 1)

            def y_of(i, v):
                at = bias_of(i)
                dve.wait_ge(S.y_ps, i + 1)
                after(dve, S.y_gated, i - 1)
                dve.scalar_tensor_tensor(y_sb[v], ps_y[:, 0:D], inv, biases[:, ds(at + 2 * H, D)], mul, add).then_inc(S.y, 1)

            def step(i, v, peeled=False):
                n = SLOT_TILES
                if not peeled or 1 <= i <= n:
                    gT_low(i - 1, 1 - v)
                if not peeled or i < n:
                    at = bias_of(i)
                    h1_of(i, v, at)
                    g_of(i, v, at)
                if not peeled or 2 <= i:
                    y_of(i - 2, v)

            dve.wait_ge(S.tile_expert, 1)
            dve.wait_ge(S.biases_in, 16)
            for i in range(4):
                step(i, i % 2, peeled=True)
            turns = (SLOT_TILES - 5) // 2
            with dve.Fori(2, 2 + turns) as m:
                for v in range(2):
                    step(m * 2 + v, v)
            for i in range(4 + 2 * turns, SLOT_TILES + 2):
                step(i, i % 2, peeled=True)

        @block.tensor
        def _(pe):
            def transpose_T(b):
                for src, ready, freed, dst, done in ((xh, S.xhat, S.xhT, ps_xT, S.xT_ps),
                                                     (hh, S.hhat, S.hhT, ps_hT, S.hT_ps)):
                    pe.wait_ge(ready, (b + 1) * KB)
                    after(pe, freed, b)
                    for k in range(KB):
                        for c in range(DC):
                            last = pe.transpose(dst[:, c * BT + k * P:c * BT + (k + 1) * P],
                                                src[:, k, c * P:(c + 1) * P], ident[:, :])
                    last.then_inc(done, 1)

            def gains(b, kind, dst, freed, n, done):
                after(pe, freed, n)
                for c in range(DC):
                    last = pe.matmul(dst[:, c * BT:(c + 1) * BT], gain_tab[:, kind, c * P:(c + 1) * P],
                                     onehot[:, ds(b * BT, BT)], start=True, stop=True)
                last.then_inc(done, 1)

            def lora(e, h):
                n = e * HALVES + h
                if h == 0:
                    pe.wait_ge(S.lora_k_in, 80 * (e + 1))
                after(pe, S.w_sum, n)
                if h < 4:
                    a0, b0 = (h // 2) * D + (h % 2) * P, LA + (h // 2) * H
                    last = pe.matmul(ps_lora[:, :], lora_k[0:3 * R, a0:a0 + P], lora_k[0:3 * R, b0:b0 + H],
                                     start=True, stop=True)
                else:
                    for c in range(2):
                        a0, b0 = 2 * D + ((h % 2) * 2 + c) * P, LA + 2 * H
                        last = pe.matmul(ps_lora[:, c * D:(c + 1) * D], lora_k[0:3 * R, a0:a0 + P],
                                         lora_k[0:3 * R, b0:b0 + D], start=True, stop=True)
                last.then_inc(S.lora_ps, 1)

            def layer1(b, c, between):
                hid = slice(c * P, (c + 1) * P)
                o = ps_l1[:, c * BT:(c + 1) * BT]
                if c == 0:
                    after(pe, S.zT, b * DC)
                for n in range(DC):
                    pe.matmul(o, wx[:, n, hid], xT[:, n, ds(b * BT, BT)], start=(n == 0), stop=False)
                pe.matmul(o, gain_tab[:, 3, hid], onehot[:, ds(b * BT, BT)], start=False, stop=False)
                for prod, ready, w in ((prod_t, S.prod_t, 2), (prod_s, S.prod_s, 10), (prod_h, S.prod_h, 0)):
                    if c == 0:
                        pe.wait_ge(ready, b + 1)
                    for n in range(DC):
                        last = pe.matmul(o, int_w1[:, w + n, hid], prod[:, n * BT:(n + 1) * BT],
                                         start=False, stop=(w == 0 and n == DC - 1))
                    if w == 2:
                        between()
                if c == DC - 1:
                    last.then_inc(S.l1_ps, 1)

            def layer2(b):
                pe.wait_ge(S.zT, (b + 1) * DC)
                after(pe, S.c, b)
                for k in range(KB):
                    for c in range(DC):
                        last = pe.matmul(ps_l2[:, k * D:(k + 1) * D], zT[:, c, k * P:(k + 1) * P], int_w2[:, c, :],
                                         start=(c == 0), stop=(c == DC - 1))
                last.then_inc(S.l2_ps, 1)

            def transpose_u(b):
                pe.wait_ge(S.u, b + 1)
                after(pe, S.lg, b)
                for n in range(KB * DC):
                    last = pe.transpose(ps_u[:, n * P:(n + 1) * P], u[:, n // DC, (n % DC) * P:(n % DC + 1) * P],
                                        ident[:, :])
                last.then_inc(S.uT_ps, 1)

            def logits(b):
                pe.wait_ge(S.uT, b + 1)
                for k in range(KB):
                    for c in range(DC):
                        last = pe.matmul(ps_u[:, k * E:(k + 1) * E], uT_sb[:, (k * DC + c) * P:(k * DC + c + 1) * P],
                                         wgT[:, c, :], start=(c == 0), stop=(c == DC - 1))
                last.then_inc(S.lg_ps, 1)

            def gains_ts(b):
                gains(b, 1, ps_g0, S.prod_h, b, S.gt_ps)
                gains(b, 2, ps_g1, S.prod_s, b, S.gs_ps)

            def gains_h(b):
                gains(b, 0, ps_g0, S.prod_t, b + 1, S.gh_ps)

            pe.wait_ge(S.w1_in, 32)
            pe.wait_ge(S.shift_z, 3)
            for n, (k, c) in enumerate((k, c) for k in range(NKIND) for c in range(DC)):
                last = pe.matmul(ps_hT[0:ROWS, 0:D], shift_Z[:, c, k, :], int_w1[:, (0, 2, 10)[k] + c, :],
                                 start=(n == 0), stop=(n == 2 * NKIND - 1))
            last.then_inc(S.shift_ps, 1)
            pe.wait_ge(S.net_in, 16)
            for k, n in enumerate((128, 64, 32)):
                for c in range(DC):
                    last = pe.matmul(ps_lora[:, (k * DC + c) * 2:(k * DC + c) * 2 + 2], mlp_w1[0:n, k, c * P:(c + 1) * P],
                                     mlp_s[0:n, k, :], start=True, stop=True)
            last.then_inc(S.mlp_h_ps, 1)
            pe.wait_ge(S.gain_s, 4)
            pe.wait_ge(S.const, 1)
            transpose_T(0)
            pe.wait_ge(S.tab, 10)
            pe.wait_ge(S.onehot, 1)
            gains_ts(0)
            gains_h(0)
            pe.wait_ge(S.xT_first, 16)
            pe.wait_ge(S.wx, 3)

            def networks_layer2():
                pe.wait_ge(S.mlp_h, 6)
                for k in range(3):
                    o = ps_u[0:NBATCH, k * D:(k + 1) * D] if k < 2 else ps_l2[0:NBATCH, 0:D]
                    for c in range(DC):
                        last = pe.matmul(o, mlp_h[:, k, c, :], mlp_w2[:, k, c, :], start=(c == 0), stop=(c == DC - 1))
                last.then_inc(S.mlp_o_ps, 1)

            def networks_bias():
                pe.wait_ge(S.v, 10)
                for n in range(3 * DC):
                    last = pe.transpose(ps_l2[:, D + 2 * n:D + 2 * n + 2], mlp_v[0:NBATCH, n // DC, (n % DC) * P:(n % DC + 1) * P],
                                        ident[0:NBATCH, 0:NBATCH])
                last.then_inc(S.vT_ps, 1)
                pe.wait_ge(S.vT, 1)
                for c in range(DC):
                    for n in range(3 * DC):
                        last = pe.matmul(ps_u[:, c * NBATCH:(c + 1) * NBATCH], int_w1[:, 4 + n, c * P:(c + 1) * P],
                                         mlp_vT[:, n, :], start=(n == 0), stop=(n == 3 * DC - 1))
                last.then_inc(S.bias_ps, 1)
                pe.wait_ge(S.int_w2_in, 16)

            def block_of(b, first=False, last=False):
                layer1(b, 0, lambda: None)
                if first:
                    networks_layer2()
                lora(b, 0)
                layer1(b, 1, lambda: lora(b, 1))
                if first:
                    networks_bias()
                lora(b, 2)
                if not first:
                    transpose_u(b - 1)
                if not last:
                    transpose_T(b + 1)
                    gains_ts(b + 1)
                lora(b, 3)
                layer2(b)
                lora(b, 4)
                if not first:
                    logits(b - 1)
                if not last:
                    gains_h(b + 1)
                lora(b, 5)

            block_of(0, first=True)
            block_of(1)
            pe.wait_ge(S.xT_rest, 16)
            with pe.Fori(2, NB - 1) as b:
                block_of(b)
            block_of(NB - 1, last=True)
            transpose_u(NB - 1)
            logits(NB - 1)

            pe.wait_ge(S.const_d, 2)
            pe.wait_ge(S.const, 10)
            pe.wait_ge(S.picked, 2)
            o = ps_l1[:, 0:(TILES + 1) * E].rearrange("p (j e) -> p j e", e=E)
            for j in range(TILES):
                pe.matmul(o[:, j + 1:, :], ones16[:, :], picked[:, j:j + 1, :].to_broadcast([P, TILES - j, E]),
                          start=(j == 0), stop=False, skip_group_check=True)
            last = pe.matmul(o, before[:, :], picked, start=False, stop=True, skip_group_check=True)
            last.then_inc(S.place_ps, 1)
            pe.wait_ge(S.tile_val, 3)
            for n in range(NC_):
                pe.wait_ge(S.col_hot, n + 1)
                last = pe.matmul(ps_l2[:, 0:3 * SLOT_TILES], col_hot[:, n, :], tile_val[:, n, :, :],
                                 start=(n == 0), stop=(n == NC_ - 1))
            last.then_inc(S.slots_ps, 1)

            def rows_T(i, h, v):
                pe.wait_ge((S.rows0, S.rows1)[v], 16 * (h + 1))
                after(pe, S.rowsT, i - 1)
                for n in range(2 * DC):
                    last = pe.transpose(ps_rowsT[v][:, n * P:(n + 1) * P], rows_in[v][:, n * P:(n + 1) * P], ident16[:, :])
                last.then_inc((S.rowsT_ps0, S.rowsT_ps1)[v], 1)

            def first_layer(i, v):
                at = pe.value_load(tile_expert[0:1, ds(i, 1)], min_val=0, max_val=E - 1) * WE
                pe.wait_ge(S.rowsT, i + 1)
                for w, bank_, freed, done in ((0, ps_h1[v], S.h1, S.h1_ps), (DC * H, ps_h3[v], S.h3, S.h3_ps)):
                    after(pe, freed, i - 1)
                    passes = [(part_, c, w_) for c in range(DC) for part_, w_ in ((0, w_hi), (0, w_lo), (DC, w_hi))]
                    for n, (part_, c, w_) in enumerate(passes):
                        last = pe.matmul(bank_[:, :], rowsT[v][:, (part_ + c) * P:(part_ + c + 1) * P],
                                         w_[:, ds(at + (w + c * H), H)], start=(n == 0), stop=(n == len(passes) - 1))
                    last.then_inc(done, 1)

            def g_T(i, v):
                pe.wait_ge(S.g, i + 1)
                after(pe, S.gT_lo, i)
                for n in range(HC):
                    last = pe.transpose(ps_gT[:, n * P:(n + 1) * P], g_sb[v][:, n * P:(n + 1) * P], ident[:, :])
                last.then_inc(S.gT_ps, 1)

            def second_layer(i, v):
                at = pe.value_load(tile_expert[0:1, ds(i, 1)], min_val=0, max_val=E - 1) * WE
                pe.wait_ge(S.gT_lo, i + 1)
                after(pe, S.y, i)
                passes = [(g_, c, w_) for c in range(HC) for g_, w_ in ((gT_hi, w_hi), (gT_hi, w_lo), (gT_lo, w_hi))]
                for n, (g_, c, w_) in enumerate(passes):
                    last = pe.matmul(ps_y[:, 0:D], g_[v][:, c * P:(c + 1) * P], w_[:, ds(at + (2 * DC * H + c * D), D)],
                                     start=(n == 0), stop=(n == len(passes) - 1))
                last.then_inc(S.y_ps, 1)

            def step(i, h, v, peeled=False):
                n = SLOT_TILES
                if not peeled or i < n:
                    first_layer(i, v)
                if not peeled or i + 1 < n:
                    rows_T(i + 1, h + v, 1 - v)
                if not peeled or 1 <= i <= n:
                    g_T(i - 1, 1 - v)
                if not peeled or 2 <= i:
                    second_layer(i - 2, v)

            pe.wait_ge(S.tile_expert, 1)
            pe.wait_ge(S.w_lo, E * HALVES)
            rows_T(0, 0, 0)
            for i in range(4):
                step(i, i // 2, i % 2, peeled=True)
            turns = (SLOT_TILES - 5) // 2
            with pe.Fori(2, 2 + turns) as m:
                for v in range(2):
                    step(m * 2 + v, m, v)
            for i in range(4 + 2 * turns, SLOT_TILES + 2):
                step(i, i // 2, i % 2, peeled=True)


SEMAPHORES = """
ids_in x_first aw_in onehot_ids_in w1_in w1x_in x_rest net_in net_rows_in xT_first xT_rest int_w2_in norm_in out_in lora_scaled w1s_in w3s_in w2s_in lora_k_in
u_out biases_in added0 added1 const0 const path_now path_in x_ve h_ve c_ve v_ve x_rstd h_rstd c_rstd v_rstd
w_sum w_hi w_lo u_scaled u gather_now rows0 rows1 scatter_now y_gated slot_rows slot_gate
aw_max aw_exp shift_in gain_in lora_in lora_hi lora_lo lora_d_out mlp_h_ps mlp_h xT_ps hT_ps
prod_t prod_s prod_h xhT hhT l1_ps l2_ps zT u_hi u_lo uT_ps uT lg_ps lg bias_blk gap e2 rowsT_ps0 rowsT_ps1
rowsT h1_ps h3_ps h1 h3 silu gT_ps gT_hi gT_lo g y_ps y
x_st x_mv xhat h_scaled h_pre h_st h_mv hhat gt_ps gs_ps gh_ps c c_st c_mv chat top top_i top_e
const_d row16 onehot mixw shift_z gain_s wx shift_ps tab mlp_o_ps v v_st v_mv vT_ps vT bias_ps
chosen picked gate place_ps tiles place in_tile tile_val col_hot started tile_expert slots_ps slot_v
lora_ps passed
"""
REGION = 27808


def kernel(**inputs):
    import concourse.bacc as _bacc
    from concourse.bass_utils import run_bass_kernel_spmd as _run

    i = {k.replace("L0_cond_", "").replace("L0_ffn_", ""): np.asarray(v) for k, v in inputs.items()}
    f = np.ascontiguousarray

    def by_chunk(w):
        e, r, n = w.shape
        return f(w.reshape(e, r // P, P, n).transpose(0, 2, 1, 3).reshape(e * P, -1))

    x = f(i["x"].reshape(T, D))
    er = lambda w: w.reshape(E * R, -1)
    arrays = {
        "x": x, "xT": f(x.T),
        "path_ids": f(i["itok_BxS_0_999"].reshape(TILES, P).T),
        "onehot_ids": f(np.tile(np.repeat(np.stack([i["itok_BxS_0_4"].reshape(T), i["mask_BxS_ik0"].reshape(T)]),
                                          16, axis=0), (3, 1))),
        "path_tab": f(np.concatenate([i["pw_g"], i["pw_b"]], axis=1)),
        "aw": f(i["aw"]),
        "int_W1": f(i["int_W1"]), "int_w2g": f(np.concatenate([i["int_W2"], i["Wg"].T], axis=1)),
        "norm_rows": f(np.concatenate([i["int_b2"], i["int_g"], i["int_be"]])),
        "W1T": by_chunk(i["W1"].transpose(0, 2, 1)), "W3T": by_chunk(i["W3"].transpose(0, 2, 1)),
        "W2T": by_chunk(i["W2"].transpose(0, 2, 1)),
        "lora": f(np.concatenate([er(i["A1"]), er(i["A3"]), er(i["A2"]),
                                  er(i["B1"].transpose(0, 2, 1)), er(i["B3"].transpose(0, 2, 1)),
                                  er(i["B2"].transpose(0, 2, 1))], axis=1)),
        "biases": f(np.concatenate([i["b1"], i["b3"], i["b2"]], axis=1).reshape(-1)),
    }
    gains, shifts = np.zeros((ROWS, 4, D), np.float32), np.zeros((D, NKIND, ROWS), np.float32)
    for k, name in enumerate(("cp", "tm", "ms")):
        g, b = i[name + "_g"], i[name + "_b"]
        for r in range(16 * (k // 2), ROWS, 32):
            gains[r:r + len(g), k], shifts[:, k, r:r + len(b)] = g, b.T
    arrays["gains"], arrays["shiftZ"] = gains, shifts
    net = np.zeros((P, NET), np.float32)
    names = ("mem", "noi", "res")
    for k, (name, s) in enumerate(zip(names, ("cond_512", "cond_64", "fside_Bx32_0"))):
        w1 = i[name + "_W1"]
        net[:len(w1), NET_S + k * NBATCH:NET_S + (k + 1) * NBATCH] = i[s].T
        net[:, NET_B1 + k * DC:NET_B1 + (k + 1) * DC] = i[name + "_b1"].reshape(DC, P).T
        net[:len(w1), NET_W1 + k * D:NET_W1 + (k + 1) * D] = w1
        net[:, NET_W2 + k * DC * D:NET_W2 + (k + 1) * DC * D] = i[name + "_W2"].reshape(DC, P, D).transpose(1, 0, 2).reshape(P, -1)
    net[:, NET_INT:NET_INT + DC] = i["int_b1"].reshape(DC, P).T
    arrays["net"] = net
    arrays["net_rows"] = f(np.concatenate([i[name + part] for part in ("_b2", "_g", "_be") for name in names]))

    nc = _bacc.Bacc("TRN2", target_bir_lowering=False, num_devices=1)
    aps = {k: nc.dram_tensor(f"in_{k}", v.shape, mybir.dt.from_np(v.dtype), kind="ExternalInput").ap()
           for k, v in arrays.items()}
    out = nc.dram_tensor("out_rows", (T + PAD, D), F32, kind="ExternalOutput").ap()
    a = namedtuple("Inputs", aps)(*aps.values())
    build(nc, a, out)
    r = _run(nc, [{f"in_{k}": v for k, v in arrays.items()}], core_ids=[0])
    return r.results[0]["out_rows"][:T].reshape(inputs["x"].shape)
```

```python
from collections import namedtuple
from contextlib import ExitStack

import numpy as np

import concourse.bass as bass
from concourse import mybir

F32 = mybir.dt.float32
F16 = mybir.dt.float16
BF16 = mybir.dt.bfloat16
I32 = mybir.dt.int32
U32 = mybir.dt.uint32
ALU = mybir.AluOpType
ACT = mybir.ActivationFunctionType
AX_X = mybir.AxisListType.X

P = 128
T, D, H, E, R, K = 2048, 256, 512, 8, 16, 2
DC, HC = D // P, H // P
TILES = T // P
KB = 2
BT = KB * P
NB = T // BT
NBATCH = 2
SLOT_TILES = (T * K) // P + E - 1
PAD = P
WE = 2 * D * H // P + D * H // P
HALF = 512
HALVES = WE // HALF
LA13, LB, LA2 = slice(0, 2 * D), slice(2 * D, 2 * D + 2 * H + D), slice(2 * D + 2 * H + D, 3 * D + 3 * H)
LORA = LA2.stop
LK13 = 2 * D + 2 * H
BE = 2 * H + D
WSCALE = 64.0
EPS = 1e-5
NKIND = 3
ROWS = 96
NET_S, NET_B1 = 0, NKIND * NBATCH
NET_INT, NET_W1 = NET_B1 + 3 * DC, NET_B1 + 4 * DC
NET_W2 = NET_W1 + 3 * D
NET = NET_W2 + 3 * DC * D
ds = bass.ds


def build(nc, a, out):
    with ExitStack() as ctx:
        def sb(name, shape, dt):
            return ctx.enter_context(nc.sbuf_tensor(name, shape, dt))

        def psum(name, shape, dt=F32):
            return ctx.enter_context(nc.psum_tensor(name, shape, dt))

        S = namedtuple("Semaphores", SEMAPHORES)(*[ctx.enter_context(nc.semaphore(n)) for n in SEMAPHORES.split()])

        u_rows = nc.dram_tensor("u_rows", (T, 2 * D), F16, kind="Internal").ap()
        lora_d = nc.dram_tensor("lora_d", (E, 3, R, LORA), F16, kind="Internal").ap()

        w_hi = sb("w_hi", [P, E * WE], F16)
        w_lo = sb("w_lo", [P, E * WE], F16)
        ident = sb("ident", [P, P], F32)
        ident16 = sb("ident16", [P, P], F16)
        ones16 = sb("ones16", [P, P], F16)
        before = sb("before", [P, P], F16)
        before8 = sb("before8", [P, E, E], F32)
        iota_p = sb("iota_p", [P, P], F16)
        iota_e = sb("iota_e", [P, E], F32)
        iota_s = sb("iota_s", [P, SLOT_TILES], F16)
        token1 = sb("token1", [P, K, TILES], F16)
        pad_row = sb("pad_row", [P, 1], F32)
        top = sb("top", [P, TILES * 8], F32)
        top_e = sb("top_e", [P, TILES * 8], U32)

        region = sb("region", [P, REGION], F32)
        at = [0]

        def part(words, dt=F32):
            v = region[:, at[0]:at[0] + words]
            at[0] += words
            return v if dt == F32 else v.bitcast(dt)

        x_tok = part(TILES * D)
        xT = part(DC * T).rearrange("p (c t) -> p c t", c=DC)
        int_w1 = part(12 * D).rearrange("p (c n) -> p c n", c=12)
        wx = part(DC * D).rearrange("p (c n) -> p c n", c=DC)
        int_w2g = part(DC * (D + E)).rearrange("p (c n) -> p c n", c=DC)
        int_w2, wgT = int_w2g[:, :, 0:D], int_w2g[:, :, D:]
        onehot = part(T // 2, BF16)[0:ROWS, :]
        gain_tab = part(4 * D // 2, BF16)[0:ROWS, :].rearrange("p (k d) -> p k d", k=4)
        norm_flat = part(3 * D)
        norm_rows = norm_flat.rearrange("p (k d) -> p k d", k=3)
        bias_blk = part(NB * DC)
        xh = part(KB * D).rearrange("p (k d) -> p k d", k=KB)
        hh = part(KB * D).rearrange("p (k d) -> p k d", k=KB)
        xhT = part(DC * BT)
        hhT = part(DC * BT)
        prod_t = part(DC * BT)
        prod_s = part(DC * BT)
        prod_h = part(DC * BT)
        zT = part(DC * BT).rearrange("p (c t) -> p c t", c=DC)
        c_flat = part(KB * D)
        c_sb = c_flat.rearrange("p (k d) -> p k d", k=KB)
        u = part(KB * D).rearrange("p (k d) -> p k d", k=KB)
        u_split = part(KB * D, F16).rearrange("p (k n) -> p k n", k=KB)
        uT_sb = part(KB * D)
        pw_rows = part(KB * 2 * D).rearrange("p (k n) -> p k n", k=KB)
        w_stage = [part(2 * HALF) for _ in range(3)]
        w_full = [part(HALF) for _ in range(3)]
        lora_k = part(LORA // 2, F16)
        small = part(96)
        x_st, x_mv = small[:, 0:12], small[:, 12:16].rearrange("p (k n) -> p k n", k=KB)
        h_st, h_mv = small[:, 16:28], small[:, 28:32].rearrange("p (k n) -> p k n", k=KB)
        c_st, c_mv = small[:, 32:44], small[:, 44:48].rearrange("p (k n) -> p k n", k=KB)
        x_ve, x_rs = small[:, 48:50], small[:, 50:52]
        h_ve, h_rs = small[:, 52:54], small[:, 54:56]
        c_ve, c_rs = small[:, 56:58], small[:, 58:60]
        v_ve, v_rs = small[:, 60:63], small[:, 63:66]
        minus_half, eps_sb = small[:, 66:69], small[:, 92:95]
        aw_e, aw_m, aw_s, aw_r = small[:, 70:76], small[:, 76:77], small[:, 77:78], small[:, 78:79]
        mixw = small[:, 80:86]
        lg_sb = part(KB * E)
        top_now = part(KB * 8)
        top_e_now = part(KB * 8, U32)
        path_ids = part(TILES, I32)
        path_now = part(KB, I32)
        aw_sb = part(6)
        cond_end = at[0]

        lo5 = w_lo[:, 3 * WE + 2 * LORA:6 * WE].bitcast(F32)
        hi5 = w_hi[:, 3 * WE + 2 * LORA:6 * WE].bitcast(F32)
        ids_i = hi5[:, 0:T].bitcast(I32)
        setup_f = hi5[:, T:T + P]
        gain_f = lo5[0:ROWS, 0:4 * D].rearrange("p (k d) -> p k d", k=4)
        gain_r = lo5[0:ROWS, 4 * D:8 * D].rearrange("p (k d) -> p k d", k=4)
        gain_h = c_flat[0:ROWS, :].bitcast(BF16).rearrange("p (k d) -> p k d", k=4)
        row16, row16_f = small[:, 88:90].bitcast(I32), small[:, 90:91]
        wl = w_lo[:, (E - 2) * WE:E * WE].bitcast(F32)
        wh = w_hi[:, (E - 2) * WE:E * WE].bitcast(F32)
        net = wl[:, 0:NET]
        mlp_s = net[:, NET_S:NET_B1].rearrange("p (k b) -> p k b", k=3)
        mlp_b1 = net[:, NET_B1:NET_INT].rearrange("p (k c) -> p k c", k=3)
        int_b1 = net[:, NET_INT:NET_W1]
        mlp_w1 = net[:, NET_W1:NET_W2].rearrange("p (k n) -> p k n", k=3)
        mlp_w2 = net[:, NET_W2:].rearrange("p (k c n) -> p k c n", k=3, c=DC)
        shift_Z = wl[:, NET:NET + DC * NKIND * ROWS].rearrange("p (c k r) -> p c k r", c=DC, k=NKIND)
        net_small = wl[:, NET + DC * NKIND * ROWS:]
        mlp_h = net_small[:, 0:12].rearrange("p (k c b) -> p k c b", k=3, c=DC)
        mlp_vT = net_small[:, 12:24].rearrange("p (k b) -> p k b", b=NBATCH)
        mlp_st = net_small[:, 24:42].rearrange("p (k n) -> p k n", k=3)
        mlp_mv = net_small[:, 42:48].rearrange("p (k n) -> p k n", k=3)
        net_rows = wh[:, 0:9 * D]
        mlp_b2, mlp_g, mlp_be = (net_rows[:, n * 3 * D:(n + 1) * 3 * D].rearrange("p (k n) -> p k n", k=3)
                                 for n in range(3))
        mlp_v = wh[:, 9 * D:12 * D].rearrange("p (k n) -> p k n", k=3)
        lora_f = w_lo[:, 3 * WE:3 * WE + 2 * LORA].bitcast(F32)
        lora_h = w_hi[:, 3 * WE:3 * WE + LORA]
        lora_l = w_hi[:, 3 * WE + LORA:3 * WE + 2 * LORA]

        at[0] = 0
        biases = part(E * BE)
        rows_in = [part(D, F16) for _ in range(2)]
        rowsT = [part(D, F16) for _ in range(2)]
        h1_sb = [part(H) for _ in range(2)]
        h3_sb = [part(H) for _ in range(2)]
        silu_sb = [part(H) for _ in range(2)]
        g_sb = [part(H) for _ in range(2)]
        gT_hi = [part(H // 2, F16) for _ in range(2)]
        gT_lo = [part(H // 2, F16) for _ in range(2)]
        y_sb = [part(D) for _ in range(2)]
        y_gated = [part(D) for _ in range(2)]
        gather_now = [part(1, I32) for _ in range(2)]
        scatter_now = [part(1, I32) for _ in range(2)]
        slot_rows = part(SLOT_TILES * 2, I32).rearrange("p (i n) -> p i n", n=2)
        slot_gate = part(SLOT_TILES)
        tile_expert = part(SLOT_TILES, I32)
        NC_ = K * TILES
        chosen = part(NC_ * E).rearrange("p (k j e) -> p k j e", k=K, e=E)
        picked = part((TILES + 1) * E // 2, F16).rearrange("p (j e) -> p j e", e=E)
        place = part(TILES * E).rearrange("p (j e) -> p j e", e=E)
        place2 = part(NC_ * E).rearrange("p (k j e) -> p k j e", k=K, e=E)
        slot_f = part(NC_)
        slot_i = part(NC_, I32)
        slot_tile = part(NC_, I32)
        slot_col = part(NC_, I32)
        slot_tile_f = part(NC_ // 2, F16)
        slot_col_f = part(NC_)
        tiles_i = part(E, I32)
        tiles_f = part(E)
        tri_f = part(E * E).rearrange("p (a b) -> p a b", a=E)
        first_tile = part(E)
        started = part(SLOT_TILES * E).rearrange("p (i e) -> p i e", e=E)
        started_n = part(SLOT_TILES)
        gap = part(TILES)
        e2 = part(TILES)
        den = part(TILES)
        gate = part(K * TILES).rearrange("p (k j) -> p k j", k=K)
        gate_f = part(K * TILES // 2, F16).rearrange("p (k j) -> p k j", k=K)
        gate_h = part(K * TILES // 2, F16).rearrange("p (k j) -> p k j", k=K)
        in_tile = part(NC_ * SLOT_TILES // 2, F16).rearrange("p (n s) -> p n s", n=NC_)
        col_hot = part(NC_ * P // 2, F16).rearrange("p (n c) -> p n c", n=NC_)
        tile_val = part(NC_ * 3 * SLOT_TILES // 2, F16).rearrange("p (n v s) -> p n v s", n=NC_, v=3)
        slot_v = part(3 * SLOT_TILES).rearrange("p (v s) -> p v s", v=3)
        empty = part(SLOT_TILES)
        main_end = at[0]
        assert max(cond_end, main_end) <= REGION, (cond_end, main_end)

        bank = [psum(f"bank{i}", [P, 512]) for i in range(8)]
        ps_xT, ps_hT, ps_g0, ps_g1, ps_l1, ps_l2, ps_u, ps_lora = bank
        ps_h1, ps_h3 = bank[0:2], bank[2:4]
        ps_rowsT = [bank[4][:, 0:256].bitcast(F16), bank[5][:, 0:256].bitcast(F16)]
        ps_gT, ps_y = bank[6], bank[7]

        block = ctx.enter_context(nc.Block())

        def after(engine, semaphore, count):
            if not isinstance(count, int) or count > 0:
                engine.wait_ge(semaphore, count)

        def before_plain(engine, semaphore, count):
            engine.wait_ge(semaphore, count)
            if not isinstance(count, int):
                engine.sem_inc(S.passed, 1)

        def experts_of(engine, i, steps):
            first, end = i - 2, i + steps
            if isinstance(i, int):
                first, end = max(first, 0), min(end, SLOT_TILES)
            _, e = nc.values_load_multi_w_load_instructions(
                tile_expert[0:1, ds(first, steps + 2 if not isinstance(i, int) else end - first)], engines=(engine,),
                min_val=0, max_val=E - 1, skip_runtime_bounds_check_because=
                "1 to E experts have started at any tile, and the value is their count less one")
            missing = max(2 - i, 0) if isinstance(i, int) else 0
            return [None] * missing + list(e) + [None] * steps

        @block.sync
        def _(sp):
            x_v = a.x.rearrange("(j p) d -> p j d", p=P)
            xt_v = x_tok.rearrange("p (j d) -> p j d", d=D)
            sp.dma_start(path_ids, a.path_ids).then_inc(S.ids_in, 16)
            sp.dma_start(xt_v[:, 0:2 * KB, :], x_v[:, 0:2 * KB, :]).then_inc(S.x_first, 16)
            sp.dma_start(ids_i[0:ROWS, :], a.onehot_ids).then_inc(S.onehot_ids_in, 16)
            w1_v = a.int_W1.rearrange("(c p) n -> p c n", p=P)
            sp.dma_start(int_w1[:, 0:4, :], w1_v[:, 0:4, :]).then_inc(S.w1_in, 16)
            sp.dma_start(int_w1[:, 10:12, :], w1_v[:, 10:12, :]).then_inc(S.w1_in, 16)
            sp.dma_start(int_w1[:, 4:10, :], w1_v[:, 4:10, :]).then_inc(S.w1x_in, 16)
            sp.dma_start(xt_v[:, 2 * KB:3 * KB, :], x_v[:, 2 * KB:3 * KB, :]).then_inc(S.x_third, 16)
            sp.dma_start(net, a.net).then_inc(S.net_in, 16)
            sp.dma_start(net_rows[0:NBATCH, :], a.net_rows.partition_broadcast(NBATCH)).then_inc(S.net_rows_in, 16)
            xT_v = a.xT.rearrange("(c p) t -> p c t", p=P)
            sp.dma_start(xT[:, :, 0:2 * BT], xT_v[:, :, 0:2 * BT]).then_inc(S.xT_first, 16)

            def load_weights(e, parts):
                for p in parts:
                    w = (a.W1T, a.W3T, a.W2T)[p]
                    after(sp, S.w_sum, (e - 1) * HALVES + 2 * p + 2)
                    sp.dma_start(w_stage[p], w[ds(e * P, P), :]).then_inc((S.w1s_in, S.w3s_in, S.w2s_in)[p], 16)

            def load_lora(e, columns, used):
                sp.wait_ge(S.lora_ps, (e - 1) * HALVES + used)
                sp.dma_start(lora_k[0:3 * R, columns], lora_rows[ds(e * 3 * R, 3 * R), columns]
                             ).then_inc(S.lora_k13_in if used == 4 else S.lora_k2_in, 16)

            def store_rows(b):
                after(sp, S.u_lo, b + 1)
                sp.dma_start(u_rows[ds(b * BT, BT), :].rearrange("(k p) n -> p k n", p=P),
                             u_split).then_inc(S.u_out, 16)

            def load_expert(e, rows):
                load_weights(e, (0,))
                load_lora(e, slice(0, LK13), 4)
                load_weights(e, (1,))
                if rows:
                    store_rows(e - 2)
                load_lora(e, slice(LK13, LORA), 6)
                load_weights(e, (2,))

            load_weights(0, (0,))
            lora_rows = lora_d.rearrange("e q r n -> (e q r) n")
            sp.wait_ge(S.lora_hi, 2)
            high = ((0, slice(0, LORA)), (1, LA13), (1, LA2), (2, LB))
            low = ((1, LB), (2, LA13), (2, LA2))
            for q, columns in high:
                sp.dma_start(lora_k[q * R:(q + 1) * R, columns], lora_h[0:R, columns]).then_inc(S.lora_k0_in, 16)
            load_weights(0, (1,))
            sp.wait_ge(S.lora_lo, 2)
            for q, columns in low:
                sp.dma_start(lora_k[q * R:(q + 1) * R, columns], lora_l[0:R, columns]).then_inc(S.lora_k0_in, 16)
            load_weights(0, (2,))
            sp.dma_start(int_w2g, a.int_w2g.rearrange("(c p) n -> p c n", p=P)).then_inc(S.int_w2_in, 16)
            sp.dma_start(norm_flat, a.norm_rows.partition_broadcast(P)).then_inc(S.norm_in, 16)
            for src, parts in ((lora_h, high), (lora_l, low)):
                for q, columns in parts:
                    sp.dma_start(lora_d[:, q, :, columns], src[:, columns]).then_inc(S.lora_d_out, 16)
            sp.dma_start(xt_v[:, 3 * KB:, :], x_v[:, 3 * KB:, :]).then_inc(S.x_rest, 16)
            sp.dma_start(xT[:, :, 2 * BT:], xT_v[:, :, 2 * BT:]).then_inc(S.xT_rest, 16)
            sp.wait_ge(S.lora_d_out, 16 * 7)
            load_expert(1, rows=False)
            sp.dma_start(out[0:T, :], a.x).then_inc(S.out_in, 16)
            sp.dma_start(out[T:T + PAD, :], a.x[0:PAD, :]).then_inc(S.out_in, 16)
            with sp.Fori(2, E) as e:
                load_expert(e, rows=True)
            store_rows(NB - 2)
            store_rows(NB - 1)
            sp.wait_ge(S.lg, NB)
            sp.wait_ge(S.u_lo, NB)
            sp.wait_ge(S.w_lo, E * HALVES)
            sp.wait_ge(S.u_out, 16 * NB)
            sp.dma_start(biases, a.biases.partition_broadcast(P)).then_inc(S.biases_in, 16)
            sp.wait_ge(S.added0, 16 * ((SLOT_TILES + 1) // 2))
            sp.wait_ge(S.added1, 16 * (SLOT_TILES // 2))

        @block.gpsimd
        def _(pool):
            eq, gt = ALU.not_equal, ALU.is_gt
            pool.memset(ident[:, :], 0.0).then_inc(S.const0, 1)
            pool.memset(setup_f, 1.0).then_inc(S.const0, 1)
            pool.memset(before8[:, :, :], 1.0).then_inc(S.const0, 1)
            pool.memset(minus_half, -0.5).then_inc(S.const0, 1)
            pool.memset(eps_sb, EPS).then_inc(S.const0, 1)
            pool.wait_ge(S.const0, 5)
            pool.affine_select(out=ident[:, :], in_=ident[:, :], compare_op=eq, fill=1.0, base=0,
                               pattern=[[-1, P]], channel_multiplier=1).then_inc(S.const, 1)
            pool.affine_select(out=setup_f, in_=setup_f, compare_op=gt, fill=0.0, base=0,
                               pattern=[[1, P]], channel_multiplier=-1).then_inc(S.const, 1)
            pool.affine_select(out=before8[:, :, :], in_=before8[:, :, :], compare_op=gt, fill=0.0, base=0,
                               pattern=[[1, E], [-1, E]], channel_multiplier=0).then_inc(S.const, 1)
            pool.iota(row16[:, 0:1], [[0, 1]], base=0, channel_multiplier=1).then_inc(S.const, 1)

            def gather_path(b):
                if not isinstance(b, int) or b:
                    pool.wait_ge(S.h_pre, b)
                n = b + 1
                pool.tensor_copy(path_now, path_ids[:, ds(b * KB, KB)]).then_inc(S.path_now, 1)
                before_plain(pool, S.path_now, n)
                for k in range(KB):
                    pool.indirect_dma_start(pw_rows[:, k, :], None, a.path_tab,
                                            bass.IndirectOffsetOnAxis(ap=path_now[:, k:k + 1], axis=0)
                                            ).then_inc(S.path_in, 16)

            def rstd(mv, ve, rs, mv_ready, n, shifted, done, count):
                pool.wait_ge(mv_ready, n)
                pool.tensor_tensor(ve, mv, eps_sb[0:rs.shape[0], 0:rs.shape[1]], ALU.add).then_inc(shifted, 1)
                pool.wait_ge(shifted, count)
                pool.tensor_tensor(rs, ve, minus_half[0:rs.shape[0], 0:rs.shape[1]], ALU.pow).then_inc(done, 1)

            def rstd_x(b):
                rstd(x_mv[:, :, 1], x_ve, x_rs, S.x_mv, (b + 1) * KB, S.x_ve, S.x_rstd, b + 1)

            def rstd_h(b):
                rstd(h_mv[:, :, 1], h_ve, h_rs, S.h_mv, (b + 1) * KB, S.h_ve, S.h_rstd, b + 1)

            def rstd_c(b):
                rstd(c_mv[:, :, 1], c_ve, c_rs, S.c_mv, (b + 1) * KB, S.c_ve, S.c_rstd, b + 1)

            def low_part(e, h):
                n = e * HALVES + h
                pool.wait_ge(S.w_hi, n + 1)
                pool.tensor_tensor(w_lo[:, ds(e * WE + h * HALF, HALF)], w_full[h % 3],
                                   w_hi[:, ds(e * WE + h * HALF, HALF)], ALU.subtract).then_inc(S.w_lo, 1)

            pool.wait_ge(S.ids_in, 16)
            gather_path(0)
            pool.iota(iota_p[:, :], [[1, P]], base=0, channel_multiplier=0,
                      allow_small_or_imprecise_dtypes=True).then_inc(S.const, 1)
            pool.iota(iota_e[:, :], [[1, E]], base=0, channel_multiplier=0,
                      allow_small_or_imprecise_dtypes=True).then_inc(S.const, 1)
            pool.iota(iota_s[:, :], [[1, SLOT_TILES]], base=0, channel_multiplier=0,
                      allow_small_or_imprecise_dtypes=True).then_inc(S.const, 1)
            pool.iota(token1[:, :, :], [[0, K], [P, TILES]], base=1, channel_multiplier=1,
                      allow_small_or_imprecise_dtypes=True).then_inc(S.const, 1)
            pool.iota(pad_row[:, :], [[0, 1]], base=T + 1, channel_multiplier=1,
                      allow_small_or_imprecise_dtypes=True).then_inc(S.const, 1)
            pool.memset(ones16[:, :], 1.0).then_inc(S.const, 1)
            rstd_x(0)
            rstd_h(0)
            gather_path(1)
            rstd_x(1)
            pool.wait_ge(S.mixw, 2)
            pool.wait_ge(S.net_rows_in, 16)
            mix3 = mixw[0:NBATCH, 2:5].unsqueeze(2).to_broadcast([NBATCH, 3, D])
            for rows in (mlp_g, mlp_be):
                pool.tensor_tensor(rows[0:NBATCH, :, :], rows[0:NBATCH, :, :], mix3, ALU.mult).then_inc(S.net_mixed, 1)
            pool.wait_ge(S.lora_hi, 2)
            for half in (slice(0, LORA // 2), slice(LORA // 2, LORA)):
                pool.tensor_tensor(lora_l[:, half], lora_f[:, half], lora_h[:, half], ALU.subtract).then_inc(S.lora_lo, 1)
            rstd_h(1)
            rstd(mlp_mv[0:NBATCH, :, 1], v_ve[0:NBATCH, :], v_rs[0:NBATCH, :], S.v_mv, 3, S.v_ve, S.v_rstd, 1)
            gather_path(2)

            def block_of(b, first=False, norms=True, paths=True):
                if not first:
                    rstd_c(b - 1)
                if norms:
                    rstd_x(b + 2)
                low_part(b, 0)
                low_part(b, 1)
                if norms:
                    rstd_h(b + 2)
                low_part(b, 2)
                low_part(b, 3)
                if paths:
                    gather_path(b + 3)
                low_part(b, 4)
                low_part(b, 5)

            block_of(0, first=True)
            block_of(1)
            with pool.Fori(2, NB - 3) as b:
                block_of(b)
            block_of(NB - 3, paths=False)
            block_of(NB - 2, norms=False, paths=False)
            block_of(NB - 1, norms=False, paths=False)
            rstd_c(NB - 1)

            pool.wait_ge(S.in_tile, 1)
            pool.wait_ge(S.gate, 5)
            for n, val in ((1, gate_h), (2, gate_f)):
                pool.tensor_tensor(tile_val[:, :, n, :], in_tile,
                                   val.rearrange("p k j -> p (k j)").unsqueeze(2).to_broadcast([P, NC_, SLOT_TILES]),
                                   ALU.mult).then_inc(S.gate_val, 1)

            def gather_rows(i, h, v):
                after(pool, (S.rowsT_ps0, S.rowsT_ps1)[v], h)
                n = i + 1
                pool.tensor_copy(gather_now[v], slot_rows[:, ds(i, 1), 0]).then_inc(S.gather_now, 1)
                before_plain(pool, S.gather_now, n)
                pool.indirect_dma_start(rows_in[v], None, u_rows,
                                        bass.IndirectOffsetOnAxis(ap=gather_now[v], axis=0)
                                        ).then_inc((S.rows0, S.rows1)[v], 16)

            def add_rows(i, h, v):
                after(pool, (S.added1, S.added0)[v], 16 * (h + v))
                n = i + 1
                pool.tensor_copy(scatter_now[v], slot_rows[:, ds(i, 1), 1]).then_inc(S.scatter_now, 1)
                pool.wait_ge(S.scatter_now, n)
                before_plain(pool, S.y_gated, n)
                pool.indirect_dma_start(out, bass.IndirectOffsetOnAxis(ap=scatter_now[v], axis=0),
                                        y_gated[v], None, compute_op=ALU.add
                                        ).then_inc((S.added0, S.added1)[v], 16)

            pool.wait_ge(S.u_out, 16 * NB)
            pool.wait_ge(S.slot_rows, 2)
            pool.wait_ge(S.out_in, 32)
            ahead = 5
            for i in range(ahead):
                gather_rows(i, i // 2, i % 2)
            for i in range(2):
                gather_rows(i + ahead, (i + ahead) // 2, (i + ahead) % 2)
                add_rows(i, 0, i)
            turns = (SLOT_TILES - ahead) // 2
            with pool.Fori(1, turns) as m:
                for v in range(2):
                    gather_rows(m * 2 + v + ahead, m + (v + ahead) // 2, 1 - v)
                    add_rows(m * 2 + v, m, v)
            for i in range(2 * turns, SLOT_TILES):
                if i + ahead < SLOT_TILES:
                    gather_rows(i + ahead, (i + ahead) // 2, (i + ahead) % 2)
                add_rows(i, i // 2, i % 2)

        @block.scalar
        def _(act):
            act.dma_start(aw_sb, a.aw.partition_broadcast(P)).then_inc(S.aw_in, 16)
            act.dma_start(gain_f, a.gains).then_inc(S.gain_in, 16)
            act.dma_start(shift_Z, a.shiftZ.rearrange("(c p) k r -> p c k r", p=P)).then_inc(S.shift_in, 16)
            act.dma_start(lora_f, a.lora).then_inc(S.lora_in, 16)
            act.wait_ge(S.aw_max, 1)
            act.activation(aw_e, aw_sb, ACT.Exp, bias=aw_m, accum_out=aw_s).then_inc(S.aw_exp, 1)
            act.wait_ge(S.lora_in, 16)
            for n, columns in enumerate((LA13, LA2)):
                act.activation(lora_f[:, columns], lora_f[:, columns], ACT.Copy, scale=WSCALE).then_inc(S.lora_scaled, 1)
            act.wait_ge(S.lora_scaled, 2)
            for half in (slice(0, LORA // 2), slice(LORA // 2, LORA)):
                act.copy(lora_h[:, half], lora_f[:, half]).then_inc(S.lora_hi, 1)
            act.wait_ge(S.mlp_h_ps, 1)
            for k in range(3):
                for c in range(DC):
                    act.activation(mlp_h[:, k, c, :], ps_lora[:, (k * DC + c) * 2:(k * DC + c) * 2 + 2], ACT.Silu,
                                   bias=mlp_b1[:, k, c:c + 1]).then_inc(S.mlp_h, 1)

            def high_part(e, h):
                n = e * HALVES + h
                act.wait_ge(S.w_sum, n + 1)
                act.copy(w_hi[:, ds(e * WE + h * HALF, HALF)], w_full[h % 3]).then_inc(S.w_hi, 1)

            def copy_T(b):
                act.wait_ge(S.xT_ps, b + 1)
                after(act, S.prod_s, b)
                act.copy(xhT, ps_xT[:, :]).then_inc(S.xhT, 1)
                act.wait_ge(S.hT_ps, b + 1)
                after(act, S.prod_h, b)
                act.copy(hhT, ps_hT[:, :]).then_inc(S.hhT, 1)

            def hidden(b):
                act.wait_ge(S.l1_ps, b + 1)
                after(act, S.l2_ps, b)
                for c in range(DC):
                    act.activation(zT[:, c, :], ps_l1[:, c * BT:(c + 1) * BT], ACT.Silu,
                                   bias=bias_blk[:, ds(b * DC + c, 1)]).then_inc(S.zT, 1)

            def u_high(b):
                act.wait_ge(S.u, (b + 1) * KB)
                after(act, S.u_out, 16 * b)
                act.copy(u_split[:, :, 0:D], u).then_inc(S.u_hi, 1)

            def copy_uT(b):
                act.wait_ge(S.uT_ps, b + 1)
                after(act, S.lg_ps, b)
                act.copy(uT_sb, ps_u[:, :]).then_inc(S.uT, 1)

            copy_T(0)

            def block_of(b, first=False, last=False):
                high_part(b, 0)
                if not last:
                    copy_T(b + 1)
                high_part(b, 1)
                if not first:
                    u_high(b - 1)
                if first:
                    act.wait_ge(S.bias_blk, DC * NBATCH)
                hidden(b)
                high_part(b, 2)
                if not first:
                    copy_uT(b - 1)
                for h in range(3, HALVES):
                    high_part(b, h)

            block_of(0, first=True)
            block_of(1)
            with act.Fori(2, NB - 1) as b:
                block_of(b)
            block_of(NB - 1, last=True)
            u_high(NB - 1)
            copy_uT(NB - 1)

            act.wait_ge(S.gap, 1)
            act.activation(e2, gap, ACT.Exp).then_inc(S.e2, 1)

            def copy_rowsT(i, v):
                act.wait_ge((S.rowsT_ps0, S.rowsT_ps1)[v], i[1] + 1)
                after(act, S.h3_ps, i[0] - 1)
                act.copy(rowsT[v], ps_rowsT[v]).then_inc(S.rowsT, 1)

            def silu_of(i, v):
                act.wait_ge(S.h1, i[0] + 1)
                act.activation(silu_sb[v], h1_sb[v], ACT.Silu).then_inc(S.silu, 1)

            def gT_high(i, v):
                act.wait_ge(S.gT_ps, i[0] + 1)
                after(act, S.y_ps, i[0] - 1)
                act.copy(gT_hi[v], ps_gT[:, :]).then_inc(S.gT_hi, 1)

            def gated(i, v):
                act.wait_ge(S.y, i[0] + 1)
                after(act, (S.added0, S.added1)[v], 16 * i[1])
                act.activation(y_gated[v], y_sb[v], ACT.Copy, scale=slot_gate[:, ds(i[0], 1)]).then_inc(S.y_gated, 1)

            def step(i, h, v, peeled=False):
                n = SLOT_TILES
                if not peeled or i < n:
                    silu_of((i, h), v)
                if not peeled or i + 1 < n:
                    copy_rowsT((i + 1, h + v), 1 - v)
                if not peeled or 1 <= i <= n:
                    gT_high((i - 1, h - 1 + v), 1 - v)
                if not peeled or 2 <= i:
                    gated((i - 2, h - 1), v)

            act.wait_ge(S.slot_gate, 1)
            copy_rowsT((0, 0), 0)
            for i in range(4):
                step(i, i // 2, i % 2, peeled=True)
            turns = (SLOT_TILES - 5) // 2
            with act.Fori(2, 2 + turns) as m:
                for v in range(2):
                    step(m * 2 + v, m, v)
            for i in range(4 + 2 * turns, SLOT_TILES + 2):
                step(i, i // 2, i % 2, peeled=True)

        @block.vector
        def _(dve):
            mul, add, sub = ALU.mult, ALU.add, ALU.subtract

            def norm_x(b):
                n = (b + 1) * KB
                for k in range(KB):
                    dve.bn_stats(x_st[:, 6 * k:6 * k + 6], x_tok[:, ds((b * KB + k) * D, D)]).then_inc(S.x_st, 1)
                before_plain(dve, S.x_st, n)
                for k in range(KB):
                    dve.bn_aggr(x_mv[:, k, :], x_st[:, 6 * k:6 * k + 6]).then_inc(S.x_mv, 1)

            def norm_h(b):
                n = (b + 1) * KB
                dve.wait_ge(S.x_rstd, b + 1)
                after(dve, S.xT_ps, b)
                for k in range(KB):
                    dve.tensor_scalar(xh[:, k, :], x_tok[:, ds((b * KB + k) * D, D)], x_mv[:, k, 0:1],
                                      x_rs[:, k:k + 1], sub, mul).then_inc(S.xhat, 1)
                dve.wait_ge(S.xhat, (b + 1) * KB)
                dve.wait_ge(S.path_in, (b + 1) * KB * 16)
                after(dve, S.hT_ps, b)
                dve.tensor_tensor(hh, xh, pw_rows[:, :, 0:D], mul).then_inc(S.h_scaled, 1)
                dve.wait_ge(S.h_scaled, b + 1)
                dve.tensor_tensor(hh, hh, pw_rows[:, :, D:], add).then_inc(S.h_pre, 1)
                dve.wait_ge(S.h_pre, b + 1)
                for k in range(KB):
                    dve.bn_stats(h_st[:, 6 * k:6 * k + 6], hh[:, k, :]).then_inc(S.h_st, 1)
                before_plain(dve, S.h_st, n)
                for k in range(KB):
                    dve.bn_aggr(h_mv[:, k, :], h_st[:, 6 * k:6 * k + 6]).then_inc(S.h_mv, 1)

            def finish_h(b):
                dve.wait_ge(S.h_rstd, b + 1)
                for k in range(KB):
                    dve.tensor_scalar(hh[:, k, :], hh[:, k, :], h_mv[:, k, 0:1], h_rs[:, k:k + 1],
                                      sub, mul).then_inc(S.hhat, 1)

            def products_x(b):
                dve.wait_ge(S.xhT, b + 1)
                dve.wait_ge(S.gt_ps, b + 1)
                after(dve, S.l1_ps, b)
                dve.tensor_tensor(prod_t, xhT, ps_g0[:, :], mul).then_inc(S.prod_t, 1)
                dve.wait_ge(S.gs_ps, b + 1)
                dve.tensor_tensor(prod_s, xhT, ps_g1[:, :], mul).then_inc(S.prod_s, 1)

            def products_h(b):
                dve.wait_ge(S.hhT, b + 1)
                dve.wait_ge(S.gh_ps, b + 1)
                dve.tensor_tensor(prod_h, hhT, ps_g0[:, :], mul).then_inc(S.prod_h, 1)

            def second_layer(b):
                n = (b + 1) * KB
                dve.wait_ge(S.l2_ps, b + 1)
                dve.tensor_tensor(c_sb, ps_l2[:, :].rearrange("p (k d) -> p k d", k=KB),
                                  norm_rows[:, 0:1, :].to_broadcast([P, KB, D]), add).then_inc(S.c, 1)
                dve.wait_ge(S.c, b + 1)
                for k in range(KB):
                    dve.bn_stats(c_st[:, 6 * k:6 * k + 6], c_sb[:, k, :]).then_inc(S.c_st, 1)
                before_plain(dve, S.c_st, n)
                for k in range(KB):
                    dve.bn_aggr(c_mv[:, k, :], c_st[:, 6 * k:6 * k + 6]).then_inc(S.c_mv, 1)

            def norm_c(b):
                dve.wait_ge(S.c_mv, (b + 1) * KB)
                after(dve, S.uT_ps, b)
                for k in range(KB):
                    dve.scalar_tensor_tensor(c_sb[:, k, :], c_sb[:, k, :], c_mv[:, k, 0:1], norm_rows[:, 1, :],
                                             sub, mul).then_inc(S.chat, 1)
                dve.wait_ge(S.chat, (b + 1) * KB)
                dve.wait_ge(S.c_rstd, b + 1)
                for k in range(KB):
                    dve.scalar_tensor_tensor(u[:, k, :], c_sb[:, k, :], c_rs[:, k:k + 1], norm_rows[:, 2, :],
                                             mul, add).then_inc(S.u, 1)

            def u_low(b):
                dve.wait_ge(S.u_hi, b + 1)
                dve.tensor_tensor(u_split[:, :, D:], u, u_split[:, :, 0:D], sub).then_inc(S.u_lo, 1)

            def top_two(b):
                n = (b + 1) * KB
                dve.wait_ge(S.lg_ps, b + 1)
                after(dve, S.top_e, b * 2)
                dve.tensor_copy(lg_sb, ps_u[:, 0:KB * E]).then_inc(S.lg, 1)
                before_plain(dve, S.lg, b + 1)
                for k in range(KB):
                    dve.max(top_now[:, k * 8:(k + 1) * 8], lg_sb[:, k * E:(k + 1) * E]).then_inc(S.top, 1)
                before_plain(dve, S.top, n)
                for k in range(KB):
                    dve.max_index(top_e_now[:, k * 8:(k + 1) * 8], top_now[:, k * 8:(k + 1) * 8],
                                  lg_sb[:, k * E:(k + 1) * E]).then_inc(S.top_i, 1)
                dve.wait_ge(S.top_i, (b + 1) * KB)
                dve.tensor_copy(top[:, ds(b * KB * 8, KB * 8)], top_now).then_inc(S.top_e, 1)
                dve.tensor_copy(top_e[:, ds(b * KB * 8, KB * 8)], top_e_now).then_inc(S.top_e, 1)

            def merge(e, h):
                n = e * HALVES + h
                dve.wait_ge(S.lora_ps, n + 1)
                dve.wait_ge((S.w1s_in, S.w3s_in, S.w2s_in)[h // 2], (e + 1) * 16)
                after(dve, S.w_lo, n - 2)
                dve.scalar_tensor_tensor(w_full[h % 3], w_stage[h // 2][:, (h % 2) * HALF:(h % 2 + 1) * HALF],
                                         WSCALE, ps_lora[:, :], mul, add).then_inc(S.w_sum, 1)

            def split_table(kinds, n):
                dve.wait_ge(S.gain_s, 3 + n)
                dve.tensor_copy(gain_tab[:, kinds, :], gain_f[:, kinds, :]).then_inc(S.tab, 1)
                dve.wait_ge(S.tab, 5 * n + 1)
                dve.tensor_tensor(gain_r[:, kinds, :], gain_f[:, kinds, :], gain_tab[:, kinds, :], sub).then_inc(S.tab, 1)
                dve.wait_ge(S.tab, 5 * n + 2)
                dve.tensor_copy(gain_tab[32:64, kinds, :], gain_r[32:64, kinds, :]).then_inc(S.tab, 1)
                dve.tensor_copy(gain_h[:, kinds, :], gain_r[:, kinds, :]).then_inc(S.tab, 1)
                dve.wait_ge(S.tab, 5 * n + 4)
                dve.tensor_tensor(gain_tab[64:96, kinds, :], gain_r[64:96, kinds, :], gain_h[64:96, kinds, :], sub).then_inc(S.tab, 1)

            v = mlp_v[0:NBATCH, :, :]

            def networks_add():
                dve.wait_ge(S.mlp_o_ps, 1)
                dve.wait_ge(S.net_rows_in, 16)
                dve.tensor_tensor(v[:, 0:2, :], ps_u[0:NBATCH, :].rearrange("p (k n) -> p k n", k=2),
                                  mlp_b2[0:NBATCH, 0:2, :], add).then_inc(S.v, 1)
                dve.tensor_tensor(v[:, 2, :], ps_l2[0:NBATCH, 0:D], mlp_b2[0:NBATCH, 2, :], add).then_inc(S.v, 1)
                dve.wait_ge(S.v, 2)
                for k in range(3):
                    dve.bn_stats(mlp_st[0:NBATCH, k, :], v[:, k, :]).then_inc(S.v_st, 1)
                dve.wait_ge(S.v_st, 3)
                for k in range(3):
                    dve.bn_aggr(mlp_mv[0:NBATCH, k, :], mlp_st[0:NBATCH, k, :]).then_inc(S.v_mv, 1)

            def networks_norm():
                dve.wait_ge(S.v_mv, 3)
                dve.wait_ge(S.net_mixed, 2)
                for k in range(3):
                    dve.scalar_tensor_tensor(v[:, k, :], v[:, k, :], mlp_mv[0:NBATCH, k, 0:1], mlp_g[0:NBATCH, k, :],
                                             sub, mul).then_inc(S.v, 1)
                dve.wait_ge(S.v, 5)
                dve.wait_ge(S.v_rstd, 1)
                for k in range(3):
                    dve.scalar_tensor_tensor(v[:, k, :], v[:, k, :], v_rs[0:NBATCH, k:k + 1], mlp_be[0:NBATCH, k, :],
                                             mul, add).then_inc(S.v, 1)

            def networks_out():
                dve.wait_ge(S.vT_ps, 1)
                dve.tensor_copy(mlp_vT, ps_l2[:, D:D + 12].rearrange("p (k b) -> p k b", b=NBATCH)).then_inc(S.vT, 1)
                dve.wait_ge(S.bias_ps, 1)
                for bat in range(NBATCH):
                    for c in range(DC):
                        n = NB // NBATCH
                        dst = bias_blk.rearrange("p (b c) -> p b c", c=DC)[:, bat * n:(bat + 1) * n, c]
                        src = ps_u[:, c * NBATCH + bat:c * NBATCH + bat + 1].to_broadcast([P, n])
                        dve.tensor_scalar(dst, src, int_b1[:, c:c + 1], None, add).then_inc(S.bias_blk, 1)

            dve.wait_ge(S.aw_in, 16)
            dve.tensor_reduce(aw_m, aw_sb, AX_X, ALU.max, negate=True).then_inc(S.aw_max, 1)
            dve.wait_ge(S.x_first, 16)
            norm_x(0)
            dve.wait_ge(S.const, 4)
            dve.tensor_copy(ident16[:, :], ident[:, :]).then_inc(S.const_d, 1)
            dve.tensor_copy(before[:, :], setup_f).then_inc(S.const_d, 1)
            dve.tensor_scalar(row16[:, 1:2], row16[:, 0:1], 15, None, ALU.bitwise_and).then_inc(S.row16, 1)
            dve.wait_ge(S.row16, 1)
            dve.tensor_copy(row16_f, row16[:, 1:2]).then_inc(S.row16, 1)
            dve.wait_ge(S.aw_exp, 1)
            dve.reciprocal(aw_r, aw_s).then_inc(S.mixw, 1)
            dve.wait_ge(S.mixw, 1)
            dve.tensor_scalar(mixw, aw_e, aw_r, None, mul).then_inc(S.mixw, 1)
            dve.wait_ge(S.mixw, 2)
            dve.wait_ge(S.gain_in, 16)
            for k, w in enumerate((0, 1, 5)):
                dve.tensor_scalar(gain_f[:, k, :], gain_f[:, k, :], mixw[0:ROWS, w:w + 1], None, mul).then_inc(S.gain_s, 1)
            dve.wait_ge(S.shift_in, 16)
            for k, w in enumerate((0, 1, 5)):
                dve.tensor_scalar(shift_Z[:, :, k, :], shift_Z[:, :, k, :], mixw[:, w:w + 1], None, mul).then_inc(S.shift_z, 1)
            dve.wait_ge(S.onehot_ids_in, 16)
            dve.wait_ge(S.row16, 2)
            dve.tensor_scalar(onehot, ids_i[0:ROWS, :], row16_f[0:ROWS, :], None, ALU.is_equal).then_inc(S.onehot, 1)
            split_table(slice(0, NKIND), 0)
            norm_h(0)
            norm_x(1)
            finish_h(0)
            dve.wait_ge(S.shift_ps, 1)
            dve.tensor_copy(gain_f[:, 3, :], ps_hT[0:ROWS, 0:D]).then_inc(S.gain_s, 1)
            split_table(slice(NKIND, NKIND + 1), 1)
            dve.wait_ge(S.w1x_in, 16)
            dve.tensor_scalar(wx, int_w1[:, 4:6, :], mixw[:, 2:3], None, mul).then_inc(S.wx, 1)
            for n in (3, 4):
                dve.wait_ge(S.wx, n - 2)
                dve.scalar_tensor_tensor(wx, int_w1[:, 2 * n:2 * n + 2, :], mixw[:, n:n + 1], wx, mul, add).then_inc(S.wx, 1)
            products_x(0)
            products_h(0)
            norm_h(1)
            networks_add()
            finish_h(1)

            def block_of(b, first=False, norms=True, last=False):
                if first:
                    merge(b, 0)
                    dve.wait_ge(S.x_third, 16)
                    norm_x(b + 2)
                    networks_norm()
                    merge(b, 1)
                    networks_out()
                    merge(b, 2)
                    products_x(b + 1)
                    merge(b, 3)
                    products_h(b + 1)
                    norm_h(b + 2)
                    merge(b, 4)
                    finish_h(b + 2)
                    merge(b, 5)
                    return
                second_layer(b - 1)
                merge(b, 0)
                if norms:
                    norm_x(b + 2)
                norm_c(b - 1)
                merge(b, 1)
                if norms:
                    norm_h(b + 2)
                merge(b, 2)
                if not last:
                    products_x(b + 1)
                merge(b, 3)
                if not last:
                    products_h(b + 1)
                u_low(b - 1)
                merge(b, 4)
                if norms:
                    finish_h(b + 2)
                merge(b, 5)
                top_two(b - 1)

            block_of(0, first=True)
            dve.wait_ge(S.x_rest, 16)
            dve.wait_ge(S.norm_in, 16)
            block_of(1)
            with dve.Fori(2, NB - 2) as b:
                block_of(b)
            block_of(NB - 2, norms=False)
            block_of(NB - 1, norms=False, last=True)
            second_layer(NB - 1)
            norm_c(NB - 1)
            u_low(NB - 1)
            top_two(NB - 1)

            dve.wait_ge(S.const, 10)
            top3 = top[:, :].rearrange("p (j n) -> p j n", n=8)
            tope3 = top_e[:, :].rearrange("p (j n) -> p j n", n=8)
            dve.wait_ge(S.top_e, 2 * NB)
            dve.wait_ge(S.w_lo, E * HALVES)
            dve.wait_ge(S.u_out, 16 * NB)
            ie = iota_e[:, :].unsqueeze(1).to_broadcast([P, TILES, E])
            for k in range(K):
                dve.tensor_tensor(chosen[:, k, :, :], ie, tope3[:, :, k:k + 1].to_broadcast([P, TILES, E]),
                                  ALU.is_equal).then_inc(S.chosen, 1)
            dve.memset(picked[:, TILES, :], 0.0).then_inc(S.picked, 1)
            dve.tensor_tensor(gap, top3[:, :, 1], top3[:, :, 0], sub).then_inc(S.gap, 1)
            dve.wait_ge(S.chosen, 2)
            dve.tensor_tensor(picked[:, 0:TILES, :], chosen[:, 0, :, :], chosen[:, 1, :, :], add).then_inc(S.picked, 1)
            dve.wait_ge(S.e2, 1)
            dve.tensor_scalar(den, e2, 1.0, None, add).then_inc(S.gate, 1)
            dve.wait_ge(S.gate, 1)
            dve.reciprocal(gate[:, 0, :], den).then_inc(S.gate, 1)
            dve.wait_ge(S.gate, 2)
            dve.tensor_tensor(gate[:, 1, :], gate[:, 0, :], e2, mul).then_inc(S.gate, 1)
            dve.wait_ge(S.gate, 3)
            dve.tensor_copy(gate_h, gate).then_inc(S.gate, 1)
            dve.wait_ge(S.gate, 4)
            dve.tensor_tensor(gate_f, gate, gate_h, sub).then_inc(S.gate, 1)
            dve.wait_ge(S.place_ps, 1)
            counts = ps_l1[:, 0:(TILES + 1) * E].rearrange("p (j e) -> p j e", e=E)
            dve.tensor_scalar(tiles_i, counts[:, TILES, :], float(P - 1), None, add).then_inc(S.tiles, 1)
            dve.wait_ge(S.tiles, 1)
            dve.tensor_scalar(tiles_i, tiles_i, 7, None, ALU.logical_shift_right).then_inc(S.tiles, 1)
            dve.wait_ge(S.tiles, 2)
            dve.tensor_tensor(tri_f, before8[:, :, :], tiles_i.unsqueeze(1).to_broadcast([P, E, E]), mul).then_inc(S.tiles, 1)
            dve.wait_ge(S.tiles, 3)
            dve.tensor_reduce(first_tile, tri_f, AX_X, add).then_inc(S.tiles, 1)
            dve.wait_ge(S.tiles, 4)
            dve.scalar_tensor_tensor(place, first_tile.unsqueeze(1).to_broadcast([P, TILES, E]), float(P),
                                     counts[:, 0:TILES, :], mul, add).then_inc(S.place, 1)
            dve.wait_ge(S.place, 1)
            for k in range(K):
                dve.tensor_tensor(place2[:, k, :, :], chosen[:, k, :, :], place, mul).then_inc(S.place, 1)
            dve.wait_ge(S.place, 3)
            dve.tensor_reduce(slot_f.rearrange("p (n o) -> p n o", o=1), place2.rearrange("p k j e -> p (k j) e"),
                              AX_X, add).then_inc(S.place, 1)
            dve.wait_ge(S.place, 4)
            dve.tensor_copy(slot_i, slot_f).then_inc(S.place, 1)
            dve.wait_ge(S.place, 5)
            dve.tensor_scalar(slot_tile, slot_i, 7, None, ALU.logical_shift_right).then_inc(S.place, 1)
            dve.tensor_scalar(slot_col, slot_i, P - 1, None, ALU.bitwise_and).then_inc(S.place, 1)
            dve.wait_ge(S.place, 7)
            dve.tensor_copy(slot_tile_f, slot_tile).then_inc(S.place, 1)
            dve.tensor_copy(slot_col_f, slot_col).then_inc(S.place, 1)
            dve.wait_ge(S.place, 9)
            dve.tensor_tensor(in_tile, iota_s[:, :].unsqueeze(1).to_broadcast([P, NC_, SLOT_TILES]),
                              slot_tile_f.unsqueeze(2).to_broadcast([P, NC_, SLOT_TILES]), ALU.is_equal).then_inc(S.in_tile, 1)
            dve.wait_ge(S.in_tile, 1)
            dve.tensor_tensor(tile_val[:, :, 0, :], in_tile, token1[:, :, :].rearrange("p k j -> p (k j)").unsqueeze(2)
                              .to_broadcast([P, NC_, SLOT_TILES]), mul).then_inc(S.tile_val, 1)
            for n in range(NC_):
                dve.tensor_scalar(col_hot[:, n, :], iota_p[:, :], slot_col_f[:, n:n + 1], None,
                                  ALU.is_equal).then_inc(S.col_hot, 1)
            dve.tensor_tensor(started, first_tile.unsqueeze(1).to_broadcast([P, SLOT_TILES, E]),
                              iota_s[:, :].unsqueeze(2).to_broadcast([P, SLOT_TILES, E]), ALU.is_le).then_inc(S.started, 1)
            dve.wait_ge(S.started, 1)
            dve.tensor_reduce(started_n, started, AX_X, add).then_inc(S.started, 1)
            dve.wait_ge(S.started, 2)
            dve.tensor_scalar(tile_expert, started_n, -1.0, None, add).then_inc(S.tile_expert, 1)
            dve.wait_ge(S.slots_ps, 1)
            dve.tensor_copy(slot_v, ps_l2[:, 0:3 * SLOT_TILES].rearrange("p (v s) -> p v s", v=3)).then_inc(S.slot_v, 1)
            dve.wait_ge(S.slot_v, 1)
            dve.tensor_scalar(slot_rows[:, :, 0], slot_v[:, 0, :], -1.0, 0.0, add, ALU.max).then_inc(S.slot_rows, 1)
            dve.tensor_scalar(empty, slot_v[:, 0, :], 0.0, pad_row[:, 0:1], ALU.is_equal, mul).then_inc(S.slot_v, 1)
            dve.tensor_tensor(slot_gate, slot_v[:, 1, :], slot_v[:, 2, :], add).then_inc(S.slot_gate, 1)
            dve.wait_ge(S.slot_v, 2)
            dve.scalar_tensor_tensor(slot_rows[:, :, 1], slot_v[:, 0, :], -1.0, empty, add, add).then_inc(S.slot_rows, 1)

            inv = 1.0 / WSCALE

            def h1_of(i, v, at):
                dve.wait_ge(S.h1_ps, i + 1)
                after(dve, S.silu, i - 1)
                dve.scalar_tensor_tensor(h1_sb[v], ps_h1[v][:, :], inv, biases[:, ds(at, H)], mul, add).then_inc(S.h1, 1)

            def g_of(i, v, at):
                dve.wait_ge(S.h3_ps, i + 1)
                dve.scalar_tensor_tensor(h3_sb[v], ps_h3[v][:, :], inv, biases[:, ds(at + H, H)], mul, add).then_inc(S.h3, 1)
                dve.wait_ge(S.h3, i + 1)
                dve.wait_ge(S.silu, i + 1)
                after(dve, S.gT_ps, i - 1)
                dve.tensor_tensor(g_sb[v], h3_sb[v], silu_sb[v], mul).then_inc(S.g, 1)

            def gT_low(i, v):
                dve.wait_ge(S.gT_hi, i + 1)
                dve.tensor_tensor(gT_lo[v], ps_gT[:, :], gT_hi[v], sub).then_inc(S.gT_lo, 1)

            def y_of(i, v, at):
                dve.wait_ge(S.y_ps, i + 1)
                after(dve, S.y_gated, i - 1)
                dve.scalar_tensor_tensor(y_sb[v], ps_y[:, 0:D], inv, biases[:, ds(at + 2 * H, D)], mul, add).then_inc(S.y, 1)

            def step(i, v, expert, expert2, peeled=False):
                n = SLOT_TILES
                if not peeled or i < n:
                    h1_of(i, v, expert * BE)
                    g_of(i, v, expert * BE)
                if not peeled or 1 <= i <= n:
                    gT_low(i - 1, 1 - v)
                if not peeled or 2 <= i:
                    y_of(i - 2, v, expert2 * BE)

            def pair(i, peeled=False):
                e = experts_of(mybir.EngineType.DVE, i, 2)
                for v in range(2):
                    if not peeled or i + v < SLOT_TILES + 2:
                        step(i + v, v, e[2 + v], e[v], peeled)

            dve.wait_ge(S.tile_expert, 1)
            dve.wait_ge(S.biases_in, 16)
            pair(0, peeled=True)
            pair(2, peeled=True)
            turns = (SLOT_TILES - 5) // 2
            with dve.Fori(2, 2 + turns) as m:
                pair(m * 2)
            for i in range(4 + 2 * turns, SLOT_TILES + 2, 2):
                pair(i, peeled=True)

        @block.tensor
        def _(pe):
            def transpose_T(b):
                for src, ready, freed, dst, done in ((xh, S.xhat, S.xhT, ps_xT, S.xT_ps),
                                                     (hh, S.hhat, S.hhT, ps_hT, S.hT_ps)):
                    pe.wait_ge(ready, (b + 1) * KB)
                    after(pe, freed, b)
                    for k in range(KB):
                        for c in range(DC):
                            last = pe.transpose(dst[:, c * BT + k * P:c * BT + (k + 1) * P],
                                                src[:, k, c * P:(c + 1) * P], ident[:, :])
                    last.then_inc(done, 1)

            def gains(b, kind, dst, freed, n, done):
                after(pe, freed, n)
                for c in range(DC):
                    last = pe.matmul(dst[:, c * BT:(c + 1) * BT], gain_tab[:, kind, c * P:(c + 1) * P],
                                     onehot[:, ds(b * BT, BT)], start=True, stop=True)
                last.then_inc(done, 1)

            def lora(e, h):
                n = e * HALVES + h
                if isinstance(e, int) and e == 0:
                    pe.wait_ge(S.lora_k0_in, 16 * 7)
                elif h in (0, 4):
                    pe.wait_ge(S.lora_k13_in if h == 0 else S.lora_k2_in, 16 * e)
                after(pe, S.w_sum, n)
                if h < 4:
                    a0, b0 = (h // 2) * D + (h % 2) * P, LB.start + (h // 2) * H
                    last = pe.matmul(ps_lora[:, :], lora_k[0:3 * R, a0:a0 + P], lora_k[0:3 * R, b0:b0 + H],
                                     start=True, stop=True)
                else:
                    for c in range(2):
                        a0, b0 = LA2.start + ((h % 2) * 2 + c) * P, LB.start + 2 * H
                        last = pe.matmul(ps_lora[:, c * D:(c + 1) * D], lora_k[0:3 * R, a0:a0 + P],
                                         lora_k[0:3 * R, b0:b0 + D], start=True, stop=True)
                last.then_inc(S.lora_ps, 1)

            def layer1(b, c, between):
                hid = slice(c * P, (c + 1) * P)
                o = ps_l1[:, c * BT:(c + 1) * BT]
                if c == 0:
                    after(pe, S.zT, b * DC)
                for n in range(DC):
                    pe.matmul(o, wx[:, n, hid], xT[:, n, ds(b * BT, BT)], start=(n == 0), stop=False)
                pe.matmul(o, gain_tab[:, 3, hid], onehot[:, ds(b * BT, BT)], start=False, stop=False)
                for prod, ready, w in ((prod_t, S.prod_t, 2), (prod_s, S.prod_s, 10), (prod_h, S.prod_h, 0)):
                    if c == 0:
                        pe.wait_ge(ready, b + 1)
                    for n in range(DC):
                        last = pe.matmul(o, int_w1[:, w + n, hid], prod[:, n * BT:(n + 1) * BT],
                                         start=False, stop=(w == 0 and n == DC - 1))
                    if w == 2:
                        between()
                if c == DC - 1:
                    last.then_inc(S.l1_ps, 1)

            def layer2(b):
                pe.wait_ge(S.zT, (b + 1) * DC)
                after(pe, S.c, b)
                for k in range(KB):
                    for c in range(DC):
                        last = pe.matmul(ps_l2[:, k * D:(k + 1) * D], zT[:, c, k * P:(k + 1) * P], int_w2[:, c, :],
                                         start=(c == 0), stop=(c == DC - 1))
                last.then_inc(S.l2_ps, 1)

            def transpose_u(b):
                pe.wait_ge(S.u, (b + 1) * KB)
                after(pe, S.lg, b)
                for n in range(KB * DC):
                    last = pe.transpose(ps_u[:, n * P:(n + 1) * P], u[:, n // DC, (n % DC) * P:(n % DC + 1) * P],
                                        ident[:, :])
                last.then_inc(S.uT_ps, 1)

            def logits(b):
                pe.wait_ge(S.uT, b + 1)
                for k in range(KB):
                    for c in range(DC):
                        last = pe.matmul(ps_u[:, k * E:(k + 1) * E], uT_sb[:, (k * DC + c) * P:(k * DC + c + 1) * P],
                                         wgT[:, c, :], start=(c == 0), stop=(c == DC - 1))
                last.then_inc(S.lg_ps, 1)

            def gains_ts(b):
                gains(b, 1, ps_g0, S.prod_h, b, S.gt_ps)
                gains(b, 2, ps_g1, S.prod_s, b, S.gs_ps)

            def gains_h(b):
                gains(b, 0, ps_g0, S.prod_t, b + 1, S.gh_ps)

            def networks_layer2():
                for k in range(3):
                    o = ps_u[0:NBATCH, k * D:(k + 1) * D] if k < 2 else ps_l2[0:NBATCH, 0:D]
                    for c in range(DC):
                        last = pe.matmul(o, mlp_h[:, k, c, :], mlp_w2[:, k, c, :], start=(c == 0), stop=(c == DC - 1))
                last.then_inc(S.mlp_o_ps, 1)

            pe.wait_ge(S.w1_in, 32)
            pe.wait_ge(S.shift_z, 3)
            for n, (k, c) in enumerate((k, c) for k in range(NKIND) for c in range(DC)):
                last = pe.matmul(ps_hT[0:ROWS, 0:D], shift_Z[:, c, k, :], int_w1[:, (0, 2, 10)[k] + c, :],
                                 start=(n == 0), stop=(n == 2 * NKIND - 1))
            last.then_inc(S.shift_ps, 1)
            pe.wait_ge(S.net_in, 16)
            for k, n in enumerate((128, 64, 32)):
                for c in range(DC):
                    last = pe.matmul(ps_lora[:, (k * DC + c) * 2:(k * DC + c) * 2 + 2], mlp_w1[0:n, k, c * P:(c + 1) * P],
                                     mlp_s[0:n, k, :], start=True, stop=True)
            last.then_inc(S.mlp_h_ps, 1)
            pe.wait_ge(S.gain_s, 4)
            pe.wait_ge(S.const, 1)
            transpose_T(0)
            pe.wait_ge(S.tab, 10)
            pe.wait_ge(S.onehot, 1)
            gains_ts(0)
            pe.wait_ge(S.mlp_h, 6)
            networks_layer2()
            gains_h(0)
            pe.wait_ge(S.xT_first, 16)
            pe.wait_ge(S.wx, 3)

            def networks_bias():
                pe.wait_ge(S.v, 8)
                for n in range(3 * DC):
                    last = pe.transpose(ps_l2[:, D + 2 * n:D + 2 * n + 2], mlp_v[0:NBATCH, n // DC, (n % DC) * P:(n % DC + 1) * P],
                                        ident[0:NBATCH, 0:NBATCH])
                last.then_inc(S.vT_ps, 1)
                pe.wait_ge(S.vT, 1)
                for c in range(DC):
                    for n in range(3 * DC):
                        last = pe.matmul(ps_u[:, c * NBATCH:(c + 1) * NBATCH], int_w1[:, 4 + n, c * P:(c + 1) * P],
                                         mlp_vT[:, n, :], start=(n == 0), stop=(n == 3 * DC - 1))
                last.then_inc(S.bias_ps, 1)
                pe.wait_ge(S.int_w2_in, 16)

            def block_of(b, first=False, last=False):
                layer1(b, 0, (lambda: None) if first else (lambda: lora(b, 0)))
                if not first:
                    lora(b, 1)
                if not last:
                    transpose_T(b + 1)
                    gains_ts(b + 1)
                if first:
                    lora(b, 0)
                layer1(b, 1, lambda: lora(b, 1 if first else 2))
                if first:
                    networks_bias()
                    lora(b, 2)
                else:
                    transpose_u(b - 1)
                lora(b, 3)
                if not last:
                    gains_h(b + 1)
                layer2(b)
                lora(b, 4)
                if not first:
                    logits(b - 1)
                lora(b, 5)

            block_of(0, first=True)
            block_of(1)
            pe.wait_ge(S.xT_rest, 16)
            with pe.Fori(2, NB - 1) as b:
                block_of(b)
            block_of(NB - 1, last=True)
            transpose_u(NB - 1)
            logits(NB - 1)

            pe.wait_ge(S.const_d, 2)
            pe.wait_ge(S.const, 10)
            pe.wait_ge(S.picked, 2)
            o = ps_l1[:, 0:(TILES + 1) * E].rearrange("p (j e) -> p j e", e=E)
            for j in range(TILES):
                pe.matmul(o[:, j + 1:, :], ones16[:, :], picked[:, j:j + 1, :].to_broadcast([P, TILES - j, E]),
                          start=(j == 0), stop=False, skip_group_check=True)
            last = pe.matmul(o, before[:, :], picked, start=False, stop=True, skip_group_check=True)
            last.then_inc(S.place_ps, 1)
            pe.wait_ge(S.tile_val, 1)
            pe.wait_ge(S.gate_val, 2)
            for n in range(NC_):
                pe.wait_ge(S.col_hot, n + 1)
                last = pe.matmul(ps_l2[:, 0:3 * SLOT_TILES], col_hot[:, n, :], tile_val[:, n, :, :],
                                 start=(n == 0), stop=(n == NC_ - 1))
            last.then_inc(S.slots_ps, 1)

            def rows_T(i, h, v):
                pe.wait_ge((S.rows0, S.rows1)[v], 16 * (h + 1))
                after(pe, S.rowsT, i - 1)
                for n in range(2 * DC):
                    last = pe.transpose(ps_rowsT[v][:, n * P:(n + 1) * P], rows_in[v][:, n * P:(n + 1) * P], ident16[:, :])
                last.then_inc((S.rowsT_ps0, S.rowsT_ps1)[v], 1)

            def first_layer(i, v, at):
                pe.wait_ge(S.rowsT, i + 1)
                for w, bank_, freed, done in ((0, ps_h1[v], S.h1, S.h1_ps), (DC * H, ps_h3[v], S.h3, S.h3_ps)):
                    after(pe, freed, i - 1)
                    passes = [(part_, c, w_) for c in range(DC) for part_, w_ in ((0, w_hi), (0, w_lo), (DC, w_hi))]
                    for n, (part_, c, w_) in enumerate(passes):
                        last = pe.matmul(bank_[:, :], rowsT[v][:, (part_ + c) * P:(part_ + c + 1) * P],
                                         w_[:, ds(at + (w + c * H), H)], start=(n == 0), stop=(n == len(passes) - 1))
                    last.then_inc(done, 1)

            def g_T(i, v):
                pe.wait_ge(S.g, i + 1)
                after(pe, S.gT_lo, i)
                for n in range(HC):
                    last = pe.transpose(ps_gT[:, n * P:(n + 1) * P], g_sb[v][:, n * P:(n + 1) * P], ident[:, :])
                last.then_inc(S.gT_ps, 1)

            def second_layer(i, v, at):
                pe.wait_ge(S.gT_lo, i + 1)
                after(pe, S.y, i)
                passes = [(g_, c, w_) for c in range(HC) for g_, w_ in ((gT_hi, w_hi), (gT_hi, w_lo), (gT_lo, w_hi))]
                for n, (g_, c, w_) in enumerate(passes):
                    last = pe.matmul(ps_y[:, 0:D], g_[v][:, c * P:(c + 1) * P], w_[:, ds(at + (2 * DC * H + c * D), D)],
                                     start=(n == 0), stop=(n == len(passes) - 1))
                last.then_inc(S.y_ps, 1)

            def step(i, h, v, expert, expert2, peeled=False):
                n = SLOT_TILES
                if not peeled or i < n:
                    first_layer(i, v, expert * WE)
                if not peeled or i + 1 < n:
                    rows_T(i + 1, h + v, 1 - v)
                if not peeled or 1 <= i <= n:
                    g_T(i - 1, 1 - v)
                if not peeled or 2 <= i:
                    second_layer(i - 2, v, expert2 * WE)

            def steps(i, n, h, peeled=False):
                e = experts_of(mybir.EngineType.PE, i, n)
                for v in range(n):
                    if not peeled or i + v < SLOT_TILES + 2:
                        step(i + v, h + v // 2, v % 2, e[2 + v], e[v], peeled)

            pe.wait_ge(S.tile_expert, 1)
            pe.wait_ge(S.w_lo, E * HALVES)
            rows_T(0, 0, 0)
            steps(0, 4, 0, peeled=True)
            turns = (SLOT_TILES - 5) // 4
            with pe.Fori(1, 1 + turns) as m:
                steps(m * 4, 4, m * 2)
            for i in range(4 + 4 * turns, SLOT_TILES + 2, 4):
                steps(i, 4, i // 2, peeled=True)


SEMAPHORES = """
ids_in x_first aw_in onehot_ids_in w1_in w1x_in x_rest net_in net_rows_in xT_first xT_rest int_w2_in norm_in out_in lora_scaled w1s_in w3s_in w2s_in x_third lora_k0_in lora_k13_in lora_k2_in
u_out biases_in added0 added1 const0 const path_now path_in x_ve h_ve c_ve v_ve x_rstd h_rstd c_rstd v_rstd
w_sum w_hi w_lo u gather_now rows0 rows1 scatter_now y_gated slot_rows slot_gate
aw_max aw_exp shift_in gain_in lora_in lora_hi lora_lo lora_d_out mlp_h_ps mlp_h xT_ps hT_ps
prod_t prod_s prod_h xhT hhT l1_ps l2_ps zT u_hi u_lo uT_ps uT lg_ps lg bias_blk gap e2 rowsT_ps0 rowsT_ps1
rowsT h1_ps h3_ps h1 h3 silu gT_ps gT_hi gT_lo g y_ps y
x_st x_mv xhat h_scaled h_pre h_st h_mv hhat gt_ps gs_ps gh_ps c c_st c_mv chat top top_i top_e
const_d row16 onehot mixw shift_z gain_s wx shift_ps tab mlp_o_ps v v_st v_mv vT_ps vT bias_ps
net_mixed chosen picked gate place_ps tiles place in_tile tile_val col_hot gate_val started tile_expert slots_ps slot_v
lora_ps passed
"""
REGION = 27808


def kernel(**inputs):
    import concourse.bacc as _bacc
    from concourse.bass_utils import run_bass_kernel_spmd as _run

    i = {k.replace("L0_cond_", "").replace("L0_ffn_", ""): np.asarray(v) for k, v in inputs.items()}
    f = np.ascontiguousarray

    def by_chunk(w):
        e, r, n = w.shape
        return f(w.reshape(e, r // P, P, n).transpose(0, 2, 1, 3).reshape(e * P, -1))

    x = f(i["x"].reshape(T, D))
    er = lambda w: w.reshape(E * R, -1)
    arrays = {
        "x": x, "xT": f(x.T),
        "path_ids": f(i["itok_BxS_0_999"].reshape(TILES, P).T),
        "onehot_ids": f(np.tile(np.repeat(np.stack([i["itok_BxS_0_4"].reshape(T), i["mask_BxS_ik0"].reshape(T)]),
                                          16, axis=0), (3, 1))),
        "path_tab": f(np.concatenate([i["pw_g"], i["pw_b"]], axis=1)),
        "aw": f(i["aw"]),
        "int_W1": f(i["int_W1"]), "int_w2g": f(np.concatenate([i["int_W2"], i["Wg"].T], axis=1)),
        "norm_rows": f(np.concatenate([i["int_b2"], i["int_g"], i["int_be"]])),
        "W1T": by_chunk(i["W1"].transpose(0, 2, 1)), "W3T": by_chunk(i["W3"].transpose(0, 2, 1)),
        "W2T": by_chunk(i["W2"].transpose(0, 2, 1)),
        "lora": f(np.concatenate([er(i["A1"]), er(i["A3"]), er(i["B1"].transpose(0, 2, 1)),
                                  er(i["B3"].transpose(0, 2, 1)), er(i["B2"].transpose(0, 2, 1)),
                                  er(i["A2"])], axis=1)),
        "biases": f(np.concatenate([i["b1"], i["b3"], i["b2"]], axis=1).reshape(-1)),
    }
    gains, shifts = np.zeros((ROWS, 4, D), np.float32), np.zeros((D, NKIND, ROWS), np.float32)
    for k, name in enumerate(("cp", "tm", "ms")):
        g, b = i[name + "_g"], i[name + "_b"]
        for r in range(16 * (k // 2), ROWS, 32):
            gains[r:r + len(g), k], shifts[:, k, r:r + len(b)] = g, b.T
    arrays["gains"], arrays["shiftZ"] = gains, shifts
    net = np.zeros((P, NET), np.float32)
    names = ("mem", "noi", "res")
    for k, (name, s) in enumerate(zip(names, ("cond_512", "cond_64", "fside_Bx32_0"))):
        w1 = i[name + "_W1"]
        net[:len(w1), NET_S + k * NBATCH:NET_S + (k + 1) * NBATCH] = i[s].T
        net[:, NET_B1 + k * DC:NET_B1 + (k + 1) * DC] = i[name + "_b1"].reshape(DC, P).T
        net[:len(w1), NET_W1 + k * D:NET_W1 + (k + 1) * D] = w1
        net[:, NET_W2 + k * DC * D:NET_W2 + (k + 1) * DC * D] = i[name + "_W2"].reshape(DC, P, D).transpose(1, 0, 2).reshape(P, -1)
    net[:, NET_INT:NET_INT + DC] = i["int_b1"].reshape(DC, P).T
    arrays["net"] = net
    arrays["net_rows"] = f(np.concatenate([i[name + part] for part in ("_b2", "_g", "_be") for name in names]))

    nc = _bacc.Bacc("TRN2", target_bir_lowering=False, num_devices=1)
    aps = {k: nc.dram_tensor(f"in_{k}", v.shape, mybir.dt.from_np(v.dtype), kind="ExternalInput").ap()
           for k, v in arrays.items()}
    out = nc.dram_tensor("out_rows", (T + PAD, D), F32, kind="ExternalOutput").ap()
    a = namedtuple("Inputs", aps)(*aps.values())
    build(nc, a, out)
    r = _run(nc, [{f"in_{k}": v for k, v in arrays.items()}], core_ids=[0])
    return r.results[0]["out_rows"][:T].reshape(inputs["x"].shape)
```

```python
from collections import namedtuple
from contextlib import ExitStack

import numpy as np

import concourse.bass as bass
from concourse import mybir

F32 = mybir.dt.float32
F16 = mybir.dt.float16
BF16 = mybir.dt.bfloat16
I32 = mybir.dt.int32
U32 = mybir.dt.uint32
ALU = mybir.AluOpType
ACT = mybir.ActivationFunctionType
AX_X = mybir.AxisListType.X

P = 128
T, D, H, E, R, K = 2048, 256, 512, 8, 16, 2
DC, HC = D // P, H // P
TILES = T // P
KB = 2
BT = KB * P
NB = T // BT
WARM = 6
EARLY = TILES - 2 * KB
NBATCH = 2
SLOT_TILES = (T * K) // P + E - 1
PAD = P
WE = 2 * D * H // P + D * H // P
HALF = 512
HALVES = WE // HALF
LA13, LB, LA2 = slice(0, 2 * D), slice(2 * D, 2 * D + 2 * H + D), slice(2 * D + 2 * H + D, 3 * D + 3 * H)
LORA = LA2.stop
LK13 = 2 * D + 2 * H
BE = 2 * H + D
WSCALE = 64.0
EPS = 1e-5
NKIND = 3
ROWS = 96
NET_S, NET_B1 = 0, NKIND * NBATCH
NET_INT, NET_W1 = NET_B1 + 3 * DC, NET_B1 + 4 * DC
NET_W2 = NET_W1 + 3 * D
NET = NET_W2 + 3 * DC * D
ds = bass.ds


def build(nc, a, out):
    with ExitStack() as ctx:
        def sb(name, shape, dt):
            return ctx.enter_context(nc.sbuf_tensor(name, shape, dt))

        def psum(name, shape, dt=F32):
            return ctx.enter_context(nc.psum_tensor(name, shape, dt))

        S = namedtuple("Semaphores", SEMAPHORES)(*[ctx.enter_context(nc.semaphore(n)) for n in SEMAPHORES.split()])

        u_rows = nc.dram_tensor("u_rows", (T, 2 * D), F16, kind="Internal").ap()
        lora_d = nc.dram_tensor("lora_d", (E, 3, R, LORA), F16, kind="Internal").ap()

        w_hi = sb("w_hi", [P, E * WE], F16)
        w_lo = sb("w_lo", [P, E * WE], F16)
        ident = sb("ident", [P, P], F32)
        ident16 = sb("ident16", [P, P], F16)
        ones16 = sb("ones16", [P, P], F16)
        before = sb("before", [P, P], F16)
        before8 = sb("before8", [P, E, E], F32)
        iota_p = sb("iota_p", [P, P], F16)
        iota_e = sb("iota_e", [P, E], F32)
        iota_s = sb("iota_s", [P, SLOT_TILES], F16)
        token1 = sb("token1", [P, K, TILES], F16)
        pad_row = sb("pad_row", [P, 1], F32)
        top = sb("top", [P, TILES * 8], F32)
        top_e = sb("top_e", [P, TILES * 8], U32)

        region = sb("region", [P, REGION], F32)
        at = [0]

        def part(words, dt=F32):
            v = region[:, at[0]:at[0] + words]
            at[0] += words
            return v if dt == F32 else v.bitcast(dt)

        x_tok = part(TILES * D)
        int_w1x = part(3 * DC * D).rearrange("p (c n) -> p c n", c=3 * DC)
        xh = part(KB * D).rearrange("p (k d) -> p k d", k=KB)
        hh = part(KB * D).rearrange("p (k d) -> p k d", k=KB)
        xhT = part(DC * BT)
        hhT = part(DC * BT)
        pw_rows = part(KB * 2 * D).rearrange("p (k n) -> p k n", k=KB)
        xT_at = at[0]
        xT_flat = part(DC * T)
        xT = xT_flat.rearrange("p (b c t) -> p b c t", b=NB, c=DC)
        prod_t = part(DC * BT)
        prod_s = part(DC * BT)
        prod_h = part(DC * BT)
        int_w1 = part(3 * DC * D).rearrange("p (c n) -> p c n", c=3 * DC)
        wx = part(DC * D).rearrange("p (c n) -> p c n", c=DC)
        int_w2g = part(DC * (D + E)).rearrange("p (c n) -> p c n", c=DC)
        int_w2, wgT = int_w2g[:, :, 0:D], int_w2g[:, :, D:]
        onehot = part(T // 2, BF16)[0:ROWS, :]
        gain_tab = part(4 * D // 2, BF16)[0:ROWS, :].rearrange("p (k d) -> p k d", k=4)
        norm_flat = part(3 * D)
        norm_rows = norm_flat.rearrange("p (k d) -> p k d", k=3)
        bias_blk = part(NB * DC)
        zT = part(DC * BT).rearrange("p (c t) -> p c t", c=DC)
        c_flat = part(KB * D)
        c_sb = c_flat.rearrange("p (k d) -> p k d", k=KB)
        u = part(KB * D).rearrange("p (k d) -> p k d", k=KB)
        u_split = part(KB * D, F16).rearrange("p (k n) -> p k n", k=KB)
        uT_sb = part(KB * D)
        w_stage = [part(2 * HALF) for _ in range(3)]
        w_full = [part(HALF) for _ in range(3)]
        lora_k = part(LORA // 2, F16)
        small = part(96)
        x_st, x_mv = small[:, 0:12], small[:, 12:16].rearrange("p (k n) -> p k n", k=KB)
        h_st, h_mv = small[:, 16:28], small[:, 28:32].rearrange("p (k n) -> p k n", k=KB)
        c_st, c_mv = small[:, 32:44], small[:, 44:48].rearrange("p (k n) -> p k n", k=KB)
        x_ve, x_rs = small[:, 48:50], small[:, 50:52]
        h_ve, h_rs = small[:, 52:54], small[:, 54:56]
        c_ve, c_rs = small[:, 56:58], small[:, 58:60]
        v_ve, v_rs = small[:, 60:63], small[:, 63:66]
        minus_half, eps_sb = small[:, 66:69], small[:, 92:95]
        aw_e, aw_m, aw_s, aw_r = small[:, 70:76], small[:, 76:77], small[:, 77:78], small[:, 78:79]
        mixw = small[:, 80:86]
        lg_sb = part(KB * E)
        top_now = part(KB * 8)
        top_e_now = part(KB * 8, U32)
        path_ids = part(TILES, I32)
        path_now = part(KB, I32)
        aw_sb = part(6)
        cond_end = at[0]

        lo5 = w_lo[:, 3 * WE + 2 * LORA:6 * WE].bitcast(F32)
        hi5 = w_hi[:, 3 * WE + 2 * LORA:6 * WE].bitcast(F32)
        ids_i = hi5[:, 0:T].bitcast(I32)
        setup_f = hi5[:, T:T + P]
        gain_f = lo5[0:ROWS, 0:4 * D].rearrange("p (k d) -> p k d", k=4)
        gain_r = lo5[0:ROWS, 4 * D:8 * D].rearrange("p (k d) -> p k d", k=4)
        gain_h = c_flat[0:ROWS, :].bitcast(BF16).rearrange("p (k d) -> p k d", k=4)
        row16, row16_f = small[:, 88:90].bitcast(I32), small[:, 90:91]
        wl = w_lo[:, (E - 2) * WE:E * WE].bitcast(F32)
        wh = w_hi[:, (E - 2) * WE:E * WE].bitcast(F32)
        net = wl[:, 0:NET]
        mlp_s = net[:, NET_S:NET_B1].rearrange("p (k b) -> p k b", k=3)
        mlp_b1 = net[:, NET_B1:NET_INT].rearrange("p (k c) -> p k c", k=3)
        int_b1 = net[:, NET_INT:NET_W1]
        mlp_w1 = net[:, NET_W1:NET_W2].rearrange("p (k n) -> p k n", k=3)
        mlp_w2 = net[:, NET_W2:].rearrange("p (k c n) -> p k c n", k=3, c=DC)
        shift_Z = wl[:, NET:NET + DC * NKIND * ROWS].rearrange("p (c k r) -> p c k r", c=DC, k=NKIND)
        net_small = wl[:, NET + DC * NKIND * ROWS:]
        mlp_h = net_small[:, 0:12].rearrange("p (k c b) -> p k c b", k=3, c=DC)
        mlp_vT = net_small[:, 12:24].rearrange("p (k b) -> p k b", b=NBATCH)
        mlp_st = net_small[:, 24:42].rearrange("p (k n) -> p k n", k=3)
        mlp_mv = net_small[:, 42:48].rearrange("p (k n) -> p k n", k=3)
        net_rows = wh[:, 0:9 * D]
        mlp_b2, mlp_g, mlp_be = (net_rows[:, n * 3 * D:(n + 1) * 3 * D].rearrange("p (k n) -> p k n", k=3)
                                 for n in range(3))
        mlp_v = wh[:, 9 * D:12 * D].rearrange("p (k n) -> p k n", k=3)
        lora_f = w_lo[:, 3 * WE:3 * WE + 2 * LORA].bitcast(F32)
        lora_h = w_hi[:, 3 * WE:3 * WE + LORA]
        lora_l = w_hi[:, 3 * WE + LORA:3 * WE + 2 * LORA]

        at[0] = 0
        NC_ = K * TILES
        chosen = part(NC_ * E).rearrange("p (k j e) -> p k j e", k=K, e=E)
        picked = part((TILES + 1) * E // 2, F16).rearrange("p (j e) -> p j e", e=E)
        place = part(NC_ * E).rearrange("p (k j e) -> p k j e", k=K, e=E)
        pos_f = part(NC_).rearrange("p (k j) -> p k j", k=K)
        pos_i = part(NC_, I32).rearrange("p (k j) -> p k j", k=K)
        pos_tile = part(NC_, I32).rearrange("p (k j) -> p k j", k=K)
        pos_col = part(NC_, I32).rearrange("p (k j) -> p k j", k=K)
        pos_tile_f = part(NC_)
        pos_col_f = part(NC_)
        col_hot = part(NC_ * P // 2, F16).rearrange("p (n c) -> p n c", n=NC_)
        iota_sn = part(SLOT_TILES * NC_ // 2, F16).rearrange("p (s n) -> p s n", s=SLOT_TILES)
        assert at[0] <= TILES * D
        early_biases = (xT_at + (NB - 1) * DC * BT - at[0]) // BE * BE
        biases = part(E * BE)
        assert at[0] <= xT_at + DC * T + 3 * DC * BT
        rows_in = [part(D, F16) for _ in range(2)]
        rowsT = [part(D, F16) for _ in range(2)]
        h1_sb = [part(H) for _ in range(2)]
        h3_sb = [part(H) for _ in range(2)]
        silu_sb = [part(H) for _ in range(2)]
        g_sb = [part(H) for _ in range(2)]
        gT_hi = [part(H // 2, F16) for _ in range(2)]
        gT_lo = [part(H // 2, F16) for _ in range(2)]
        y_sb = [part(D) for _ in range(2)]
        y_gated = [part(D) for _ in range(2)]
        gather_now = [part(1, I32) for _ in range(2)]
        scatter_now = [part(1, I32) for _ in range(2)]
        slot_rows = part(SLOT_TILES * 2, I32).rearrange("p (i n) -> p i n", n=2)
        slot_gate = part(SLOT_TILES)
        tile_expert = part(SLOT_TILES, I32)
        start_of = part(NC_ * E).rearrange("p (n e) -> p n e", e=E)
        start_f = part(NC_)
        slot_tile_f = part(NC_ // 2, F16)
        tiles_i = part(E, I32)
        tiles_f = part(E)
        tri_f = part(E * E).rearrange("p (a b) -> p a b", a=E)
        first_tile = part(E)
        started = part(SLOT_TILES * E).rearrange("p (i e) -> p i e", e=E)
        started_n = part(SLOT_TILES)
        gap = part(TILES)
        e2 = part(TILES)
        den = part(TILES)
        gate = part(K * TILES).rearrange("p (k j) -> p k j", k=K)
        gate_l = part(K * TILES // 2, F16).rearrange("p (k j) -> p k j", k=K)
        gate_h = part(K * TILES // 2, F16).rearrange("p (k j) -> p k j", k=K)
        in_tile = part(NC_ * SLOT_TILES // 2, F16).rearrange("p (s n) -> p s n", s=SLOT_TILES)
        tile_val = part(NC_ * 3 * SLOT_TILES // 2, F16).rearrange("p (v s n) -> p v s n", v=3, s=SLOT_TILES)
        gate_v = part(2 * SLOT_TILES).rearrange("p (v s) -> p v s", v=2)
        empty = part(SLOT_TILES)
        main_end = at[0]
        assert max(cond_end, main_end) <= REGION, (cond_end, main_end)

        bank = [psum(f"bank{i}", [P, 512]) for i in range(8)]
        ps_xT, ps_hT, ps_g0, ps_g1, ps_l1, ps_l2, ps_u, ps_lora = bank
        ps_counts, ps_rows, ps_gates = ps_g0, ps_l2, ps_u
        ps_h1, ps_h3 = bank[0:2], bank[2:4]
        ps_rowsT = [bank[4][:, 0:256].bitcast(F16), bank[5][:, 0:256].bitcast(F16)]
        ps_gT, ps_y = bank[6], bank[7]

        block = ctx.enter_context(nc.Block())

        def after(engine, semaphore, count):
            if not isinstance(count, int) or count > 0:
                engine.wait_ge(semaphore, count)

        def before_plain(engine, semaphore, count):
            engine.wait_ge(semaphore, count)
            if not isinstance(count, int):
                engine.sem_inc(S.passed, 1)

        def experts_of(engine, i, steps):
            first, end = i - 2, i + steps
            if isinstance(i, int):
                first, end = max(first, 0), min(end, SLOT_TILES)
            _, e = nc.values_load_multi_w_load_instructions(
                tile_expert[0:1, ds(first, steps + 2 if not isinstance(i, int) else end - first)], engines=(engine,),
                min_val=0, max_val=E - 1, skip_runtime_bounds_check_because=
                "1 to E experts have started at any tile, and the value is their count less one")
            missing = max(2 - i, 0) if isinstance(i, int) else 0
            return [None] * missing + list(e) + [None] * steps

        @block.sync
        def _(sp):
            x_v = a.x.rearrange("(j p) d -> p j d", p=P)
            xt_v = x_tok.rearrange("p (j d) -> p j d", d=D)
            sp.dma_start(path_ids, a.path_ids).then_inc(S.ids_in, 16)
            sp.dma_start(xt_v[:, 0:2 * KB, :], x_v[:, 0:2 * KB, :]).then_inc(S.x_first, 16)
            sp.dma_start(ids_i[0:ROWS, :], a.onehot_ids).then_inc(S.onehot_ids_in, 16)
            w1_v = a.int_W1.rearrange("(c p) n -> p c n", p=P)
            sp.dma_start(int_w1[:, 0:4, :], w1_v[:, 0:4, :]).then_inc(S.w1_in, 16)
            sp.dma_start(int_w1[:, 4:6, :], w1_v[:, 10:12, :]).then_inc(S.w1_in, 16)
            sp.dma_start(int_w1x, w1_v[:, 4:10, :]).then_inc(S.w1x_in, 16)
            sp.dma_start(xt_v[:, 2 * KB:3 * KB, :], x_v[:, 2 * KB:3 * KB, :]).then_inc(S.x_third, 16)
            sp.dma_start(net, a.net).then_inc(S.net_in, 16)
            sp.dma_start(net_rows[0:NBATCH, :], a.net_rows.partition_broadcast(NBATCH)).then_inc(S.net_rows_in, 16)
            xT_v = a.xT.rearrange("p (b c t) -> p b c t", b=NB, c=DC)
            sp.dma_start(xT[:, 0:2], xT_v[:, 0:2]).then_inc(S.xT_first, 16)

            def load_weights(e, parts):
                for p in parts:
                    w = (a.W1T, a.W3T, a.W2T)[p]
                    after(sp, S.w_sum, (e - 1) * HALVES + 2 * p + 2)
                    sp.dma_start(w_stage[p], w[ds(e * P, P), :]).then_inc((S.w1s_in, S.w3s_in, S.w2s_in)[p], 16)

            def load_lora(e, columns, used):
                sp.wait_ge(S.lora_ps, (e - 1) * HALVES + used)
                sp.dma_start(lora_k[0:3 * R, columns], lora_rows[ds(e * 3 * R, 3 * R), columns]
                             ).then_inc(S.lora_k13_in if used == 4 else S.lora_k2_in, 16)

            def store_rows(b):
                after(sp, S.u_lo, b + 1)
                sp.dma_start(u_rows[ds(b * BT, BT), :].rearrange("(k p) n -> p k n", p=P),
                             u_split).then_inc(S.u_out, 16)

            def load_expert(e, rows):
                load_weights(e, (0,))
                load_lora(e, slice(0, LK13), 4)
                load_weights(e, (1,))
                if rows:
                    store_rows(e - 2)
                load_lora(e, slice(LK13, LORA), 6)
                load_weights(e, (2,))

            load_weights(0, (0,))
            lora_rows = lora_d.rearrange("e q r n -> (e q r) n")
            sp.wait_ge(S.lora_hi, 2)
            high = ((0, slice(0, LORA)), (1, LA13), (1, LA2), (2, LB))
            low = ((1, LB), (2, LA13), (2, LA2))
            for q, columns in high:
                sp.dma_start(lora_k[q * R:(q + 1) * R, columns], lora_h[0:R, columns]).then_inc(S.lora_k0_in, 16)
            load_weights(0, (1,))
            sp.wait_ge(S.lora_lo, 2)
            for q, columns in low:
                sp.dma_start(lora_k[q * R:(q + 1) * R, columns], lora_l[0:R, columns]).then_inc(S.lora_k0_in, 16)
            load_weights(0, (2,))
            sp.dma_start(int_w2g, a.int_w2g.rearrange("(c p) n -> p c n", p=P)).then_inc(S.int_w2_in, 16)
            sp.dma_start(norm_flat, a.norm_rows.partition_broadcast(P)).then_inc(S.norm_in, 16)
            for src, parts in ((lora_h, high), (lora_l, low)):
                for q, columns in parts:
                    sp.dma_start(lora_d[:, q, :, columns], src[:, columns]).then_inc(S.lora_d_out, 16)
            sp.dma_start(xt_v[:, 3 * KB:, :], x_v[:, 3 * KB:, :]).then_inc(S.x_rest, 16)
            sp.dma_start(xT[:, 2:], xT_v[:, 2:]).then_inc(S.xT_rest, 16)
            sp.wait_ge(S.lora_d_out, 16 * 7)
            load_expert(1, rows=False)
            sp.dma_start(out[0:T, :], a.x).then_inc(S.out_in, 16)
            sp.dma_start(out[T:T + PAD, :], a.x[0:PAD, :]).then_inc(S.out_in, 16)
            with sp.Fori(2, E) as e:
                load_expert(e, rows=True)
            sp.wait_ge(S.prod_h, NB)
            sp.wait_ge(S.l1_ps, NB - 1)
            sp.dma_start(biases[:, 0:early_biases], a.biases[0:early_biases].partition_broadcast(P)).then_inc(S.biases_in, 16)
            store_rows(NB - 2)
            sp.wait_ge(S.l1_ps, NB)
            sp.dma_start(biases[:, early_biases:], a.biases[early_biases:].partition_broadcast(P)).then_inc(S.biases_in, 16)
            store_rows(NB - 1)
            sp.wait_ge(S.added0, 16 * ((SLOT_TILES + 1) // 2))
            sp.wait_ge(S.added1, 16 * (SLOT_TILES // 2))

        @block.gpsimd
        def _(pool):
            eq, gt = ALU.not_equal, ALU.is_gt
            pool.memset(ident[:, :], 0.0).then_inc(S.const0, 1)
            pool.memset(setup_f, 1.0).then_inc(S.const0, 1)
            pool.memset(before8[:, :, :], 1.0).then_inc(S.const0, 1)
            pool.memset(minus_half, -0.5).then_inc(S.const0, 1)
            pool.memset(eps_sb, EPS).then_inc(S.const0, 1)
            pool.wait_ge(S.const0, 5)
            pool.affine_select(out=ident[:, :], in_=ident[:, :], compare_op=eq, fill=1.0, base=0,
                               pattern=[[-1, P]], channel_multiplier=1).then_inc(S.const, 1)
            pool.affine_select(out=setup_f, in_=setup_f, compare_op=gt, fill=0.0, base=0,
                               pattern=[[1, P]], channel_multiplier=-1).then_inc(S.const, 1)
            pool.affine_select(out=before8[:, :, :], in_=before8[:, :, :], compare_op=gt, fill=0.0, base=0,
                               pattern=[[1, E], [-1, E]], channel_multiplier=0).then_inc(S.const, 1)
            pool.iota(row16[:, 0:1], [[0, 1]], base=0, channel_multiplier=1).then_inc(S.const, 1)

            def gather_path(b):
                if not isinstance(b, int) or b:
                    pool.wait_ge(S.h_pre, b)
                n = b + 1
                pool.tensor_copy(path_now, path_ids[:, ds(b * KB, KB)]).then_inc(S.path_now, 1)
                before_plain(pool, S.path_now, n)
                for k in range(KB):
                    pool.indirect_dma_start(pw_rows[:, k, :], None, a.path_tab,
                                            bass.IndirectOffsetOnAxis(ap=path_now[:, k:k + 1], axis=0)
                                            ).then_inc(S.path_in, 16)

            def rstd(mv, ve, rs, mv_ready, n, shifted, done, count):
                pool.wait_ge(mv_ready, n)
                pool.tensor_tensor(ve, mv, eps_sb[0:rs.shape[0], 0:rs.shape[1]], ALU.add).then_inc(shifted, 1)
                pool.wait_ge(shifted, count)
                pool.tensor_tensor(rs, ve, minus_half[0:rs.shape[0], 0:rs.shape[1]], ALU.pow).then_inc(done, 1)

            def rstd_x(b):
                rstd(x_mv[:, :, 1], x_ve, x_rs, S.x_mv, (b + 1) * KB, S.x_ve, S.x_rstd, b + 1)

            def rstd_h(b):
                rstd(h_mv[:, :, 1], h_ve, h_rs, S.h_mv, (b + 1) * KB, S.h_ve, S.h_rstd, b + 1)

            def rstd_c(b):
                rstd(c_mv[:, :, 1], c_ve, c_rs, S.c_mv, (b + 1) * KB, S.c_ve, S.c_rstd, b + 1)

            def low_part(e, h):
                n = e * HALVES + h
                pool.wait_ge(S.w_hi, n + 1)
                pool.tensor_tensor(w_lo[:, ds(e * WE + h * HALF, HALF)], w_full[h % 3],
                                   w_hi[:, ds(e * WE + h * HALF, HALF)], ALU.subtract).then_inc(S.w_lo, 1)

            def u_low(b):
                pool.wait_ge(S.u_hi, b + 1)
                pool.tensor_tensor(u_split[:, :, D:], u, u_split[:, :, 0:D], ALU.subtract).then_inc(S.u_lo, 1)

            pool.wait_ge(S.ids_in, 16)
            gather_path(0)
            pool.iota(iota_p[:, :], [[1, P]], base=0, channel_multiplier=0,
                      allow_small_or_imprecise_dtypes=True).then_inc(S.const, 1)
            pool.iota(iota_e[:, :], [[1, E]], base=0, channel_multiplier=0,
                      allow_small_or_imprecise_dtypes=True).then_inc(S.const, 1)
            pool.iota(iota_s[:, :], [[1, SLOT_TILES]], base=0, channel_multiplier=0,
                      allow_small_or_imprecise_dtypes=True).then_inc(S.const, 1)
            pool.iota(token1[:, :, :], [[0, K], [P, TILES]], base=1, channel_multiplier=1,
                      allow_small_or_imprecise_dtypes=True).then_inc(S.const, 1)
            pool.iota(pad_row[:, :], [[0, 1]], base=T + 1, channel_multiplier=1,
                      allow_small_or_imprecise_dtypes=True).then_inc(S.const, 1)
            pool.memset(ones16[:, :], 1.0).then_inc(S.const, 1)
            rstd_x(0)
            rstd_h(0)
            gather_path(1)
            rstd_x(1)
            pool.wait_ge(S.mixw, 2)
            pool.wait_ge(S.net_rows_in, 16)
            mix3 = mixw[0:NBATCH, 2:5].unsqueeze(2).to_broadcast([NBATCH, 3, D])
            for rows in (mlp_g, mlp_be):
                pool.tensor_tensor(rows[0:NBATCH, :, :], rows[0:NBATCH, :, :], mix3, ALU.mult).then_inc(S.net_mixed, 1)
            pool.wait_ge(S.lora_hi, 2)
            for half in (slice(0, LORA // 2), slice(LORA // 2, LORA)):
                pool.tensor_tensor(lora_l[:, half], lora_f[:, half], lora_h[:, half], ALU.subtract).then_inc(S.lora_lo, 1)
            rstd_h(1)
            gather_path(2)

            def block_of(b, first=False, norms=True, paths=True, last=False):
                if first:
                    rstd_x(2)
                    rstd(mlp_mv[0:NBATCH, :, 1], v_ve[0:NBATCH, :], v_rs[0:NBATCH, :], S.v_mv, 3, S.v_ve, S.v_rstd, 1)
                    low_part(0, 0)
                    low_part(0, 1)
                    rstd_h(2)
                    gather_path(3)
                    low_part(0, 2)
                    low_part(0, 3)
                    low_part(0, 4)
                    low_part(0, 5)
                    return
                rstd_c(b - 1)
                if norms:
                    rstd_x(b + 2)
                low_part(b, 0)
                low_part(b, 1)
                u_low(b - 1)
                if norms:
                    rstd_h(b + 2)
                low_part(b, 2)
                low_part(b, 3)
                if paths:
                    gather_path(b + 3)
                if last:
                    rstd_c(b)
                low_part(b, 4)
                if last:
                    u_low(b)
                    pool.wait_ge(S.picked, 1)
                    pool.iota(iota_sn, [[1, SLOT_TILES], [0, NC_]], base=0, channel_multiplier=0,
                              allow_small_or_imprecise_dtypes=True).then_inc(S.tile_iota, 1)
                low_part(b, 5)

            block_of(0, first=True)
            block_of(1)
            with pool.Fori(2, NB - 3) as b:
                block_of(b)
            block_of(NB - 3, paths=False)
            block_of(NB - 2, norms=False, paths=False)
            block_of(NB - 1, norms=False, paths=False, last=True)

            def gather_rows(i, h, v):
                after(pool, (S.rowsT_ps0, S.rowsT_ps1)[v], h)
                n = i + 1
                pool.tensor_copy(gather_now[v], slot_rows[:, ds(i, 1), 0]).then_inc(S.gather_now, 1)
                before_plain(pool, S.gather_now, n)
                pool.indirect_dma_start(rows_in[v], None, u_rows,
                                        bass.IndirectOffsetOnAxis(ap=gather_now[v], axis=0)
                                        ).then_inc((S.rows0, S.rows1)[v], 16)

            def add_rows(i, h, v):
                after(pool, (S.added1, S.added0)[v], 16 * (h + v))
                n = i + 1
                pool.tensor_copy(scatter_now[v], slot_rows[:, ds(i, 1), 1]).then_inc(S.scatter_now, 1)
                pool.wait_ge(S.scatter_now, n)
                before_plain(pool, S.y_gated, n)
                pool.indirect_dma_start(out, bass.IndirectOffsetOnAxis(ap=scatter_now[v], axis=0),
                                        y_gated[v], None, compute_op=ALU.add
                                        ).then_inc((S.added0, S.added1)[v], 16)

            pool.wait_ge(S.u_out, 16 * NB)
            pool.wait_ge(S.slot_rows, 1)
            pool.wait_ge(S.out_in, 32)
            ahead = 5
            for i in range(ahead):
                gather_rows(i, i // 2, i % 2)
            pool.wait_ge(S.slot_rows, 2)
            for i in range(2):
                gather_rows(i + ahead, (i + ahead) // 2, (i + ahead) % 2)
                add_rows(i, 0, i)
            turns = (SLOT_TILES - ahead) // 2
            with pool.Fori(1, turns) as m:
                for v in range(2):
                    gather_rows(m * 2 + v + ahead, m + (v + ahead) // 2, 1 - v)
                    add_rows(m * 2 + v, m, v)
            for i in range(2 * turns, SLOT_TILES):
                if i + ahead < SLOT_TILES:
                    gather_rows(i + ahead, (i + ahead) // 2, (i + ahead) % 2)
                add_rows(i, i // 2, i % 2)

        @block.scalar
        def _(act):
            act.dma_start(aw_sb, a.aw.partition_broadcast(P)).then_inc(S.aw_in, 16)
            act.dma_start(gain_f, a.gains).then_inc(S.gain_in, 16)
            act.dma_start(shift_Z, a.shiftZ.rearrange("(c p) k r -> p c k r", p=P)).then_inc(S.shift_in, 16)
            act.wait_ge(S.aw_max, 1)
            act.activation(aw_e, aw_sb, ACT.Exp, bias=aw_m, accum_out=aw_s).then_inc(S.aw_exp, 1)
            act.dma_start(lora_f, a.lora).then_inc(S.lora_in, 16)
            act.wait_ge(S.lora_in, 16)
            for n, columns in enumerate((LA13, LA2)):
                act.activation(lora_f[:, columns], lora_f[:, columns], ACT.Copy, scale=WSCALE).then_inc(S.lora_scaled, 1)
            act.wait_ge(S.lora_scaled, 2)
            for half in (slice(0, LORA // 2), slice(LORA // 2, LORA)):
                act.copy(lora_h[:, half], lora_f[:, half]).then_inc(S.lora_hi, 1)
            act.wait_ge(S.mlp_h_ps, 1)
            for k in range(3):
                for c in range(DC):
                    act.activation(mlp_h[:, k, c, :], ps_lora[:, (k * DC + c) * 2:(k * DC + c) * 2 + 2], ACT.Silu,
                                   bias=mlp_b1[:, k, c:c + 1]).then_inc(S.mlp_h, 1)

            def high_part(e, h):
                n = e * HALVES + h
                act.wait_ge(S.w_sum, n + 1)
                act.copy(w_hi[:, ds(e * WE + h * HALF, HALF)], w_full[h % 3]).then_inc(S.w_hi, 1)

            def copy_T(b):
                act.wait_ge(S.xT_ps, b + 1)
                after(act, S.prod_s, b)
                act.copy(xhT, ps_xT[:, :]).then_inc(S.xhT, 1)
                act.wait_ge(S.hT_ps, b + 1)
                after(act, S.prod_h, b)
                act.copy(hhT, ps_hT[:, :]).then_inc(S.hhT, 1)

            def hidden(b):
                act.wait_ge(S.l1_ps, b + 1)
                after(act, S.l2_ps, b)
                for c in range(DC):
                    act.activation(zT[:, c, :], ps_l1[:, c * BT:(c + 1) * BT], ACT.Silu,
                                   bias=bias_blk[:, ds(b * DC + c, 1)]).then_inc(S.zT, 1)

            def u_high(b):
                act.wait_ge(S.u, (b + 1) * KB)
                after(act, S.u_out, 16 * b)
                act.copy(u_split[:, :, 0:D], u).then_inc(S.u_hi, 1)

            def copy_uT(b):
                act.wait_ge(S.uT_ps, b + 1)
                after(act, S.lg_ps, b)
                act.copy(uT_sb, ps_u[:, :]).then_inc(S.uT, 1)

            def networks_out():
                act.wait_ge(S.vT_ps, 1)
                act.copy(mlp_vT, ps_l2[:, D:D + 12].rearrange("p (k b) -> p k b", b=NBATCH)).then_inc(S.vT, 1)
                act.wait_ge(S.bias_ps, 1)
                for bat in range(NBATCH):
                    for c in range(DC):
                        n = NB // NBATCH
                        dst = bias_blk.rearrange("p (b c) -> p b c", c=DC)[:, bat * n:(bat + 1) * n, c]
                        src = ps_u[:, c * NBATCH + bat:c * NBATCH + bat + 1].to_broadcast([P, n])
                        act.activation(dst, src, ACT.Identity, bias=int_b1[:, c:c + 1]).then_inc(S.bias_blk, 1)

            copy_T(0)

            def block_of(b, first=False, last=False):
                high_part(b, 0)
                if not last:
                    copy_T(b + 1)
                high_part(b, 1)
                if not first:
                    u_high(b - 1)
                if first:
                    networks_out()
                    act.wait_ge(S.bias_blk, DC * NBATCH)
                hidden(b)
                high_part(b, 2)
                if not first:
                    copy_uT(b - 1)
                for h in range(3, 5):
                    high_part(b, h)
                if last:
                    u_high(b)
                    copy_uT(b)
                high_part(b, 5)

            block_of(0, first=True)
            block_of(1)
            with act.Fori(2, NB - 1) as b:
                block_of(b)
            block_of(NB - 1, last=True)

            act.wait_ge(S.gap, 1)
            act.activation(e2, gap, ACT.Exp).then_inc(S.e2, 1)

            def copy_rowsT(i, v):
                act.wait_ge((S.rowsT_ps0, S.rowsT_ps1)[v], i[1] + 1)
                after(act, S.h3_ps, i[0] - 1)
                act.copy(rowsT[v], ps_rowsT[v]).then_inc(S.rowsT, 1)

            def silu_of(i, v):
                act.wait_ge(S.h1, i[0] + 1)
                act.activation(silu_sb[v], h1_sb[v], ACT.Silu).then_inc(S.silu, 1)

            def gT_high(i, v):
                act.wait_ge(S.gT_ps, i[0] + 1)
                after(act, S.y_ps, i[0] - 1)
                act.copy(gT_hi[v], ps_gT[:, :]).then_inc(S.gT_hi, 1)

            def gated(i, v):
                act.wait_ge(S.y, i[0] + 1)
                if isinstance(i[0], int) and i[0] == 0:
                    act.wait_ge(S.slot_gate, 1)
                after(act, (S.added0, S.added1)[v], 16 * i[1])
                act.activation(y_gated[v], y_sb[v], ACT.Copy, scale=slot_gate[:, ds(i[0], 1)]).then_inc(S.y_gated, 1)

            def step(i, h, v, peeled=False):
                n = SLOT_TILES
                if not peeled or i < n:
                    silu_of((i, h), v)
                if not peeled or i + 1 < n:
                    copy_rowsT((i + 1, h + v), 1 - v)
                if not peeled or 1 <= i <= n:
                    gT_high((i - 1, h - 1 + v), 1 - v)
                if not peeled or 2 <= i:
                    gated((i - 2, h - 1), v)

            copy_rowsT((0, 0), 0)
            for i in range(4):
                step(i, i // 2, i % 2, peeled=True)
            turns = (SLOT_TILES - 5) // 2
            with act.Fori(2, 2 + turns) as m:
                for v in range(2):
                    step(m * 2 + v, m, v)
            for i in range(4 + 2 * turns, SLOT_TILES + 2):
                step(i, i // 2, i % 2, peeled=True)

        @block.vector
        def _(dve):
            mul, add, sub = ALU.mult, ALU.add, ALU.subtract

            def stats_x(b):
                for k in range(KB):
                    dve.bn_stats(x_st[:, 6 * k:6 * k + 6], x_tok[:, ds((b * KB + k) * D, D)]).then_inc(S.x_st, 1)

            def moments_x(b):
                before_plain(dve, S.x_st, (b + 1) * KB)
                for k in range(KB):
                    dve.bn_aggr(x_mv[:, k, :], x_st[:, 6 * k:6 * k + 6]).then_inc(S.x_mv, 1)

            def norm_x(b):
                stats_x(b)
                moments_x(b)

            def xhat(b):
                dve.wait_ge(S.x_rstd, b + 1)
                after(dve, S.xT_ps, b)
                for k in range(KB):
                    dve.tensor_scalar(xh[:, k, :], x_tok[:, ds((b * KB + k) * D, D)], x_mv[:, k, 0:1],
                                      x_rs[:, k:k + 1], sub, mul).then_inc(S.xhat, 1)

            def scale_h(b):
                dve.wait_ge(S.xhat, (b + 1) * KB)
                dve.wait_ge(S.path_in, (b + 1) * KB * 16)
                after(dve, S.hT_ps, b)
                dve.tensor_tensor(hh, xh, pw_rows[:, :, 0:D], mul).then_inc(S.h_scaled, 1)
                dve.wait_ge(S.h_scaled, b + 1)
                dve.tensor_tensor(hh, hh, pw_rows[:, :, D:], add).then_inc(S.h_pre, 1)
                dve.wait_ge(S.h_pre, b + 1)
                for k in range(KB):
                    dve.bn_stats(h_st[:, 6 * k:6 * k + 6], hh[:, k, :]).then_inc(S.h_st, 1)

            def moments_h(b):
                before_plain(dve, S.h_st, (b + 1) * KB)
                for k in range(KB):
                    dve.bn_aggr(h_mv[:, k, :], h_st[:, 6 * k:6 * k + 6]).then_inc(S.h_mv, 1)

            def norm_h(b):
                xhat(b)
                scale_h(b)
                moments_h(b)

            def finish_h(b):
                dve.wait_ge(S.h_rstd, b + 1)
                for k in range(KB):
                    dve.tensor_scalar(hh[:, k, :], hh[:, k, :], h_mv[:, k, 0:1], h_rs[:, k:k + 1],
                                      sub, mul).then_inc(S.hhat, 1)

            def products_x(b):
                dve.wait_ge(S.xhT, b + 1)
                dve.wait_ge(S.gt_ps, b + 1)
                after(dve, S.l1_ps, b)
                dve.tensor_tensor(prod_t, xhT, ps_g0[:, :], mul).then_inc(S.prod_t, 1)
                dve.wait_ge(S.gs_ps, b + 1)
                dve.tensor_tensor(prod_s, xhT, ps_g1[:, :], mul).then_inc(S.prod_s, 1)

            def products_h(b):
                dve.wait_ge(S.hhT, b + 1)
                dve.wait_ge(S.gh_ps, b + 1)
                dve.tensor_tensor(prod_h, hhT, ps_g0[:, :], mul).then_inc(S.prod_h, 1)

            def second_layer(b):
                dve.wait_ge(S.l2_ps, b + 1)
                dve.tensor_tensor(c_sb, ps_l2[:, :].rearrange("p (k d) -> p k d", k=KB),
                                  norm_rows[:, 0:1, :].to_broadcast([P, KB, D]), add).then_inc(S.c, 1)

            def stats_c(b):
                dve.wait_ge(S.c, b + 1)
                for k in range(KB):
                    dve.bn_stats(c_st[:, 6 * k:6 * k + 6], c_sb[:, k, :]).then_inc(S.c_st, 1)

            def moments_c(b):
                before_plain(dve, S.c_st, (b + 1) * KB)
                for k in range(KB):
                    dve.bn_aggr(c_mv[:, k, :], c_st[:, 6 * k:6 * k + 6]).then_inc(S.c_mv, 1)

            def center_c(b):
                dve.wait_ge(S.c_mv, (b + 1) * KB)
                for k in range(KB):
                    dve.scalar_tensor_tensor(c_sb[:, k, :], c_sb[:, k, :], c_mv[:, k, 0:1], norm_rows[:, 1, :],
                                             sub, mul).then_inc(S.chat, 1)

            def finish_u(b):
                dve.wait_ge(S.chat, (b + 1) * KB)
                dve.wait_ge(S.c_rstd, b + 1)
                after(dve, S.uT_ps, b)
                after(dve, S.u_lo, b)
                for k in range(KB):
                    dve.scalar_tensor_tensor(u[:, k, :], c_sb[:, k, :], c_rs[:, k:k + 1], norm_rows[:, 2, :],
                                             mul, add).then_inc(S.u, 1)

            def keep_logits(b):
                dve.wait_ge(S.lg_ps, b + 1)
                dve.tensor_copy(lg_sb, ps_u[:, 0:KB * E]).then_inc(S.lg, 1)

            def sort_logits(b):
                before_plain(dve, S.lg, b + 1)
                for k in range(KB):
                    dve.max(top_now[:, k * 8:(k + 1) * 8], lg_sb[:, k * E:(k + 1) * E]).then_inc(S.top, 1)

            def find_experts(b):
                before_plain(dve, S.top, (b + 1) * KB)
                for k in range(KB):
                    dve.max_index(top_e_now[:, k * 8:(k + 1) * 8], top_now[:, k * 8:(k + 1) * 8],
                                  lg_sb[:, k * E:(k + 1) * E]).then_inc(S.top_i, 1)

            def keep_top(b):
                dve.wait_ge(S.top_i, (b + 1) * KB)
                dve.tensor_copy(top[:, ds(b * KB * 8, KB * 8)], top_now).then_inc(S.top_e, 1)
                dve.tensor_copy(top_e[:, ds(b * KB * 8, KB * 8)], top_e_now).then_inc(S.top_e, 1)

            def merge(e, h):
                n = e * HALVES + h
                dve.wait_ge(S.lora_ps, n + 1)
                dve.wait_ge((S.w1s_in, S.w3s_in, S.w2s_in)[h // 2], (e + 1) * 16)
                after(dve, S.w_lo, n - 2)
                dve.scalar_tensor_tensor(w_full[h % 3], w_stage[h // 2][:, (h % 2) * HALF:(h % 2 + 1) * HALF],
                                         WSCALE, ps_lora[:, :], mul, add).then_inc(S.w_sum, 1)

            def split_table(kinds, n):
                dve.wait_ge(S.gain_s, 3 + n)
                dve.tensor_copy(gain_tab[:, kinds, :], gain_f[:, kinds, :]).then_inc(S.tab, 1)
                dve.wait_ge(S.tab, 5 * n + 1)
                dve.tensor_tensor(gain_r[:, kinds, :], gain_f[:, kinds, :], gain_tab[:, kinds, :], sub).then_inc(S.tab, 1)
                dve.wait_ge(S.tab, 5 * n + 2)
                dve.tensor_copy(gain_tab[32:64, kinds, :], gain_r[32:64, kinds, :]).then_inc(S.tab, 1)
                dve.tensor_copy(gain_h[:, kinds, :], gain_r[:, kinds, :]).then_inc(S.tab, 1)
                dve.wait_ge(S.tab, 5 * n + 4)
                dve.tensor_tensor(gain_tab[64:96, kinds, :], gain_r[64:96, kinds, :], gain_h[64:96, kinds, :], sub).then_inc(S.tab, 1)

            v = mlp_v[0:NBATCH, :, :]

            def networks_add():
                dve.wait_ge(S.mlp_o_ps, 1)
                dve.wait_ge(S.net_rows_in, 16)
                dve.tensor_tensor(v[:, 0:2, :], ps_u[0:NBATCH, :].rearrange("p (k n) -> p k n", k=2),
                                  mlp_b2[0:NBATCH, 0:2, :], add).then_inc(S.v, 1)
                dve.tensor_tensor(v[:, 2, :], ps_l2[0:NBATCH, 0:D], mlp_b2[0:NBATCH, 2, :], add).then_inc(S.v, 1)
                dve.wait_ge(S.v, 2)
                for k in range(3):
                    dve.bn_stats(mlp_st[0:NBATCH, k, :], v[:, k, :]).then_inc(S.v_st, 1)
                dve.wait_ge(S.v_st, 3)
                for k in range(3):
                    dve.bn_aggr(mlp_mv[0:NBATCH, k, :], mlp_st[0:NBATCH, k, :]).then_inc(S.v_mv, 1)

            def networks_norm():
                dve.wait_ge(S.v_mv, 3)
                dve.wait_ge(S.net_mixed, 2)
                for k in range(3):
                    dve.scalar_tensor_tensor(v[:, k, :], v[:, k, :], mlp_mv[0:NBATCH, k, 0:1], mlp_g[0:NBATCH, k, :],
                                             sub, mul).then_inc(S.v, 1)
                dve.wait_ge(S.v, 5)
                dve.wait_ge(S.v_rstd, 1)
                for k in range(3):
                    dve.scalar_tensor_tensor(v[:, k, :], v[:, k, :], v_rs[0:NBATCH, k:k + 1], mlp_be[0:NBATCH, k, :],
                                             mul, add).then_inc(S.v, 1)

            dve.wait_ge(S.aw_in, 16)
            dve.tensor_reduce(aw_m, aw_sb, AX_X, ALU.max, negate=True).then_inc(S.aw_max, 1)
            dve.wait_ge(S.x_first, 16)
            norm_x(0)
            dve.wait_ge(S.const, 4)
            dve.tensor_copy(ident16[:, :], ident[:, :]).then_inc(S.const_d, 1)
            dve.tensor_copy(before[:, :], setup_f).then_inc(S.const_d, 1)
            dve.tensor_scalar(row16[:, 1:2], row16[:, 0:1], 15, None, ALU.bitwise_and).then_inc(S.row16, 1)
            dve.wait_ge(S.row16, 1)
            dve.tensor_copy(row16_f, row16[:, 1:2]).then_inc(S.row16, 1)
            dve.wait_ge(S.aw_exp, 1)
            dve.reciprocal(aw_r, aw_s).then_inc(S.mixw, 1)
            dve.wait_ge(S.mixw, 1)
            dve.tensor_scalar(mixw, aw_e, aw_r, None, mul).then_inc(S.mixw, 1)
            dve.wait_ge(S.mixw, 2)
            dve.wait_ge(S.gain_in, 16)
            for k, w in enumerate((0, 1, 5)):
                dve.tensor_scalar(gain_f[:, k, :], gain_f[:, k, :], mixw[0:ROWS, w:w + 1], None, mul).then_inc(S.gain_s, 1)
            dve.wait_ge(S.shift_in, 16)
            for k, w in enumerate((0, 1, 5)):
                dve.tensor_scalar(shift_Z[:, :, k, :], shift_Z[:, :, k, :], mixw[:, w:w + 1], None, mul).then_inc(S.shift_z, 1)
            dve.wait_ge(S.onehot_ids_in, 16)
            dve.wait_ge(S.row16, 2)
            dve.tensor_scalar(onehot, ids_i[0:ROWS, :], row16_f[0:ROWS, :], None, ALU.is_equal).then_inc(S.onehot, 1)
            split_table(slice(0, NKIND), 0)
            norm_h(0)
            norm_x(1)
            finish_h(0)
            dve.wait_ge(S.shift_ps, 1)
            dve.tensor_copy(gain_f[:, 3, :], ps_hT[0:ROWS, 0:D]).then_inc(S.gain_s, 1)
            split_table(slice(NKIND, NKIND + 1), 1)
            dve.wait_ge(S.w1x_in, 16)
            dve.tensor_scalar(wx, int_w1x[:, 0:DC, :], mixw[:, 2:3], None, mul).then_inc(S.wx, 1)
            for n in (3, 4):
                dve.wait_ge(S.wx, n - 2)
                dve.scalar_tensor_tensor(wx, int_w1x[:, (n - 2) * DC:(n - 1) * DC, :], mixw[:, n:n + 1], wx, mul, add).then_inc(S.wx, 1)
            products_x(0)
            products_h(0)
            norm_h(1)
            finish_h(1)

            early, late = slice(0, EARLY), slice(EARLY, TILES)
            by_part = [k * TILES + j for tiles in (early, late) for k in range(K) for j in range(tiles.start, tiles.stop)]
            top3 = top[:, :].rearrange("p (j n) -> p j n", n=8)
            tope3 = top_e[:, :].rearrange("p (j n) -> p j n", n=8)
            counts = ps_counts[:, 0:(TILES + 1) * E].rearrange("p (j e) -> p j e", e=E)

            def choose(tiles, blocks, n):
                j = tiles.stop - tiles.start
                dve.wait_ge(S.top_e, 2 * blocks)
                for k in range(K):
                    dve.tensor_tensor(chosen[:, k, tiles, :], iota_e[:, :].unsqueeze(1).to_broadcast([P, j, E]),
                                      tope3[:, tiles, k:k + 1].to_broadcast([P, j, E]), ALU.is_equal).then_inc(S.chosen, 1)
                dve.wait_ge(S.chosen, 2 * n)
                dve.tensor_tensor(picked[:, tiles, :], chosen[:, 0, tiles, :], chosen[:, 1, tiles, :], add).then_inc(S.picked, 1)

            def positions(tiles, n):
                done = 8 * (n - 1)
                dve.wait_ge(S.place_ps, n)
                for k in range(K):
                    dve.tensor_tensor(place[:, k, tiles, :], chosen[:, k, tiles, :], counts[:, tiles, :], mul).then_inc(S.place, 1)
                dve.wait_ge(S.place, done + 2)
                dve.tensor_reduce(pos_f[:, :, tiles], place[:, :, tiles, :], AX_X, add).then_inc(S.place, 1)
                dve.wait_ge(S.place, done + 3)
                dve.tensor_copy(pos_i[:, :, tiles], pos_f[:, :, tiles]).then_inc(S.place, 1)
                dve.wait_ge(S.place, done + 4)
                dve.tensor_scalar(pos_tile[:, :, tiles], pos_i[:, :, tiles], 7, None, ALU.logical_shift_right).then_inc(S.place, 1)
                dve.tensor_scalar(pos_col[:, :, tiles], pos_i[:, :, tiles], P - 1, None, ALU.bitwise_and).then_inc(S.place, 1)
                dve.wait_ge(S.place, done + 6)
                for dst, src in ((pos_tile_f, pos_tile), (pos_col_f, pos_col)):
                    dve.tensor_copy(dst.rearrange("p (k j) -> p k j", k=K)[:, :, tiles], src[:, :, tiles]).then_inc(S.place, 1)
                dve.wait_ge(S.place, done + 8)

            def columns(first, end):
                for n in by_part[first:end]:
                    dve.tensor_scalar(col_hot[:, n, :], iota_p[:, :], pos_col_f[:, n:n + 1], None,
                                      ALU.is_equal).then_inc(S.col_hot, 1)

            def block_of(b, first=False, norms=True):
                if first:
                    dve.wait_ge(S.x_third, 16)
                    norm_x(b + 2)
                    networks_add()
                    merge(b, 0)
                    networks_norm()
                    merge(b, 1)
                    norm_h(b + 2)
                    products_x(b + 1)
                    merge(b, 2)
                    products_h(b + 1)
                    merge(b, 3)
                    finish_h(b + 2)
                    merge(b, 4)
                    merge(b, 5)
                    return
                second_layer(b - 1)
                if norms:
                    stats_x(b + 2)
                stats_c(b - 1)
                merge(b, 0)
                moments_c(b - 1)
                if norms:
                    moments_x(b + 2)
                center_c(b - 1)
                merge(b, 1)
                finish_u(b - 1)
                if norms:
                    xhat(b + 2)
                if norms:
                    scale_h(b + 2)
                merge(b, 2)
                if norms:
                    moments_h(b + 2)
                products_x(b + 1)
                merge(b, 3)
                products_h(b + 1)
                merge(b, 4)
                keep_logits(b - 1)
                if norms:
                    finish_h(b + 2)
                sort_logits(b - 1)
                merge(b, 5)
                find_experts(b - 1)
                keep_top(b - 1)

            block_of(0, first=True)
            dve.wait_ge(S.x_rest, 16)
            dve.wait_ge(S.norm_in, 16)
            block_of(1)
            with dve.Fori(2, NB - 2) as b:
                block_of(b)
            block_of(NB - 2, norms=False)
            b = NB - 1
            second_layer(b - 1)
            stats_c(b - 1)
            merge(b, 0)
            moments_c(b - 1)
            dve.wait_ge(S.const, 10)
            dve.memset(picked[:, TILES, :], 0.0).then_inc(S.picked, 1)
            center_c(b - 1)
            merge(b, 1)
            finish_u(b - 1)
            choose(early, b - 1, 1)
            merge(b, 2)
            merge(b, 3)
            positions(early, 1)
            second_layer(b)
            stats_c(b)
            moments_c(b)
            merge(b, 4)
            keep_logits(b - 1)
            columns(0, 1)
            sort_logits(b - 1)
            center_c(b)
            find_experts(b - 1)
            finish_u(b)
            keep_top(b - 1)
            merge(b, 5)
            columns(1, 17)
            keep_logits(b)
            columns(17, 18)
            sort_logits(b)
            columns(18, 19)
            find_experts(b)
            columns(19, 20)
            keep_top(b)
            columns(20, 21)
            choose(late, NB, 2)
            dve.wait_ge(S.w_lo, E * HALVES)
            dve.wait_ge(S.u_out, 16 * NB)
            dve.tensor_tensor(gap, top3[:, :, 1], top3[:, :, 0], sub).then_inc(S.gap, 1)
            columns(21, 24)
            dve.wait_ge(S.place_ps, 2)
            dve.tensor_scalar(tiles_i, ps_counts[:, TILES * E:(TILES + 1) * E], float(P - 1), None, add).then_inc(S.tiles, 1)
            positions(late, 2)
            dve.wait_ge(S.tiles, 1)
            dve.tensor_scalar(tiles_i, tiles_i, 7, None, ALU.logical_shift_right).then_inc(S.tiles, 1)
            columns(24, 25)
            dve.wait_ge(S.tiles, 2)
            dve.tensor_tensor(tri_f, before8[:, :, :], tiles_i.unsqueeze(1).to_broadcast([P, E, E]), mul).then_inc(S.tiles, 1)
            columns(25, 26)
            dve.wait_ge(S.tiles, 3)
            dve.tensor_reduce(first_tile, tri_f, AX_X, add).then_inc(S.tiles, 1)
            dve.wait_ge(S.e2, 1)
            dve.tensor_scalar(den, e2, 1.0, None, add).then_inc(S.gate, 1)
            dve.wait_ge(S.tiles, 4)
            dve.tensor_tensor(start_of, chosen.rearrange("p k j e -> p (k j) e"),
                              first_tile.unsqueeze(1).to_broadcast([P, NC_, E]), mul).then_inc(S.start, 1)
            dve.wait_ge(S.gate, 1)
            dve.reciprocal(gate[:, 0, :], den).then_inc(S.gate, 1)
            dve.wait_ge(S.start, 1)
            dve.tensor_reduce(start_f.rearrange("p (n o) -> p n o", o=1), start_of, AX_X, add).then_inc(S.start, 1)
            dve.wait_ge(S.gate, 2)
            dve.tensor_tensor(gate[:, 1, :], gate[:, 0, :], e2, mul).then_inc(S.gate, 1)
            dve.wait_ge(S.start, 2)
            dve.tensor_tensor(slot_tile_f, start_f, pos_tile_f, add).then_inc(S.start, 1)
            dve.wait_ge(S.gate, 3)
            dve.tensor_copy(gate_h, gate).then_inc(S.gate, 1)
            columns(26, NC_)
            dve.wait_ge(S.start, 3)
            dve.wait_ge(S.tile_iota, 1)
            for k in range(K):
                dve.tensor_tensor(in_tile[:, :, k * TILES:(k + 1) * TILES], iota_sn[:, :, k * TILES:(k + 1) * TILES],
                                  slot_tile_f[:, k * TILES:(k + 1) * TILES].unsqueeze(1).to_broadcast([P, SLOT_TILES, TILES]),
                                  ALU.is_equal).then_inc(S.in_tile, 1)
            for k in range(K):
                dve.wait_ge(S.in_tile, k + 1)
                dve.tensor_tensor(tile_val[:, 0, :, k * TILES:(k + 1) * TILES], in_tile[:, :, k * TILES:(k + 1) * TILES],
                                  token1[:, k, :].unsqueeze(1).to_broadcast([P, SLOT_TILES, TILES]), mul).then_inc(S.token_val, 1)
            dve.wait_ge(S.gate, 4)
            dve.tensor_tensor(gate_l, gate, gate_h, sub).then_inc(S.gate, 1)
            dve.tensor_tensor(started, first_tile.unsqueeze(1).to_broadcast([P, SLOT_TILES, E]),
                              iota_s[:, :].unsqueeze(2).to_broadcast([P, SLOT_TILES, E]), ALU.is_le).then_inc(S.started, 1)
            dve.wait_ge(S.slots_ps, 1)
            dve.tensor_scalar(slot_rows[:, :, 0], ps_rows[:, 0:SLOT_TILES], -1.0, 0.0, add, ALU.max).then_inc(S.slot_rows, 1)
            dve.tensor_scalar(empty, ps_rows[:, 0:SLOT_TILES], 0.0, pad_row[:, 0:1], ALU.is_equal, mul).then_inc(S.empty, 1)
            dve.wait_ge(S.started, 1)
            dve.tensor_reduce(started_n, started, AX_X, add).then_inc(S.started, 1)
            dve.wait_ge(S.gate, 5)
            for n, val in ((1, gate_h), (2, gate_l)):
                dve.tensor_tensor(tile_val[:, n, :, :], in_tile, val.rearrange("p k j -> p (k j)").unsqueeze(1)
                                  .to_broadcast([P, SLOT_TILES, NC_]), mul).then_inc(S.gate_val, 1)
            dve.wait_ge(S.started, 2)
            dve.tensor_scalar(tile_expert, started_n, -1.0, None, add).then_inc(S.tile_expert, 1)
            dve.wait_ge(S.empty, 1)
            dve.scalar_tensor_tensor(slot_rows[:, :, 1], ps_rows[:, 0:SLOT_TILES], -1.0, empty, add, add).then_inc(S.slot_rows, 1)
            dve.wait_ge(S.gates_ps, 1)
            dve.tensor_copy(gate_v, ps_gates[:, 0:2 * SLOT_TILES].rearrange("p (v s) -> p v s", v=2)).then_inc(S.gate_v, 1)
            dve.wait_ge(S.gate_v, 1)
            dve.tensor_tensor(slot_gate, gate_v[:, 0, :], gate_v[:, 1, :], add).then_inc(S.slot_gate, 1)

            inv = 1.0 / WSCALE

            def h1_of(i, v, at):
                dve.wait_ge(S.h1_ps, i + 1)
                after(dve, S.silu, i - 1)
                dve.scalar_tensor_tensor(h1_sb[v], ps_h1[v][:, :], inv, biases[:, ds(at, H)], mul, add).then_inc(S.h1, 1)

            def g_of(i, v, at):
                dve.wait_ge(S.h3_ps, i + 1)
                dve.scalar_tensor_tensor(h3_sb[v], ps_h3[v][:, :], inv, biases[:, ds(at + H, H)], mul, add).then_inc(S.h3, 1)
                dve.wait_ge(S.h3, i + 1)
                dve.wait_ge(S.silu, i + 1)
                after(dve, S.gT_ps, i - 1)
                dve.tensor_tensor(g_sb[v], h3_sb[v], silu_sb[v], mul).then_inc(S.g, 1)

            def gT_low(i, v):
                dve.wait_ge(S.gT_hi, i + 1)
                dve.tensor_tensor(gT_lo[v], ps_gT[:, :], gT_hi[v], sub).then_inc(S.gT_lo, 1)

            def y_of(i, v, at):
                dve.wait_ge(S.y_ps, i + 1)
                after(dve, S.y_gated, i - 1)
                dve.scalar_tensor_tensor(y_sb[v], ps_y[:, 0:D], inv, biases[:, ds(at + 2 * H, D)], mul, add).then_inc(S.y, 1)

            def step(i, v, expert, expert2, peeled=False):
                n = SLOT_TILES
                if not peeled or i < n:
                    h1_of(i, v, expert * BE)
                    g_of(i, v, expert * BE)
                if not peeled or 1 <= i <= n:
                    gT_low(i - 1, 1 - v)
                if not peeled or 2 <= i:
                    y_of(i - 2, v, expert2 * BE)

            def pair(i, peeled=False):
                e = experts_of(mybir.EngineType.DVE, i, 2)
                for v in range(2):
                    if not peeled or i + v < SLOT_TILES + 2:
                        step(i + v, v, e[2 + v], e[v], peeled)

            dve.wait_ge(S.tile_expert, 1)
            dve.wait_ge(S.biases_in, 32)
            pair(0, peeled=True)
            pair(2, peeled=True)
            turns = (SLOT_TILES - 5) // 2
            with dve.Fori(2, 2 + turns) as m:
                pair(m * 2)
            for i in range(4 + 2 * turns, SLOT_TILES + 2, 2):
                pair(i, peeled=True)

        @block.tensor
        def _(pe):
            def transpose_T(b):
                for src, ready, freed, dst, done in ((xh, S.xhat, S.xhT, ps_xT, S.xT_ps),
                                                     (hh, S.hhat, S.hhT, ps_hT, S.hT_ps)):
                    pe.wait_ge(ready, (b + 1) * KB)
                    after(pe, freed, b)
                    for k in range(KB):
                        for c in range(DC):
                            last = pe.transpose(dst[:, c * BT + k * P:c * BT + (k + 1) * P],
                                                src[:, k, c * P:(c + 1) * P], ident[:, :])
                    last.then_inc(done, 1)

            def gains(b, kind, dst, freed, n, done):
                after(pe, freed, n)
                for c in range(DC):
                    last = pe.matmul(dst[:, c * BT:(c + 1) * BT], gain_tab[:, kind, c * P:(c + 1) * P],
                                     onehot[:, ds(b * BT, BT)], start=True, stop=True)
                last.then_inc(done, 1)

            def lora(e, h):
                n = e * HALVES + h
                if isinstance(e, int) and e == 0:
                    pe.wait_ge(S.lora_k0_in, 16 * 7)
                elif h in (0, 4):
                    pe.wait_ge(S.lora_k13_in if h == 0 else S.lora_k2_in, 16 * e)
                after(pe, S.w_sum, n)
                if h < 4:
                    a0, b0 = (h // 2) * D + (h % 2) * P, LB.start + (h // 2) * H
                    last = pe.matmul(ps_lora[:, :], lora_k[0:3 * R, a0:a0 + P], lora_k[0:3 * R, b0:b0 + H],
                                     start=True, stop=True)
                else:
                    for c in range(2):
                        a0, b0 = LA2.start + ((h % 2) * 2 + c) * P, LB.start + 2 * H
                        last = pe.matmul(ps_lora[:, c * D:(c + 1) * D], lora_k[0:3 * R, a0:a0 + P],
                                         lora_k[0:3 * R, b0:b0 + D], start=True, stop=True)
                last.then_inc(S.lora_ps, 1)

            def layer1(b, c, between):
                hid = slice(c * P, (c + 1) * P)
                o = ps_l1[:, c * BT:(c + 1) * BT]
                if c == 0:
                    after(pe, S.zT, b * DC)
                for n in range(DC):
                    pe.matmul(o, wx[:, n, hid], xT_flat[:, ds((b * DC + n) * BT, BT)], start=(n == 0), stop=False)
                pe.matmul(o, gain_tab[:, 3, hid], onehot[:, ds(b * BT, BT)], start=False, stop=False)
                for prod, ready, w in ((prod_t, S.prod_t, 2), (prod_s, S.prod_s, 4), (prod_h, S.prod_h, 0)):
                    if c == 0:
                        pe.wait_ge(ready, b + 1)
                    for n in range(DC):
                        last = pe.matmul(o, int_w1[:, w + n, hid], prod[:, n * BT:(n + 1) * BT],
                                         start=False, stop=(w == 0 and n == DC - 1))
                    if w == 2:
                        between()
                if c == DC - 1:
                    last.then_inc(S.l1_ps, 1)

            def layer2(b):
                pe.wait_ge(S.zT, (b + 1) * DC)
                after(pe, S.c, b)
                for k in range(KB):
                    for c in range(DC):
                        last = pe.matmul(ps_l2[:, k * D:(k + 1) * D], zT[:, c, k * P:(k + 1) * P], int_w2[:, c, :],
                                         start=(c == 0), stop=(c == DC - 1))
                last.then_inc(S.l2_ps, 1)

            def transpose_u(b):
                pe.wait_ge(S.u, (b + 1) * KB)
                after(pe, S.lg, b)
                for n in range(KB * DC):
                    last = pe.transpose(ps_u[:, n * P:(n + 1) * P], u[:, n // DC, (n % DC) * P:(n % DC + 1) * P],
                                        ident[:, :])
                last.then_inc(S.uT_ps, 1)

            def logits(b):
                pe.wait_ge(S.uT, b + 1)
                for k in range(KB):
                    for c in range(DC):
                        last = pe.matmul(ps_u[:, k * E:(k + 1) * E], uT_sb[:, (k * DC + c) * P:(k * DC + c + 1) * P],
                                         wgT[:, c, :], start=(c == 0), stop=(c == DC - 1))
                last.then_inc(S.lg_ps, 1)

            def gains_ts(b):
                gains(b, 1, ps_g0, S.prod_h, b, S.gt_ps)
                gains(b, 2, ps_g1, S.prod_s, b, S.gs_ps)

            def gains_h(b):
                gains(b, 0, ps_g0, S.prod_t, b + 1, S.gh_ps)

            def networks_layer2():
                for k in range(3):
                    o = ps_u[0:NBATCH, k * D:(k + 1) * D] if k < 2 else ps_l2[0:NBATCH, 0:D]
                    for c in range(DC):
                        last = pe.matmul(o, mlp_h[:, k, c, :], mlp_w2[:, k, c, :], start=(c == 0), stop=(c == DC - 1))
                last.then_inc(S.mlp_o_ps, 1)

            pe.wait_ge(S.w1_in, 32)
            pe.wait_ge(S.shift_z, 3)
            for n, (k, c) in enumerate((k, c) for k in range(NKIND) for c in range(DC)):
                last = pe.matmul(ps_hT[0:ROWS, 0:D], shift_Z[:, c, k, :], int_w1[:, k * DC + c, :],
                                 start=(n == 0), stop=(n == 2 * NKIND - 1))
            last.then_inc(S.shift_ps, 1)
            pe.wait_ge(S.net_in, 16)
            for k, n in enumerate((128, 64, 32)):
                for c in range(DC):
                    last = pe.matmul(ps_lora[:, (k * DC + c) * 2:(k * DC + c) * 2 + 2], mlp_w1[0:n, k, c * P:(c + 1) * P],
                                     mlp_s[0:n, k, :], start=True, stop=True)
            last.then_inc(S.mlp_h_ps, 1)
            pe.wait_ge(S.gain_s, 4)
            pe.wait_ge(S.const, 1)
            transpose_T(0)
            pe.wait_ge(S.tab, 10)
            pe.wait_ge(S.onehot, 1)
            gains_ts(0)
            gains_h(0)
            pe.wait_ge(S.xT_first, 16)
            pe.wait_ge(S.wx, 3)

            def networks_bias():
                pe.wait_ge(S.v, 8)
                for n in range(3 * DC):
                    last = pe.transpose(ps_l2[:, D + 2 * n:D + 2 * n + 2], mlp_v[0:NBATCH, n // DC, (n % DC) * P:(n % DC + 1) * P],
                                        ident[0:NBATCH, 0:NBATCH])
                last.then_inc(S.vT_ps, 1)
                pe.wait_ge(S.vT, 1)
                for c in range(DC):
                    for n in range(3 * DC):
                        last = pe.matmul(ps_u[:, c * NBATCH:(c + 1) * NBATCH], int_w1x[:, n, c * P:(c + 1) * P],
                                         mlp_vT[:, n, :], start=(n == 0), stop=(n == 3 * DC - 1))
                last.then_inc(S.bias_ps, 1)
                pe.wait_ge(S.int_w2_in, 16)

            def count_before(first, end, n):
                o = ps_counts[:, 0:(TILES + 1) * E].rearrange("p (j e) -> p j e", e=E)
                pe.wait_ge(S.picked, n + 1)
                for j in range(first, end):
                    pe.matmul(o[:, j + 1:, :], ones16[:, :], picked[:, j:j + 1, :].to_broadcast([P, TILES - j, E]),
                              start=(j == 0), stop=False, skip_group_check=True)
                last = pe.matmul(o[:, first:end, :], before[:, :], picked[:, first:end, :], start=False, stop=True,
                                 skip_group_check=True)
                last.then_inc(S.place_ps, 1)

            def block_of(b, first=False, last=False):
                layer1(b, 0, (lambda: None) if first else (lambda: lora(b, 0)))
                if not first:
                    lora(b, 1)
                if not last:
                    transpose_T(b + 1)
                    gains_ts(b + 1)
                if first:
                    pe.wait_ge(S.mlp_h, 6)
                    networks_layer2()
                    lora(b, 0)
                layer1(b, 1, lambda: lora(b, 1 if first else 2))
                if first:
                    networks_bias()
                    lora(b, 2)
                else:
                    transpose_u(b - 1)
                if last:
                    count_before(0, EARLY, 1)
                lora(b, 3)
                if not last:
                    gains_h(b + 1)
                layer2(b)
                lora(b, 4)
                if not first:
                    logits(b - 1)
                lora(b, 5)

            block_of(0, first=True)
            block_of(1)
            pe.wait_ge(S.xT_rest, 16)
            with pe.Fori(2, NB - 1) as b:
                block_of(b)
            block_of(NB - 1, last=True)
            transpose_u(NB - 1)
            logits(NB - 1)
            pe.wait_ge(S.place, 8)
            count_before(EARLY, TILES, 2)
            pe.wait_ge(S.col_hot, NC_)
            for k in range(K):
                pe.wait_ge(S.token_val, k + 1)
                for n in range(k * TILES, (k + 1) * TILES):
                    last = pe.matmul(ps_rows[:, 0:SLOT_TILES], col_hot[:, n, :], tile_val[:, 0, :, n],
                                     start=(n == 0), stop=(n == NC_ - 1))
            last.then_inc(S.slots_ps, 1)
            for _ in range(WARM):
                pe.matmul(ps_lora[:, :], ones16[:, :], w_hi[:, 0:HALF], start=True, stop=True)
            pe.wait_ge(S.gate_val, 2)
            for n in range(NC_):
                last = pe.matmul(ps_gates[:, 0:2 * SLOT_TILES], col_hot[:, n, :], tile_val[:, 1:3, :, n],
                                 start=(n == 0), stop=(n == NC_ - 1))
            last.then_inc(S.gates_ps, 1)

            def rows_T(i, h, v):
                pe.wait_ge((S.rows0, S.rows1)[v], 16 * (h + 1))
                after(pe, S.rowsT, i - 1)
                for n in range(2 * DC):
                    last = pe.transpose(ps_rowsT[v][:, n * P:(n + 1) * P], rows_in[v][:, n * P:(n + 1) * P], ident16[:, :])
                last.then_inc((S.rowsT_ps0, S.rowsT_ps1)[v], 1)

            def first_layer(i, v, at):
                pe.wait_ge(S.rowsT, i + 1)
                for w, bank_, freed, done in ((0, ps_h1[v], S.h1, S.h1_ps), (DC * H, ps_h3[v], S.h3, S.h3_ps)):
                    after(pe, freed, i - 1)
                    passes = [(part_, c, w_) for c in range(DC) for part_, w_ in ((0, w_hi), (0, w_lo), (DC, w_hi))]
                    for n, (part_, c, w_) in enumerate(passes):
                        last = pe.matmul(bank_[:, :], rowsT[v][:, (part_ + c) * P:(part_ + c + 1) * P],
                                         w_[:, ds(at + (w + c * H), H)], start=(n == 0), stop=(n == len(passes) - 1))
                    last.then_inc(done, 1)

            def g_T(i, v):
                pe.wait_ge(S.g, i + 1)
                after(pe, S.gT_lo, i)
                for n in range(HC):
                    last = pe.transpose(ps_gT[:, n * P:(n + 1) * P], g_sb[v][:, n * P:(n + 1) * P], ident[:, :])
                last.then_inc(S.gT_ps, 1)

            def second_layer(i, v, at):
                pe.wait_ge(S.gT_lo, i + 1)
                after(pe, S.y, i)
                passes = [(g_, c, w_) for c in range(HC) for g_, w_ in ((gT_hi, w_hi), (gT_hi, w_lo), (gT_lo, w_hi))]
                for n, (g_, c, w_) in enumerate(passes):
                    last = pe.matmul(ps_y[:, 0:D], g_[v][:, c * P:(c + 1) * P], w_[:, ds(at + (2 * DC * H + c * D), D)],
                                     start=(n == 0), stop=(n == len(passes) - 1))
                last.then_inc(S.y_ps, 1)

            def step(i, h, v, expert, expert2, peeled=False):
                n = SLOT_TILES
                if not peeled or i < n:
                    first_layer(i, v, expert * WE)
                if not peeled or i + 1 < n:
                    rows_T(i + 1, h + v, 1 - v)
                if not peeled or 1 <= i <= n:
                    g_T(i - 1, 1 - v)
                if not peeled or 2 <= i:
                    second_layer(i - 2, v, expert2 * WE)

            def steps(i, n, h, peeled=False):
                e = experts_of(mybir.EngineType.PE, i, n)
                for v in range(n):
                    if not peeled or i + v < SLOT_TILES + 2:
                        step(i + v, h + v // 2, v % 2, e[2 + v], e[v], peeled)

            pe.wait_ge(S.tile_expert, 1)
            pe.wait_ge(S.slot_rows, 2)
            pe.wait_ge(S.w_lo, E * HALVES)
            rows_T(0, 0, 0)
            steps(0, 4, 0, peeled=True)
            turns = (SLOT_TILES - 5) // 4
            with pe.Fori(1, 1 + turns) as m:
                steps(m * 4, 4, m * 2)
            for i in range(4 + 4 * turns, SLOT_TILES + 2, 4):
                steps(i, 4, i // 2, peeled=True)


SEMAPHORES = """
ids_in x_first aw_in onehot_ids_in w1_in w1x_in x_rest net_in net_rows_in xT_first xT_rest int_w2_in norm_in out_in lora_scaled w1s_in w3s_in w2s_in x_third lora_k0_in lora_k13_in lora_k2_in
u_out biases_in added0 added1 const0 const path_now path_in x_ve h_ve c_ve v_ve x_rstd h_rstd c_rstd v_rstd
w_sum w_hi w_lo u gather_now rows0 rows1 scatter_now y_gated slot_rows slot_gate
aw_max aw_exp shift_in gain_in lora_in lora_hi lora_lo lora_d_out mlp_h_ps mlp_h xT_ps hT_ps
prod_t prod_s prod_h xhT hhT l1_ps l2_ps zT u_hi u_lo uT_ps uT lg_ps lg bias_blk gap e2 rowsT_ps0 rowsT_ps1
rowsT h1_ps h3_ps h1 h3 silu gT_ps gT_hi gT_lo g y_ps y
x_st x_mv xhat h_scaled h_pre h_st h_mv hhat gt_ps gs_ps gh_ps c c_st c_mv chat top top_i top_e
const_d row16 onehot mixw shift_z gain_s wx shift_ps tab mlp_o_ps v v_st v_mv vT_ps vT bias_ps
net_mixed chosen picked gate place_ps tiles place start in_tile col_hot gate_val started tile_expert slots_ps token_val tile_iota gates_ps gate_v empty
lora_ps passed
"""
REGION = 27808


def kernel(**inputs):
    import concourse.bacc as _bacc
    from concourse.bass_utils import run_bass_kernel_spmd as _run

    i = {k.replace("L0_cond_", "").replace("L0_ffn_", ""): np.asarray(v) for k, v in inputs.items()}
    f = np.ascontiguousarray

    def by_chunk(w):
        e, r, n = w.shape
        return f(w.reshape(e, r // P, P, n).transpose(0, 2, 1, 3).reshape(e * P, -1))

    x = f(i["x"].reshape(T, D))
    er = lambda w: w.reshape(E * R, -1)
    arrays = {
        "x": x, "xT": f(x.reshape(NB, BT, DC, P).transpose(3, 0, 2, 1).reshape(P, -1)),
        "path_ids": f(i["itok_BxS_0_999"].reshape(TILES, P).T),
        "onehot_ids": f(np.tile(np.repeat(np.stack([i["itok_BxS_0_4"].reshape(T), i["mask_BxS_ik0"].reshape(T)]),
                                          16, axis=0), (3, 1))),
        "path_tab": f(np.concatenate([i["pw_g"], i["pw_b"]], axis=1)),
        "aw": f(i["aw"]),
        "int_W1": f(i["int_W1"]), "int_w2g": f(np.concatenate([i["int_W2"], i["Wg"].T], axis=1)),
        "norm_rows": f(np.concatenate([i["int_b2"], i["int_g"], i["int_be"]])),
        "W1T": by_chunk(i["W1"].transpose(0, 2, 1)), "W3T": by_chunk(i["W3"].transpose(0, 2, 1)),
        "W2T": by_chunk(i["W2"].transpose(0, 2, 1)),
        "lora": f(np.concatenate([er(i["A1"]), er(i["A3"]), er(i["B1"].transpose(0, 2, 1)),
                                  er(i["B3"].transpose(0, 2, 1)), er(i["B2"].transpose(0, 2, 1)),
                                  er(i["A2"])], axis=1)),
        "biases": f(np.concatenate([i["b1"], i["b3"], i["b2"]], axis=1).reshape(-1)),
    }
    gains, shifts = np.zeros((ROWS, 4, D), np.float32), np.zeros((D, NKIND, ROWS), np.float32)
    for k, name in enumerate(("cp", "tm", "ms")):
        g, b = i[name + "_g"], i[name + "_b"]
        for r in range(16 * (k // 2), ROWS, 32):
            gains[r:r + len(g), k], shifts[:, k, r:r + len(b)] = g, b.T
    arrays["gains"], arrays["shiftZ"] = gains, shifts
    net = np.zeros((P, NET), np.float32)
    names = ("mem", "noi", "res")
    for k, (name, s) in enumerate(zip(names, ("cond_512", "cond_64", "fside_Bx32_0"))):
        w1 = i[name + "_W1"]
        net[:len(w1), NET_S + k * NBATCH:NET_S + (k + 1) * NBATCH] = i[s].T
        net[:, NET_B1 + k * DC:NET_B1 + (k + 1) * DC] = i[name + "_b1"].reshape(DC, P).T
        net[:len(w1), NET_W1 + k * D:NET_W1 + (k + 1) * D] = w1
        net[:, NET_W2 + k * DC * D:NET_W2 + (k + 1) * DC * D] = i[name + "_W2"].reshape(DC, P, D).transpose(1, 0, 2).reshape(P, -1)
    net[:, NET_INT:NET_INT + DC] = i["int_b1"].reshape(DC, P).T
    arrays["net"] = net
    arrays["net_rows"] = f(np.concatenate([i[name + part] for part in ("_b2", "_g", "_be") for name in names]))

    nc = _bacc.Bacc("TRN2", target_bir_lowering=False, num_devices=1)
    aps = {k: nc.dram_tensor(f"in_{k}", v.shape, mybir.dt.from_np(v.dtype), kind="ExternalInput").ap()
           for k, v in arrays.items()}
    out = nc.dram_tensor("out_rows", (T + PAD, D), F32, kind="ExternalOutput").ap()
    a = namedtuple("Inputs", aps)(*aps.values())
    build(nc, a, out)
    r = _run(nc, [{f"in_{k}": v for k, v in arrays.items()}], core_ids=[0])
    return r.results[0]["out_rows"][:T].reshape(inputs["x"].shape)
```
